# Optimizing a Trainium2 kernel written in Bass

```python
import numpy as np
import jax
import jax.numpy as jnp

def _softmax(x, axis=-1):
    return jax.nn.softmax(x, axis=axis)

def _gelu(x):
    return jax.nn.gelu(x, approximate=True)

def _silu(x):
    return jax.nn.silu(x)

def _sigmoid(x):
    return jax.nn.sigmoid(x)

def _layernorm(x, axis=-1, eps=1e-05):
    m = jnp.mean(x, axis=axis, keepdims=True)
    v = jnp.var(x, axis=axis, keepdims=True)
    return (x - m) / jnp.sqrt(v + eps)

def _scatter_add(tgt, idx, src, axis=0):
    return tgt.at[idx].add(src)

def _segment_sum(src, seg, n):
    return jax.ops.segment_sum(src, seg, n)
kernel_name = 'mk_gnn_preln_d2_gnn_r64_7be0e9'

def setup_inputs(seed: int=0):
    np.random.seed(seed)
    _w = jnp.asarray

    def _rec_inputs():
        import jax
        import jax.numpy as jnp
        _gk = jax.random.key(seed)
        x = -0.0005121 + 1.001 * jax.random.normal(jax.random.fold_in(_gk, 1), (100000, 64), jnp.float32)
        src = jax.random.randint(jax.random.fold_in(_gk, 2), (50000,), 0, 100000, jnp.int32)
        dst = jax.random.randint(jax.random.fold_in(_gk, 3), (50000,), 0, 100000, jnp.int32)
        _o = jnp.argsort(dst, stable=True)
        src = src[_o]
        dst = dst[_o]
        edge_attr_16 = -5.3897e-05 + 0.999841 * jax.random.normal(jax.random.fold_in(_gk, 12), (50000, 16), jnp.float32)
        return (x, src, dst, edge_attr_16)
    x, src, dst, edge_attr_16 = _rec_inputs()

    def _L0_gnn_setup():
        import jax, jax.numpy as jnp
        import numpy as np
        N = 50000
        E = 12500
        H = 6
        F_IN = 64
        F_OUT = 64
        NEG_SLOPE = 0.2
        key = jax.random.key(seed)
        k1, k2, k3, k4, k5 = jax.random.split(key, 5)
        x = jax.random.normal(k1, (N, F_IN), jnp.float32)
        edge_idx = jax.random.randint(k2, (2, E), 0, N, dtype=jnp.int64)
        scale = 1.0 / np.sqrt(F_IN)
        W_l = jax.random.normal(k3, (F_IN, H * F_OUT), jnp.float32) * scale
        W_r = jax.random.normal(k4, (F_IN, H * F_OUT), jnp.float32) * scale
        att = jax.random.normal(k5, (H, F_OUT), jnp.float32) * scale
        bias = jnp.zeros((F_OUT,), jnp.float32)
        return {'x': x, 'edge_idx': edge_idx, 'W_l': W_l, 'W_r': W_r, 'att': att, 'bias': bias}
    _L0_gnn_all = _L0_gnn_setup()
    _L0_gnn_in = {k: v for k, v in _L0_gnn_all.items() if k in ('W_l', 'W_r', 'att', 'bias')}
    del _L0_gnn_all

    def _L1_gnn_setup():
        import jax, jax.numpy as jnp
        import numpy as np
        N_NODES = 100000
        N_EDGES = 25000
        D_IN = 64
        E_W = 16
        EPS = 0.0
        key = jax.random.key(seed)
        k1, k2, k3, k4, k5 = jax.random.split(key, 5)
        feat = jax.random.normal(k1, (N_NODES, D_IN), dtype=jnp.float32)
        edge_w = jax.random.normal(k2, (N_EDGES, E_W), dtype=jnp.float32)
        src = jax.random.randint(k3, (N_EDGES,), 0, N_NODES)
        dst = jax.random.randint(k4, (N_EDGES,), 0, N_NODES)
        W = jax.random.normal(k5, (D_IN + E_W, D_IN), dtype=jnp.float32) / np.float32(np.sqrt(D_IN + E_W))
        b = jnp.zeros((D_IN,), dtype=jnp.float32)
        return {'feat': feat, 'edge_w': edge_w, 'W': W, 'b': b, 'src': src, 'dst': dst}
    _L1_gnn_all = _L1_gnn_setup()
    _L1_gnn_in = {k: v for k, v in _L1_gnn_all.items() if k in ('W', 'b')}
    del _L1_gnn_all
    return {'x': x, 'src': src, 'dst': dst, 'edge_attr_16': edge_attr_16, 'L0_gnn_W_l': _L0_gnn_in['W_l'], 'L0_gnn_W_r': _L0_gnn_in['W_r'], 'L0_gnn_att': _L0_gnn_in['att'], 'L0_gnn_bias': _L0_gnn_in['bias'], 'L1_gnn_W': _L1_gnn_in['W'], 'L1_gnn_b': _L1_gnn_in['b']}

def reference(x, src, dst, edge_attr_16, L0_gnn_W_l, L0_gnn_W_r, L0_gnn_att, L0_gnn_bias, L1_gnn_W, L1_gnn_b):
    import jax
    import jax.numpy as jnp

    def _L0_gnn_ref(x, edge_idx, W_l, W_r, att, bias):
        import jax, jax.numpy as jnp
        import numpy as np
        N = 50000
        E = 12500
        H = 6
        F_IN = 64
        F_OUT = 64
        NEG_SLOPE = 0.2
        n = x.shape[0]
        loops = jnp.arange(n, dtype=edge_idx.dtype)
        src = jnp.concatenate([edge_idx[0], loops])
        dst = jnp.concatenate([edge_idx[1], loops])
        gl = (x @ W_l).reshape(n, H, F_OUT)
        gr = (x @ W_r).reshape(n, H, F_OUT)
        s = jax.nn.leaky_relu(gl[src] + gr[dst], NEG_SLOPE)
        e = jnp.einsum('ehf,hf->eh', s, att)
        m = jax.ops.segment_max(e, dst, num_segments=n)
        p = jnp.exp(e - m[dst])
        denom = jax.ops.segment_sum(p, dst, num_segments=n)
        alpha = p / (denom[dst] + 1e-16)
        msg = alpha[:, :, None] * gl[src]
        out = jax.ops.segment_sum(msg, dst, num_segments=n)
        out = out.mean(axis=1) + bias
        return jax.nn.selu(out)

    def _L1_gnn_ref(feat, edge_w, W, b, src, dst):
        import jax, jax.numpy as jnp
        import numpy as np
        N_NODES = 100000
        N_EDGES = 25000
        D_IN = 64
        E_W = 16
        EPS = 0.0
        n = feat.shape[0]
        neigh_h = jax.ops.segment_sum(feat[src], dst, num_segments=n)
        neigh_w = jax.ops.segment_sum(edge_w, dst, num_segments=n)
        neigh = jnp.concatenate([neigh_h, neigh_w], axis=-1)
        feat_pad = jnp.concatenate([feat, jnp.zeros((n, neigh.shape[-1] - feat.shape[-1]), feat.dtype)], axis=-1)
        rst = (1.0 + EPS) * feat_pad + neigh
        rst = rst @ W + b
        return jax.nn.relu(rst)
    edge_index = jnp.stack([src, dst])
    h = jnp.maximum(_layernorm(x, axis=-1), 0.0)
    x = x + _L0_gnn_ref(h, edge_index, L0_gnn_W_l, L0_gnn_W_r, L0_gnn_att, L0_gnn_bias)
    h = jnp.maximum(_layernorm(x, axis=-1), 0.0)
    x = x + _L1_gnn_ref(h, edge_attr_16, L1_gnn_W, L1_gnn_b, src, dst)
    return x

_drawn_inputs = setup_inputs


def setup_inputs(seed=0):
    import zlib

    import numpy as np

    out = dict(_drawn_inputs(seed))
    spreads = {'L0_gnn_bias': (0.0, 0.1), 'L1_gnn_b': (0.0, 0.1)}
    factors = {}
    for name, (base, spread) in spreads.items():
        noise = np.random.default_rng([zlib.crc32(name.encode()), seed]).standard_normal(out[name].shape)
        drawn = base * np.exp(spread * noise) if base else spread * noise
        out[name] = jnp.asarray(drawn.astype(out[name].dtype))
    for name, factor in factors.items():
        out[name] = (out[name] * factor).astype(out[name].dtype)
    return out
```

```python
from contextlib import ExitStack

import concourse.bass as bass
from concourse import mybir

F32 = mybir.dt.float32
I32 = mybir.dt.int32
U32 = mybir.dt.uint32
ALU = mybir.AluOpType
ACT = mybir.ActivationFunctionType
AX = mybir.AxisListType

P = 128
EPS = 1e-5
BIG = 1e30
SELU_L = 1.0507009873554805
SELU_A = 1.6732632423543772
LN_EXP_SET = 6


class Chain:

    def __init__(self, eng, sem):
        self.eng, self.sem, self.start, self.n = eng, sem, 0, 0

    def turn(self, i, per_loop):
        self.start, self.n, self.per_loop = self.base + i * per_loop, 0, per_loop

    def enter(self):
        self.base = self.start + self.n

    def leave(self, turns):
        assert self.n == self.per_loop, (self.n, self.per_loop)
        self.start, self.n = self.base + turns * self.per_loop, 0

    def mark(self, ins):
        ins.then_inc(self.sem, 1)
        self.n += 1
        return self.n

    def wait(self, n):
        self.eng.wait_ge(self.sem, self.start + n)

    def step(self, ins):
        self.wait(self.mark(ins))


def gnn_program(nc, x, src, dst, edge_attr, w_l, w_r, att, bias0, w1, bias1, out):
    N, D = x.shape
    E = src.shape[0]
    H = att.shape[0]
    EW = edge_attr.shape[1]
    KW = D + EW
    CT = 4
    PER = 2 * CT
    TURNS = -(-E // (P * PER))
    T = TURNS * PER
    FULL = E // T
    REST = E - FULL * T
    HD = H * D
    NZ = HD // P
    ROWS = 8
    BLOCK = 2 * ROWS * P
    LAST = N - BLOCK
    assert (TURNS - 1) * BLOCK < N <= TURNS * BLOCK and NZ == 3 and FULL == P - 1

    h1_table = nc.dram_tensor("h1_table", (N, D), F32).ap()
    stash = nc.dram_tensor("stash", (P, T, 3 * D), F32).ap()
    x1_edges = nc.dram_tensor("x1_edges", (P, T, D), F32).ap()
    h1_edges = nc.dram_tensor("h1_edges", (P, T, D), F32).ap()

    keep = ExitStack()
    last_row = [N - 1]

    def sb(name, shape, dt=F32, ctx=keep):
        return ctx.enter_context(nc.sbuf_tensor(name, shape, dt))

    def sem(name):
        return keep.enter_context(nc.semaphore(name))

    def exists(i, c):
        return not isinstance(i, int) or 0 <= 2 * i + c < 2 * TURNS

    def ago(i, c, k):
        return i + (c - k) // 2, (c - k) % 2

    def wait_from(eng, semaphore, value):
        if not isinstance(value, int) or value > 0:
            eng.wait_ge(semaphore, value)

    def r3(ap, f):
        return ap.rearrange("p (r f) -> p r f", f=f)

    with keep:
        gather_idx = sb("gather_idx", [P, T + PER, 2], U32)
        scatter_idx = sb("scatter_idx", [P, T], U32)
        border_idx = sb("border_idx", [P, 2], U32)
        masks = sb("masks", [P, T, 2])
        same_next = sb("same_next", [P, T])
        is_last = sb("is_last", [P, T])
        is_first = sb("is_first", [P, T])
        ident = sb("ident", [P, P])
        ones = sb("ones", [P, P])
        eps = sb("eps", [P, 1])
        w_edge = sb("w_edge", [P, HD])
        w_self = sb("w_self", [P, HD])
        att_blk = sb("att_blk", [P, NZ, 32])
        lin_e = sb("lin_e", [P, 32])
        lin_s = sb("lin_s", [P, 32])
        select = sb("select", [P, 2 * H])
        mean_blk = sb("mean_blk", [P, P])
        w_msg = sb("w_msg", [P, NZ, D])
        base_w = sb("base_w", [P, D])
        w1_blk = sb("w1_blk", [P, P])
        w1_all = sb("w1_all", [KW, D])
        bias0_b = sb("bias0_b", [P, D])
        bias1_b = sb("bias1_b", [P, D])
        same_aa = sb("same_aa", [P, P])
        same_ba = sb("same_ba", [P, P])
        same_ab = sb("same_ab", [P, P])
        same_bb = sb("same_bb", [P, P])
        pen_a = sb("pen_a", [P, 2, P])
        pen_b = sb("pen_b", [P, 2, P])
        scores = sb("scores", [P, 2 * H, T])
        alpha = sb("alpha", [P, T, H])
        first_sum = sb("first_sum", [P, 2, D])
        border_x1 = sb("border_x1", [P, 2, D])
        border_h1 = sb("border_h1", [P, 2, D])
        admitted = sem("admitted")

        with ExitStack() as own:
            def tmp(name, shape, dt=F32):
                return sb(name, shape, dt, own)

            src_i = tmp("src_i", [P, T], I32)
            dst_i = tmp("dst_i", [P, T], I32)
            dstf = tmp("dstf", [P, T])
            work = tmp("work", [P, T])
            endm = tmp("endm", [P, T])
            notab = tmp("notab", [P, 1])
            cnt = tmp("cnt", [P, 2])
            bidf = tmp("bidf", [P, 2])
            before = tmp("before", [P, P])
            dg = tmp("dg", [P, 2, P])
            eq = tmp("eq", [P, P])
            att_b = tmp("att_b", [P, HD])
            prod = tmp("prod", [P, HD])
            wl_lo = tmp("wl_lo", [P, HD])
            wl_sum = tmp("wl_sum", [P, D])
            rows_ps = own.enter_context(nc.psum_tensor("rows_ps", [P, 2, P], F32))
            zeroed, loaded_e, loaded_w, pooled, diag, rowed, step = (
                sem(n) for n in ("zeroed", "loaded_edges", "loaded_weights", "pool_consts", "diag_ready",
                                 "rows_ready", "setup_step"))
            n_w = [0]
            block = own.enter_context(nc.Block())

            @block.gpsimd
            def _(pool):
                nc.gpsimd.memset(src_i[:, :], 0).then_inc(zeroed, 1)
                nc.gpsimd.memset(dst_i[:, :], N).then_inc(zeroed, 1)
                for t in (att_blk[:, :, :], base_w[:, :], w1_blk[:, :]):
                    nc.gpsimd.memset(t, 0.0).then_inc(zeroed, 1)
                nc.gpsimd.memset(ident[:, :], 0.0).then_inc(pooled, 1)
                nc.gpsimd.memset(before[:, :], 1.0).then_inc(pooled, 1)
                pool.wait_ge(pooled, 2)
                nc.gpsimd.affine_select(out=ident[:, :], in_=ident[:, :], compare_op=ALU.not_equal, fill=1.0,
                                        base=0, pattern=[[-1, P]], channel_multiplier=1).then_inc(pooled, 1)
                nc.gpsimd.affine_select(out=before[:, :], in_=before[:, :], compare_op=ALU.is_gt, fill=0.0,
                                        base=0, pattern=[[-1, P]], channel_multiplier=1).then_inc(pooled, 1)

            @block.sync
            def _(sp):
                sp.wait_ge(zeroed, 2)
                for tile, dram in ((src_i, src), (dst_i, dst)):
                    sp.dma_start(tile[0:FULL, :], dram[0:FULL * T].rearrange("(p t) -> p t", t=T)).then_inc(loaded_e, 16)
                    sp.dma_start(tile[FULL:P, 0:REST], dram[FULL * T:E].rearrange("(p t) -> p t", p=1)).then_inc(loaded_e, 16)
                sp.wait_ge(zeroed, 5)

                def load(to, what):
                    sp.dma_start(to, what).then_inc(loaded_w, 16)
                    n_w[0] += 16

                load(w_edge[0:D, :], w_l)
                load(w_edge[D:P, :], w_r)
                load(wl_lo[0:D, :], w_l)
                load(wl_lo[D:P, :], w_l)
                for h in range(H):
                    rows = slice((h % 2) * D, (h % 2) * D + D)
                    load(att_blk[rows, h // 2, h:h + 1], att[h, :].rearrange("(f o) -> f o", o=1))
                load(att_b[:, :], att.rearrange("h f -> (h f)").partition_broadcast(P))
                load(bias0_b[:, :], bias0.partition_broadcast(P))
                load(bias1_b[:, :], bias1.partition_broadcast(P))
                load(base_w[D:D + 1, :], bias0.rearrange("(o f) -> o f", o=1))
                load(w1_all[:, :], w1)
                load(w1_blk[0:D, 0:D], w1[0:D, :])
                load(w1_blk[D:P, D:P], w1[0:D, :])

            @block.tensor
            def _(pe):
                pe.wait_ge(diag, 1)
                nc.tensor.matmul(rows_ps[:, :, :], ones[:, :], dg[:, :, :], start=True, stop=True).then_inc(rowed, 1)

            @block.vector
            def _(dve):
                v = nc.vector
                do = Chain(dve, step)
                do.step(v.memset(ones[:, :], 1.0))
                do.step(v.memset(eps[:, :], EPS))
                for t in (w_self[:, :], lin_e[:, :], lin_s[:, :], select[:, :], mean_blk[:, :]):
                    do.step(v.memset(t, 0.0))
                do.step(v.memset(first_sum[:, :, :], 0.0))
                do.step(v.memset(gather_idx[:, :, :], 0))
                dve.wait_ge(loaded_e, 64)
                do.step(v.tensor_copy(dstf[:, :], dst_i[:, :]))
                do.step(v.tensor_copy(gather_idx[:, 0:T, 0], src_i[:, :]))
                do.step(v.tensor_scalar(gather_idx[:, 0:T, 1], dstf[:, :], float(N - 1), None, ALU.min))
                a, b = dstf[:, 0:1], dstf[:, T - 1:T]
                dve.wait_ge(pooled, 4)
                do.step(v.tensor_scalar(dg[:, 0, :], ident[:, :], a, None, ALU.mult))
                v.tensor_scalar(dg[:, 1, :], ident[:, :], b, None, ALU.mult).then_inc(diag, 1)
                do.step(v.memset(masks[:, 0:1, 0:1], 0.0))
                do.step(v.memset(same_next[:, T - 1:T], 0.0))
                do.step(v.tensor_tensor(masks[:, 1:T, 0], dstf[:, 1:T], dstf[:, 0:T - 1], ALU.is_equal))
                do.step(v.tensor_copy(same_next[:, 0:T - 1], masks[:, 1:T, 0]))
                do.step(v.tensor_scalar(is_first[:, :], dstf[:, :], a, None, ALU.is_equal))
                do.step(v.tensor_copy(masks[:, :, 1], is_first[:, :]))
                do.step(v.tensor_tensor(notab[:, :], a, b, ALU.not_equal))
                do.step(v.tensor_scalar(is_last[:, :], dstf[:, :], b, notab[:, :], ALU.is_equal, ALU.mult))
                do.step(v.tensor_tensor(work[:, :], is_first[:, :], is_last[:, :], ALU.add))
                do.step(v.tensor_tensor(work[:, :], work[:, :], same_next[:, :], ALU.add))
                do.step(v.tensor_scalar(endm[:, :], work[:, :], 0.0, None, ALU.is_equal))
                do.step(v.tensor_scalar(work[:, :], dstf[:, :], float(N), None, ALU.subtract))
                do.step(v.tensor_tensor(work[:, :], work[:, :], endm[:, :], ALU.mult))
                do.step(v.tensor_scalar(scatter_idx[:, :], work[:, :], float(N), None, ALU.add))
                dve.wait_ge(rowed, 1)
                row_a, row_b = rows_ps[:, 0, :], rows_ps[:, 1, :]
                for pen, k, row, own_node in ((pen_a, 0, row_a, a), (pen_a, 1, row_b, a),
                                              (pen_b, 0, row_a, b), (pen_b, 1, row_b, b)):
                    do.step(v.tensor_scalar(eq[:, :], row, own_node, None, ALU.is_equal))
                    do.step(v.tensor_scalar(pen[:, k, :], eq[:, :], 1.0, BIG, ALU.subtract, ALU.mult))
                    if pen is pen_a and k == 0:
                        do.step(v.tensor_tensor(same_aa[:, :], eq[:, :], ident[:, :], ALU.subtract))
                        do.step(v.tensor_tensor(eq[:, :], eq[:, :], before[:, :], ALU.mult))
                        do.step(v.tensor_reduce(cnt[:, 0:1], eq[:, :], AX.X, ALU.add))
                    if pen is pen_b and k == 0:
                        do.step(v.tensor_reduce(cnt[:, 1:2], eq[:, :], AX.X, ALU.add))
                do.step(v.tensor_scalar(same_ba[:, :], row_a, b, notab[:, :], ALU.is_equal, ALU.mult))
                do.step(v.tensor_scalar(same_ab[:, :], row_b, a, None, ALU.is_equal))
                do.step(v.tensor_scalar(eq[:, :], row_b, b, None, ALU.is_equal))
                do.step(v.tensor_tensor(eq[:, :], eq[:, :], ident[:, :], ALU.subtract))
                do.step(v.tensor_scalar(same_bb[:, :], eq[:, :], notab[:, :], None, ALU.mult))
                for k, node in ((0, a), (1, b)):
                    do.step(v.tensor_scalar(cnt[:, k:k + 1], cnt[:, k:k + 1], 0.0, None, ALU.is_equal))
                    do.step(v.tensor_scalar(bidf[:, k:k + 1], node, float(N), None, ALU.subtract))
                do.step(v.tensor_tensor(bidf[:, :], bidf[:, :], cnt[:, :], ALU.mult))
                do.step(v.tensor_scalar(border_idx[:, :], bidf[:, :], float(N), None, ALU.add))
                dve.wait_ge(loaded_w, n_w[0])
                do.step(v.tensor_tensor(w_self[D:P, :], wl_lo[D:P, :], w_edge[D:P, :], ALU.add))
                for w, lin in ((w_edge, lin_e), (w_self, lin_s)):
                    do.step(v.tensor_tensor(prod[:, :], w[:, :], att_b[:, :], ALU.mult))
                    do.step(v.tensor_reduce(lin[:, 0:H], r3(prod[:, :], D), AX.X, ALU.add))
                    do.step(v.tensor_scalar(lin[:, 0:H], lin[:, 0:H], 0.2, None, ALU.mult))
                do.step(v.tensor_scalar(prod[:, :], wl_lo[:, :], 1.0 / H, None, ALU.mult))
                do.step(v.tensor_reduce(wl_sum[:, :], prod[:, :].rearrange("p (h f) -> p f h", f=D), AX.X, ALU.add))
                do.step(v.tensor_copy(mean_blk[0:D, 0:D], wl_sum[0:D, :]))
                do.step(v.tensor_copy(mean_blk[D:P, D:P], wl_sum[D:P, :]))
                do.step(v.tensor_copy(base_w[0:D, :], wl_sum[0:D, :]))
                for h in range(H):
                    rows = slice((h % 2) * D, (h % 2) * D + D)
                    do.step(v.tensor_copy(w_msg[rows, h // 2, :], prod[rows, h * D:(h + 1) * D]))
                for g in range(4):
                    do.step(v.tensor_copy(select[32 * g:32 * g + H, H * (g // 2):H * (g // 2) + H],
                                          ident[32 * g:32 * g + H, 32 * g:32 * g + H]))

        with ExitStack() as own:
            def tmp(name, shape, dt=F32):
                return sb(name, shape, dt, own)

            def pair(name, shape, dt=F32):
                return [tmp(f"{name}{c}", shape, dt) for c in range(2)]

            R2 = 2 * ROWS
            idx_c = pair("idx_c", [P, CT, 2], U32)
            xe = pair("xe", [P, CT, 2, D])
            xd = pair("xd", [P, ROWS, D])
            he = pair("he", [P, CT * 2 * D])
            hd = pair("hd", [P, ROWS * D])
            h1 = pair("h1", [P, ROWS * D])
            stats = pair("stats", [P, R2, 6])
            sumq = pair("sumq", [P, R2, 2])
            diff = pair("diff", [P, R2])
            var = pair("var", [P, R2])
            lnv = pair("lnv", [P, R2])
            rstd = pair("rstd", [P, R2])
            stats1 = pair("stats1", [P, ROWS, 6])
            sumq1 = pair("sumq1", [P, ROWS, 2])
            diff1 = pair("diff1", [P, ROWS])
            var1 = pair("var1", [P, ROWS])
            lnv1 = pair("lnv1", [P, ROWS])
            rstd1 = pair("rstd1", [P, ROWS])
            xc = [tmp(f"xc{k}", [P, ROWS, D]) for k in range(4)]
            heT = pair("heT", [P, CT * P])
            hdT = pair("hdT", [P, ROWS * D])
            relu_z = pair("relu_z", [P, 2 * NZ, CT * P])
            scoreT = pair("scoreT", [P, CT * P])
            gat = pair("gat", [P, ROWS * D])
            gexp = pair("gexp", [P, ROWS * D])
            grelu = pair("grelu", [P, ROWS * D])
            x1 = pair("x1", [P, ROWS, D])
            res = pair("res", [P, ROWS * D])

            def ps(name, shape):
                return own.enter_context(nc.psum_tensor(name, shape, F32))

            tr_e = ps("tr_e", [P, CT * P])
            tr_d = ps("tr_d", [P, CT * P])
            z_ps = [ps(f"z_ps{k}", [P, CT * P]) for k in range(3)]
            sc_ps = ps("sc_ps", [P, CT * P])
            sel_ps = ps("sel_ps", [P, CT, 2 * H])
            mm_d = ps("mm_d", [P, ROWS * D])

            idx_ready, gathered, x_ready, x_stashed, h_stashed, h1_stored, out_stored = (
                [sem(f"{n}{c}") for c in range(2)] for n in
                ("idx_ready", "gathered", "x_ready", "x_stashed", "h_stashed", "h1_stored", "out_stored"))
            hd_tr, hd_T, mm_ready, mm_read = (
                [sem(f"{n}{layer}") for layer in range(2)] for n in ("hd_transposed", "hdT_ready", "mm_ready", "mm_read"))
            (var_ready, rstd_ready, h_ready, he_tr, he_T, z_ready, relu_ready, round_ready, scoreT_ready,
             sel_ready, scores_done, gat_act, x1_ready, var1_ready,
             rstd1_ready, h1_ready, res_ready, dve_step, act_step) = (sem(n) for n in (
                 "var_ready", "rstd_ready", "h_ready", "he_transposed", "heT_ready", "z_ready", "relu_ready",
                 "round_ready", "scoreT_ready", "sel_ready", "scores_done",
                 "gat_act", "x1_ready", "var1_ready", "rstd1_ready", "h1_ready",
                 "res_ready", "dve_step", "act_step"))
            block = own.enter_context(nc.Block())
            LASTI = TURNS - 1

            def kth(i, c):
                return 2 * i + (c + 1)

            def nodes(i):
                return LAST if isinstance(i, int) and i == LASTI else i * BLOCK

            def dense_rows(dram, i, c):
                return dram[bass.ds(nodes(i), BLOCK), :].rearrange("(p u) f -> p u f", u=2 * ROWS)[:, c * ROWS:(c + 1) * ROWS, :]

            @block.gpsimd
            def _(pool):
                last_row[0] = pool.to_reg(N - 1)

                def gathers(i, c):
                    pool.wait_ge(idx_ready[c], 16 * (i + 1))
                    pool.sem_inc(admitted, 1)
                    for j in range(CT):
                        for s in range(2):
                            nc.gpsimd.indirect_dma_start(
                                xe[c][:, j, s, :], None, x,
                                bass.IndirectOffsetOnAxis(ap=idx_c[c][:, j, s:s + 1], axis=0),
                                bounds_check=last_row[0], oob_is_err=False).then_inc(gathered[c], 16)

                for c in range(2):
                    gathers(0, c)
                with pool.Fori(1, TURNS) as i:
                    for c in range(2):
                        pool.wait_ge(h_ready, 2 * i + (c - 1))
                        pool.wait_ge(x_stashed[c], 16 * i)
                        gathers(i, c)

            @block.sync
            def _(sp):
                def load_idx(i, c):
                    sp.dma_start(idx_c[c][:, :, :], gather_idx[:, bass.ds(i * PER + CT * c, CT), :]).then_inc(idx_ready[c], 16)

                def load_x(i, c):
                    sp.dma_start(xd[c][:, :, :], dense_rows(x, i, c)).then_inc(x_ready[c], 16)

                def stashes(i, c):
                    sp.wait_ge(h_ready, kth(i, c))
                    sp.dma_start(stash[:, bass.ds(i * PER + CT * c, CT), 0:2 * D], r3(he[c][:, :], 2 * D)).then_inc(h_stashed[c], 16)
                    sp.dma_start(stash[:, bass.ds(i * PER + CT * c, CT), 2 * D:3 * D], xe[c][:, :, 1, :]).then_inc(x_stashed[c], 16)

                def store(i, c, ready, dram, rows, stored):
                    sp.wait_ge(ready, kth(i, c))
                    if isinstance(i, int) and i == LASTI:
                        for k in range(2):
                            sp.wait_ge(stored[k], 16 * LASTI)
                    sp.dma_start(dense_rows(dram, i, c), r3(rows[c][:, :], D)).then_inc(stored[c], 16)

                def turn(i):
                    for c in range(2):
                        j, d = ago(i, c, -3)
                        if exists(j, d):
                            wait_from(sp, gathered[d], 32 * CT * j)
                            load_idx(j, d)
                        if exists(*ago(i, c, -1)):
                            stashes(*ago(i, c, -1))
                        if exists(*ago(i, c, -2)):
                            sp.wait_ge(x1_ready, kth(i, c))
                            load_x(i + 1, c)
                        if exists(*ago(i, c, 1)):
                            store(*ago(i, c, 1), res_ready, out, res, out_stored)
                        if exists(i, c):
                            store(i, c, h1_ready, h1_table, h1, h1_stored)

                for c in range(2):
                    load_idx(0, c)
                    load_x(0, c)
                wait_from(sp, gathered[0], 32 * CT)
                load_idx(1, 0)
                stashes(0, 0)
                turn(0)
                with sp.Fori(1, LASTI - 1) as i:
                    turn(i)
                turn(LASTI - 1)
                turn(LASTI)
                turn(TURNS)
                for c in range(2):
                    for s in (x_stashed, h_stashed, h1_stored, out_stored):
                        sp.wait_ge(s[c], 16 * TURNS)

            @block.tensor
            def _(pe):
                t = nc.tensor

                def transpose_e(i, c):
                    pe.wait_ge(h_ready, kth(i, c))
                    wait_from(pe, he_T, 2 * i + c)
                    for j in range(CT):
                        ins = t.transpose(tr_e[:, j * P:(j + 1) * P], he[c][:, j * P:(j + 1) * P], ident[:, :])
                    ins.then_inc(he_tr, 1)

                def before_this(i, c, layer, done):
                    if layer == 0:
                        wait_from(pe, done[1], 2 * i + (c - 1))
                    elif exists(*ago(i, c, -1)):
                        pe.wait_ge(done[0], 2 * i + (c + 2))
                    else:
                        pe.wait_ge(done[0], 2 * TURNS)

                def transpose_d(i, c, layer):
                    if layer == 0:
                        pe.wait_ge(h_ready, kth(i, c))
                    else:
                        pe.wait_ge(h1_ready, kth(i, c))
                    before_this(i, c, layer, hd_T)
                    h = (hd, h1)[layer][c]
                    for j in range(ROWS // 2):
                        ins = t.transpose(tr_d[:, j * P:(j + 1) * P], h[:, j * P:(j + 1) * P], ident[:, :])
                    ins.then_inc(hd_tr[layer], 1)

                def dense_mm(i, c, layer):
                    pe.wait_ge(hd_T[layer], kth(i, c))
                    before_this(i, c, layer, mm_read)
                    for j in range(ROWS // 2):
                        ins = t.matmul(mm_d[:, j * P:(j + 1) * P], hdT[c][:, j * P:(j + 1) * P],
                                       (mean_blk, w1_blk)[layer][:, :], start=True, stop=True)
                    ins.then_inc(mm_ready[layer], 1)

                ORDER = [(0, 0), (0, 2), (1, 0), (1, 2), (0, 1), (1, 1)]

                def project(i, c, part):
                    if part == 0:
                        pe.wait_ge(he_T, kth(i, c))
                    for n in range(3 * part, 3 * part + 3):
                        kind, z = ORDER[n]
                        pe.wait_ge(relu_ready, 12 * i + 6 * c + n + 1)
                        t.matmul(z_ps[n % 3][:, :], (w_edge, w_self)[kind][:, z * P:(z + 1) * P], heT[c][:, :],
                                 start=True, stop=True).then_inc(z_ready, 1)

                def rounds(i, c):
                    pe.wait_ge(relu_ready, 12 * i + 6 * c + 6 + 3)
                    for g, (n, z) in enumerate(((0, 0), (1, 2), (2, 0), (3, 2))):
                        t.matmul(sc_ps[32 * g:32 * g + 32, :], att_blk[:, z, :], relu_z[c][:, n, :], start=True, stop=False)
                    t.matmul(sc_ps[0:32, :], att_blk[:, 1, :], relu_z[c][:, 4, :], start=False, stop=True)
                    t.matmul(sc_ps[32:64, :], lin_e[:, :], heT[c][:, :], start=False, stop=True)
                    t.matmul(sc_ps[64:96, :], att_blk[:, 1, :], relu_z[c][:, 5, :], start=False, stop=True)
                    t.matmul(sc_ps[96:128, :], lin_s[:, :], heT[c][:, :], start=False, stop=True).then_inc(round_ready, 1)

                def select_scores(i, c):
                    pe.wait_ge(scoreT_ready, kth(i, c))
                    wait_from(pe, scores_done, 2 * i + c)
                    for j in range(CT):
                        ins = t.matmul(sel_ps[:, j, :], scoreT[c][:, j * P:(j + 1) * P], select[:, :], start=True, stop=True)
                    ins.then_inc(sel_ready, 1)

                def turn(i):
                    for c in range(2):
                        now, previous = exists(i, c), exists(*ago(i, c, 1))
                        j, d = ago(i, c, 1)
                        if now:
                            transpose_d(i, c, 0)
                            transpose_e(i, c)
                        if previous:
                            rounds(j, d)
                        if now:
                            project(i, c, 0)
                            dense_mm(i, c, 0)
                        if previous:
                            transpose_d(j, d, 1)
                        if now:
                            project(i, c, 1)
                        if previous:
                            dense_mm(j, d, 1)
                            select_scores(j, d)

                turn(0)
                with pe.Fori(1, TURNS) as i:
                    turn(i)
                turn(TURNS)

            @block.scalar
            def _(act):
                a = nc.scalar
                own_step = Chain(act, act_step)

                def rstds(i, c, layer):
                    v, l, r = ((var, lnv, rstd), (var1, lnv1, rstd1))[layer]
                    act.wait_ge((var_ready, var1_ready)[layer], kth(i, c))
                    n = own_step.mark(a.activation(l[c][:, :], v[c][:, :], ACT.Ln, bias=eps[:, :], scale=1.0 / D))
                    own_step.wait(n)
                    a.activation(r[c][:, :], l[c][:, :], ACT.Exp, scale=-0.5).then_inc((rstd_ready, rstd1_ready)[layer], 1)

                def copy_e(i, c):
                    act.wait_ge(he_tr, kth(i, c))
                    a.activation(heT[c][:, :], tr_e[:, :], ACT.Copy).then_inc(he_T, 1)

                def copy_d(i, c, layer):
                    act.wait_ge(hd_tr[layer], kth(i, c))
                    a.activation(hdT[c][:, :], tr_d[:, :], ACT.Copy).then_inc(hd_T[layer], 1)

                def relus(i, c, which):
                    for n in which:
                        act.wait_ge(z_ready, 12 * i + 6 * c + n + 1)
                        a.activation(relu_z[c][:, n, :], z_ps[n % 3][:, :], ACT.Relu, scale=0.8).then_inc(relu_ready, 1)

                def copy_scores(i, c):
                    act.wait_ge(round_ready, kth(i, c))
                    a.activation(scoreT[c][:, :], sc_ps[:, :], ACT.Copy).then_inc(scoreT_ready, 1)

                def selu_parts(i, c):
                    act.wait_ge(mm_read[0], kth(i, c))
                    a.activation(gexp[c][:, :], gat[c][:, :], ACT.Exp).then_inc(gat_act, 1)
                    a.activation(grelu[c][:, :], gat[c][:, :], ACT.Relu, scale=SELU_L).then_inc(gat_act, 1)

                def turn(i):
                    for c in range(2):
                        now, previous, following = exists(i, c), exists(*ago(i, c, 1)), exists(*ago(i, c, -1))
                        if now:
                            copy_d(i, c, 0)
                            copy_e(i, c)
                        if previous:
                            copy_scores(*ago(i, c, 1))
                            rstds(*ago(i, c, 1), 1)
                        if now:
                            relus(i, c, (0, 1, 2))
                        if previous:
                            copy_d(*ago(i, c, 1), 1)
                        if now:
                            relus(i, c, (3,))
                        if following:
                            rstds(*ago(i, c, -1), 0)
                        if now:
                            relus(i, c, (4, 5))
                            selu_parts(i, c)

                act.add_instruction(mybir.InstLoadActFuncSet(
                    name=nc.get_next_instruction_name(), act_func_set_id=LN_EXP_SET, ins=[], outs=[]))
                act.sem_inc(relu_ready, 3)
                rstds(0, 0, 0)
                turn(0)
                own_step.enter()
                with act.Fori(1, LASTI) as i:
                    own_step.turn(i - 1, 4)
                    turn(i)
                own_step.leave(LASTI - 1)
                turn(LASTI)
                turn(TURNS)

            @block.vector
            def _(dve):
                v = nc.vector
                do = Chain(dve, dve_step)

                def norm_small(i, c, st, sq, df, va, signal):
                    n = do.n
                    do.wait(n)
                    nd = do.mark(v.tensor_tensor(df[:, :], st[:, :, 1], st[:, :, 4], ALU.subtract))
                    ns = do.mark(v.tensor_tensor(sq[:, :, :], st[:, :, 1:3], st[:, :, 4:6], ALU.add))
                    do.wait(nd)
                    n = do.mark(v.scalar_tensor_tensor(va[:, :], df[:, :], D / 4.0, df[:, :], ALU.mult, ALU.mult))
                    do.wait(n)
                    v.tensor_tensor(va[:, :], va[:, :], sq[:, :, 1], ALU.add).then_inc(signal, 1)

                def norm_stats(i, c):
                    dve.wait_ge(x_ready[c], 16 * (i + 1))
                    for r in range(ROWS):
                        v.bn_stats(stats[c][:, r, :], xd[c][:, r, :])
                    dve.wait_ge(gathered[c], 32 * CT * (i + 1))
                    for r in range(ROWS):
                        ins = v.bn_stats(stats[c][:, ROWS + r, :], xe[c][:, r // 2, r % 2, :])
                    do.mark(ins)
                    norm_small(i, c, stats[c], sumq[c], diff[c], var[c], var_ready)

                def mid(ap):
                    return ap.unsqueeze(2).to_broadcast([P, ROWS, D])

                def centre(i, c):
                    xe_rows = xe[c][:, :, :, :].rearrange("p j s f -> p (j s) f")
                    wait_from(dve, h_ready, 2 * i + c)
                    do.mark(v.scalar_tensor_tensor(xc[0][:, :, :], mid(sumq[c][:, 0:ROWS, 0]), -0.5, xd[c][:, :, :], ALU.mult, ALU.add))
                    do.mark(v.scalar_tensor_tensor(xc[1][:, :, :], mid(sumq[c][:, ROWS:R2, 0]), -0.5, xe_rows, ALU.mult, ALU.add))

                def norm_apply(i, c):
                    do.wait(do.n - 1)
                    dve.wait_ge(rstd_ready, kth(i, c))
                    v.scalar_tensor_tensor(r3(hd[c][:, :], D), xc[0][:, :, :], 0.0, mid(rstd[c][:, 0:ROWS]), ALU.max, ALU.mult)
                    do.wait(do.n)
                    wait_from(dve, h_stashed[c], 16 * i)
                    v.scalar_tensor_tensor(r3(he[c][:, :], D), xc[1][:, :, :], 0.0, mid(rstd[c][:, ROWS:R2]), ALU.max, ALU.mult).then_inc(h_ready, 1)

                def add_bias(i, c):
                    dve.wait_ge(mm_ready[0], kth(i, c))
                    v.tensor_tensor(r3(gat[c][:, :], D), r3(mm_d[:, :], D), bias0_b[:, :].unsqueeze(1).to_broadcast([P, ROWS, D]), ALU.add).then_inc(mm_read[0], 1)

                def selu_residual(i, c):
                    dve.wait_ge(gat_act, 4 * i + 2 * c + 1)
                    n = do.mark(v.tensor_scalar(gexp[c][:, :], gexp[c][:, :], 1.0, SELU_L * SELU_A, ALU.min, ALU.mult))
                    do.wait(n)
                    wait_from(dve, h1_ready, 2 * i + c)
                    wait_from(dve, res_ready, 2 * i + (c - 1))
                    n = do.mark(v.scalar_tensor_tensor(xc[2][:, :, :], r3(gexp[c][:, :], D), -SELU_L * SELU_A, xd[c][:, :, :], ALU.add, ALU.add))
                    do.wait(n)
                    dve.wait_ge(gat_act, 4 * i + 2 * c + 2)
                    v.tensor_tensor(x1[c][:, :, :], xc[2][:, :, :], r3(grelu[c][:, :], D), ALU.add).then_inc(x1_ready, 1)
                    dve.wait_ge(x1_ready, kth(i, c))
                    for r in range(ROWS):
                        ins = v.bn_stats(stats1[c][:, r, :], x1[c][:, r, :])
                    do.mark(ins)
                    norm_small(i, c, stats1[c], sumq1[c], diff1[c], var1[c], var1_ready)

                def norm1_apply(i, c):
                    n = do.mark(v.scalar_tensor_tensor(xc[2][:, :, :], mid(sumq1[c][:, :, 0]), -0.5, x1[c][:, :, :], ALU.mult, ALU.add))
                    do.wait(n)
                    dve.wait_ge(rstd1_ready, kth(i, c))
                    wait_from(dve, h1_stored[c], 16 * i)
                    v.scalar_tensor_tensor(r3(h1[c][:, :], D), xc[2][:, :, :], 0.0, mid(rstd1[c][:, :]), ALU.max, ALU.mult).then_inc(h1_ready, 1)

                def keep_scores(i, c):
                    dve.wait_ge(sel_ready, kth(i, c))
                    v.tensor_copy(scores[:, :, bass.ds(i * PER + CT * c, CT)].rearrange("p g t -> p t g"), sel_ps[:, :, :]).then_inc(scores_done, 1)

                def dense_out(i, c):
                    dve.wait_ge(mm_ready[1], kth(i, c))
                    wait_from(dve, res_ready, 2 * i + c)
                    v.tensor_tensor(xc[3][:, :, :], r3(mm_d[:, :], D), bias1_b[:, :].unsqueeze(1).to_broadcast([P, ROWS, D]), ALU.add).then_inc(mm_read[1], 1)
                    dve.wait_ge(mm_read[1], kth(i, c))
                    wait_from(dve, out_stored[c], 16 * i)
                    v.scalar_tensor_tensor(r3(res[c][:, :], D), xc[3][:, :, :], 0.0, x1[c][:, :, :], ALU.max, ALU.add).then_inc(res_ready, 1)

                def turn(i):
                    for c in range(2):
                        now, previous, following = exists(i, c), exists(*ago(i, c, 1)), exists(*ago(i, c, -1))
                        if following:
                            norm_stats(*ago(i, c, -1))
                        if now:
                            add_bias(i, c)
                        if following:
                            centre(*ago(i, c, -1))
                            norm_apply(*ago(i, c, -1))
                        if now:
                            selu_residual(i, c)
                        if previous:
                            keep_scores(*ago(i, c, 1))
                            dense_out(*ago(i, c, 1))
                        if now:
                            norm1_apply(i, c)

                norm_stats(0, 0)
                centre(0, 0)
                norm_apply(0, 0)
                turn(0)
                do.enter()
                with dve.Fori(1, LASTI) as i:
                    do.turn(i - 1, 26)
                    turn(i)
                do.leave(LASTI - 1)
                turn(LASTI)
                turn(TURNS)

        with ExitStack() as own:
            def tmp(name, shape, dt=F32):
                return sb(name, shape, dt, own)

            HT = H * T
            pen_same = tmp("pen_same", [P, H, T])
            pen_next = tmp("pen_next", [P, H, T])
            one_same = tmp("one_same", [P, H, T])
            one_next = tmp("one_next", [P, H, T])
            pen_first = tmp("pen_first", [P, T])
            pen_last = tmp("pen_last", [P, T])
            top = tmp("top", [P, H, T])
            fwd = tmp("fwd", [P, H, T])
            bwd = tmp("bwd", [P, H, T])
            ends = tmp("ends", [P, 2, H])
            spread = tmp("spread", [P, 2 * H, P])
            cand = tmp("cand", [P, 2, H, P])
            best2 = tmp("best2", [P, 2, H])
            border_best = tmp("border_best", [P, 2, H])
            border_more = tmp("border_more", [P, 2, H])
            spread_ps = own.enter_context(nc.psum_tensor("spread_ps", [P, 4, 4, P], F32))
            sums_ps = own.enter_context(nc.psum_tensor("sums_ps", [P, 2, H], F32))
            step, spread_ready, rows_ready, shifted, exp_ready, ends_ready, sums_ready = (
                sem(n) for n in ("softmax_step", "spread_ready", "best_rows_ready", "shifted", "exp_ready",
                                 "ends_ready", "border_sums_ready"))
            block = own.enter_context(nc.Block())

            def flat(t):
                return t[:, :, :].rearrange("p h t -> p (h t)")

            def back(t):
                return flat(t)[:, ::-1]

            @block.tensor
            def _(pe):
                pe.wait_ge(spread_ready, 1)
                for k in range(3):
                    ins = nc.tensor.matmul(spread_ps[:, k, :, :], ones[:, :], spread[:, 4 * k:4 * k + 4, :], start=True, stop=True)
                ins.then_inc(rows_ready, 1)
                pe.wait_ge(ends_ready, 1)
                for k, (from_first, from_last) in enumerate(((same_aa, same_ba), (same_ab, same_bb))):
                    nc.tensor.matmul(sums_ps[:, k, :], from_first[:, :], ends[:, 0, :], start=True, stop=False)
                    ins = nc.tensor.matmul(sums_ps[:, k, :], from_last[:, :], ends[:, 1, :], start=False, stop=True)
                ins.then_inc(sums_ready, 1)

            @block.scalar
            def _(act):
                act.wait_ge(shifted, 1)
                nc.scalar.activation(scores[:, :, :], scores[:, :, :], ACT.Exp).then_inc(exp_ready, 1)

            @block.vector
            def _(dve):
                v = nc.vector
                do = Chain(dve, step)

                def heads(ap):
                    return ap.unsqueeze(1).to_broadcast([P, H, T])

                edge_s, self_s = scores[:, 0:H, :], scores[:, H:2 * H, :]
                v.tensor_scalar(pen_same[:, :, :], heads(masks[:, :, 0]), 1.0, BIG, ALU.subtract, ALU.mult)
                v.tensor_scalar(pen_next[:, :, :], heads(same_next[:, :]), 1.0, BIG, ALU.subtract, ALU.mult)
                v.tensor_copy(one_same[:, :, :], heads(masks[:, :, 0]))
                v.tensor_copy(one_next[:, :, :], heads(same_next[:, :]))
                v.tensor_scalar(pen_first[:, :], is_first[:, :], 1.0, BIG, ALU.subtract, ALU.mult)
                v.tensor_scalar(pen_last[:, :], is_last[:, :], 1.0, BIG, ALU.subtract, ALU.mult)
                do.step(v.tensor_tensor(top[:, :, :], edge_s, self_s, ALU.max))
                v.tensor_tensor_scan(flat(fwd), flat(pen_same), flat(top), -BIG, ALU.add, ALU.max)
                do.step(v.tensor_tensor_scan(back(bwd), back(pen_next), back(top), -BIG, ALU.add, ALU.max))
                v.tensor_copy(ends[:, 0, :], bwd[:, :, 0])
                do.step(v.tensor_copy(ends[:, 1, :], fwd[:, :, T - 1]))
                v.tensor_tensor(spread[:, :, :], ident[:, :].unsqueeze(1).to_broadcast([P, 2 * H, P]),
                                ends[:, :, :].rearrange("p k h -> p (k h)").unsqueeze(2).to_broadcast([P, 2 * H, P]),
                                ALU.mult).then_inc(spread_ready, 1)
                do.step(v.tensor_tensor(top[:, :, :], fwd[:, :, :], bwd[:, :, :], ALU.max))
                dve.wait_ge(rows_ready, 1)
                for k, pen in enumerate((pen_a, pen_b)):
                    for piece in range(2):
                        for h in range(H):
                            row = piece * H + h
                            ins = v.tensor_tensor(cand[:, piece, h, :], spread_ps[:, row // 4, row % 4, :], pen[:, piece, :], ALU.add)
                    do.step(ins)
                    do.step(v.tensor_reduce(best2[:, :, :], cand[:, :, :, :], AX.X, ALU.max))
                    do.step(v.tensor_tensor(border_best[:, k, :], best2[:, 0, :], best2[:, 1, :], ALU.max))
                for k, pen in enumerate((pen_first, pen_last)):
                    for h in range(H):
                        ins = v.scalar_tensor_tensor(top[:, h, :], pen[:, :], border_best[:, k, h:h + 1], top[:, h, :], ALU.add, ALU.max)
                    do.step(ins)
                v.tensor_tensor(edge_s, edge_s, top[:, :, :], ALU.subtract)
                v.tensor_tensor(self_s, self_s, top[:, :, :], ALU.subtract).then_inc(shifted, 1)
                dve.wait_ge(exp_ready, 1)
                v.tensor_tensor_scan(flat(fwd), flat(one_same), edge_s.rearrange("p h t -> p (h t)"), 0.0, ALU.mult, ALU.add)
                do.step(v.tensor_tensor_scan(back(bwd), back(one_next), edge_s.rearrange("p h t -> p (h t)")[:, ::-1], 0.0, ALU.mult, ALU.add))
                v.tensor_copy(ends[:, 0, :], bwd[:, :, 0])
                v.tensor_copy(ends[:, 1, :], fwd[:, :, T - 1]).then_inc(ends_ready, 1)
                do.step(v.tensor_tensor(top[:, :, :], fwd[:, :, :], bwd[:, :, :], ALU.add))
                do.step(v.tensor_tensor(top[:, :, :], top[:, :, :], edge_s, ALU.subtract))
                do.step(v.tensor_tensor(top[:, :, :], top[:, :, :], self_s, ALU.add))
                dve.wait_ge(sums_ready, 1)
                do.step(v.tensor_copy(border_more[:, :, :], sums_ps[:, :, :]))
                for k, mask in enumerate((is_first, is_last)):
                    for h in range(H):
                        ins = v.scalar_tensor_tensor(top[:, h, :], mask[:, :], border_more[:, k, h:h + 1], top[:, h, :], ALU.mult, ALU.add)
                    do.step(ins)
                do.step(v.tensor_scalar(top[:, :, :], top[:, :, :], 1e-16, None, ALU.add))
                do.step(v.reciprocal(top[:, :, :], top[:, :, :]))
                do.step(v.tensor_tensor(alpha[:, :, :].rearrange("p t h -> p h t"), edge_s, top[:, :, :], ALU.mult))

        with ExitStack() as own:
            def tmp(name, shape, dt=F32):
                return sb(name, shape, dt, own)

            def pair(name, shape, dt=F32):
                return [tmp(f"m_{name}{c}", shape, dt) for c in range(2)]

            hrow = pair("hrow", [P, CT, 3 * D])
            xrow = pair("xrow", [P, CT, D])
            idx_c = pair("idx", [P, CT], U32)
            mask_c = pair("mask", [P, CT, 2])
            hdiff = pair("hdiff", [P, CT, D])
            wdiff = pair("wdiff", [P, CT, H, D])
            parts = pair("parts", [P, (NZ + 1) * P])
            run = pair("run", [P, CT, D])
            gat = pair("gat", [P, CT, D])
            gexp = pair("gexp", [P, CT, D])
            grelu = pair("grelu", [P, CT, D])
            half = tmp("m_half", [P, CT, D])
            cen = tmp("m_cen", [P, CT, D])
            border = tmp("m_border", [P, 2, D])
            x1 = pair("x1", [P, CT, D])
            stats = pair("stats", [P, CT, 6])
            sumq = pair("sumq", [P, CT, 2])
            diff = pair("diff", [P, CT])
            sqd = pair("sqd", [P, CT])
            var = pair("var", [P, CT])
            lnv = pair("lnv", [P, CT])
            rstd = pair("rstd", [P, CT])
            h1 = pair("h1", [P, CT, D])
            tr = [own.enter_context(nc.psum_tensor(f"m_tr{k}", [P, (NZ + 1) * P], F32)) for k in range(2)]
            mm = [own.enter_context(nc.psum_tensor(f"m_mm{k}", [P, CT, 2, D], F32)) for k in range(2)]
            ext_ps = own.enter_context(nc.psum_tensor("m_ext", [P, 2, D], F32))
            hrow_ready, xrow_ready, sidx_ready, x1_stored, h1_stored, scattered = (
                [sem(f"m_{n}{c}") for c in range(2)] for n in
                ("hrow_ready", "xrow_ready", "sidx_ready", "x1_stored", "h1_stored", "scattered"))
            (row_consts, wdiff_ready, tr_ready, parts_ready, mm_ready, gat_ready, gat_act, x1_ready, var_ready,
             rstd_ready, h1_ready, dve_step, act_step, border_sum, border_scattered) = (sem(f"m_{n}") for n in (
                 "row_consts", "wdiff_ready", "tr_ready", "parts_ready", "mm_ready", "gat_ready", "gat_act",
                 "x1_ready", "var_ready", "rstd_ready", "h1_ready", "dve_step", "act_step", "border_sum",
                 "border_scattered"))
            block = own.enter_context(nc.Block())

            def kth(i, c):
                return 2 * i + (c + 1)

            def cols(i, c):
                return bass.ds(i * PER + CT * c, CT)

            def scatter(table, idx, rows_ap, done):
                nc.gpsimd.indirect_dma_start(table, bass.IndirectOffsetOnAxis(ap=idx, axis=0), rows_ap, None,
                                             bounds_check=last_row[0], oob_is_err=False).then_inc(done, 16)

            @block.gpsimd
            def _(pool):
                last_row[0] = pool.to_reg(N - 1)
                for c in range(2):
                    nc.gpsimd.memset(hrow[c][:, :, 2 * D:3 * D], 0.0).then_inc(row_consts, 1)
                pool.wait_ge(row_consts, 2)
                for c in range(2):
                    nc.gpsimd.memset(hrow[c][:, :, 2 * D:2 * D + 1], 1.0).then_inc(row_consts, 1)
                with pool.Fori(0, TURNS) as i:
                    for c in range(2):
                        pool.wait_ge(sidx_ready[c], 16 * (i + 1))
                        pool.wait_ge(h1_ready, kth(i, c))
                        pool.sem_inc(admitted, 1)
                        for j in range(CT):
                            scatter(h1_table, idx_c[c][:, j:j + 1], h1[c][:, j, :], scattered[c])
                pool.wait_ge(h1_ready, 2 * TURNS + 1)
                for k in range(2):
                    scatter(h1_table, border_idx[:, k:k + 1], border_h1[:, k, :], border_scattered)
                for c in range(2):
                    pool.wait_ge(scattered[c], 16 * CT * TURNS)
                pool.wait_ge(border_scattered, 32)

            @block.sync
            def _(sp):
                def load_h(i, c):
                    sp.dma_start(hrow[c][:, :, 0:2 * D], stash[:, cols(i, c), 0:2 * D]).then_inc(hrow_ready[c], 16)

                def load_x(i, c):
                    sp.dma_start(xrow[c][:, :, :], stash[:, cols(i, c), 2 * D:3 * D]).then_inc(xrow_ready[c], 16)

                def load_idx(i, c):
                    sp.dma_start(idx_c[c][:, :], scatter_idx[:, cols(i, c)]).then_inc(sidx_ready[c], 16)

                def store_x1(i, c):
                    sp.wait_ge(x1_ready, kth(i, c))
                    sp.dma_start(x1_edges[:, cols(i, c), :], x1[c][:, :, :]).then_inc(x1_stored[c], 16)

                def store_h1(i, c):
                    sp.wait_ge(h1_ready, kth(i, c))
                    sp.dma_start(h1_edges[:, cols(i, c), :], h1[c][:, :, :]).then_inc(h1_stored[c], 16)

                def turn(i):
                    for c in range(2):
                        if exists(*ago(i, c, -1)):
                            n, m = ago(i, c, 1), ago(i, c, -1)
                            wait_from(sp, tr_ready, 8 * n[0] + CT * (n[1] + 1))
                            load_h(*m)
                        if exists(*ago(i, c, 2)):
                            store_x1(i - 1, c)
                        if exists(i, c):
                            load_x(i, c)
                        j, d = ago(i, c, 3)
                        if exists(j, d):
                            store_h1(j, d)
                        j, d = ago(i, c, 1)
                        if exists(j, d):
                            wait_from(sp, scattered[d], 16 * CT * j)
                            load_idx(j, d)

                load_h(0, 0)
                turn(0)
                turn(1)
                with sp.Fori(2, TURNS - 1) as i:
                    turn(i)
                turn(TURNS - 1)
                turn(TURNS)
                store_h1(TURNS - 1, 1)
                for k, t in ((0, 0), (1, T - 1)):
                    sp.dma_start(hrow[0][:, k, 0:2 * D], stash[:, t, 0:2 * D]).then_inc(hrow_ready[0], 16)
                    sp.dma_start(xrow[0][:, k, :], stash[:, t, 2 * D:3 * D]).then_inc(xrow_ready[0], 16)
                for c in range(2):
                    sp.wait_ge(x1_stored[c], 16 * TURNS)
                    sp.wait_ge(h1_stored[c], 16 * TURNS)

            @block.tensor
            def _(pe):
                t = nc.tensor

                def transposes(i, n):
                    c, j = divmod(n, CT)
                    if j == 0:
                        pe.wait_ge(hrow_ready[c], 16 * (i + 1))
                        pe.wait_ge(wdiff_ready, kth(i, c))
                    wd = wdiff[c][:, j, :, :].rearrange("p h f -> p (h f)")
                    for z in range(NZ):
                        t.transpose(tr[n % 2][:, z * P:(z + 1) * P], wd[:, z * P:(z + 1) * P], ident[:, :])
                    t.transpose(tr[n % 2][:, NZ * P:], hrow[c][:, j, D:3 * D], ident[:, :]).then_inc(tr_ready, 1)

                def products(i, n):
                    c, j = divmod(n, CT)
                    pe.wait_ge(parts_ready, 8 * i + n + 1)
                    for z in range(NZ):
                        t.matmul(mm[c][:, j, 0, :], parts[n % 2][:, z * P:(z + 1) * P], w_msg[:, z, :],
                                 start=(z == 0), stop=(z == NZ - 1))
                    t.matmul(mm[c][:, j, 1, :], parts[n % 2][:, NZ * P:], base_w[:, :],
                             start=True, stop=True).then_inc(mm_ready, 1)

                pe.wait_ge(row_consts, 4)
                def turn(i, first=False):
                    for n in range(PER):
                        transposes(i, n)
                        if n:
                            products(i, n - 1)
                        elif not first:
                            products(i - 1, PER - 1)

                turn(0, True)
                with pe.Fori(1, TURNS) as i:
                    turn(i)
                products(TURNS - 1, PER - 1)
                pe.wait_ge(hrow_ready[0], 16 * TURNS + 32)
                pe.wait_ge(gat_ready, 2 * TURNS)
                for k in range(2):
                    t.transpose(tr[k][:, NZ * P:], hrow[0][:, k, D:3 * D], ident[:, :]).then_inc(tr_ready, 1)
                for k in range(2):
                    pe.wait_ge(parts_ready, 8 * TURNS + k + 1)
                    t.matmul(mm[0][:, k, 1, :], parts[k][:, NZ * P:], base_w[:, :], start=True, stop=True)
                for k, (from_first, from_last) in enumerate(((same_aa, same_ba), (same_ab, same_bb))):
                    t.matmul(ext_ps[:, k, :], from_first[:, :], first_sum[:, 0, :], start=True, stop=False)
                    ins = t.matmul(ext_ps[:, k, :], from_last[:, :], run[1][:, CT - 1, :], start=False, stop=True)
                ins.then_inc(border_sum, 1)

            @block.scalar
            def _(act):
                a = nc.scalar
                own_step = Chain(act, act_step)

                def copies(i, n):
                    act.wait_ge(tr_ready, 8 * i + n + 1)
                    a.activation(parts[n % 2][:, :], tr[n % 2][:, :], ACT.Copy).then_inc(parts_ready, 1)

                def selu_parts(i, c, k=CT):
                    act.wait_ge(gat_ready, kth(i, c))
                    a.activation(gexp[c][:, 0:k, :], gat[c][:, 0:k, :], ACT.Exp).then_inc(gat_act, 1)
                    a.activation(grelu[c][:, 0:k, :], gat[c][:, 0:k, :], ACT.Relu, scale=SELU_L).then_inc(gat_act, 1)

                def rstds(i, c, k=CT):
                    act.wait_ge(var_ready, kth(i, c))
                    own_step.step(a.activation(lnv[c][:, 0:k], var[c][:, 0:k], ACT.Ln, bias=eps[:, :], scale=1.0 / D))
                    a.activation(rstd[c][:, 0:k], lnv[c][:, 0:k], ACT.Exp, scale=-0.5).then_inc(rstd_ready, 1)

                def turn(i):
                    for c in range(2):
                        if exists(i, c):
                            copies(i, CT * c)
                        if exists(*ago(i, c, 2)):
                            rstds(*ago(i, c, 2))
                        if exists(i, c):
                            copies(i, CT * c + 1)
                        if exists(*ago(i, c, 1)):
                            selu_parts(*ago(i, c, 1))
                        if exists(i, c):
                            copies(i, CT * c + 2)
                            copies(i, CT * c + 3)

                turn(0)
                own_step.enter()
                with act.Fori(1, TURNS) as i:
                    own_step.turn(i - 1, 2)
                    turn(i)
                own_step.leave(TURNS - 1)
                turn(TURNS)
                for k in range(2):
                    act.wait_ge(tr_ready, 8 * TURNS + k + 1)
                    a.activation(parts[k][:, NZ * P:], tr[k][:, NZ * P:], ACT.Copy).then_inc(parts_ready, 1)
                selu_parts(TURNS, 0, 2)
                rstds(TURNS, 0, 2)

            @block.vector
            def _(dve):
                v = nc.vector
                do = Chain(dve, dve_step)

                def mid(ap, k):
                    return ap.unsqueeze(2).to_broadcast([P, k, D])

                def weigh(i, c):
                    dve.wait_ge(hrow_ready[c], 16 * (i + 1))
                    n = do.mark(v.tensor_tensor(hdiff[c][:, :, :], hrow[c][:, :, 0:D], hrow[c][:, :, D:2 * D], ALU.subtract))
                    wait_from(dve, gat_ready, 2 * i + (c - 1))
                    do.mark(v.tensor_copy(mask_c[c][:, :, :], masks[:, cols(i, c), :]))
                    do.wait(n)
                    v.tensor_tensor(wdiff[c][:, :, :, :], hdiff[c][:, :, :].unsqueeze(2).to_broadcast([P, CT, H, D]),
                                    alpha[:, cols(i, c), :].unsqueeze(3).to_broadcast([P, CT, H, D]), ALU.mult).then_inc(wdiff_ready, 1)

                def running_sums(i, c):
                    do.wait(do.n)
                    dve.wait_ge(mm_ready, 8 * i + CT * (c + 1))
                    for j in range(CT):
                        before = run[c][:, j - 1, :] if j else run[1 - c][:, CT - 1, :]
                        if j:
                            do.wait(do.n - 1)
                        do.mark(v.scalar_tensor_tensor(run[c][:, j, :], before, mask_c[c][:, j, 0:1], mm[c][:, j, 0, :], ALU.mult, ALU.add))
                        if j:
                            do.wait(do.n - 1)
                        do.mark(v.scalar_tensor_tensor(first_sum[:, 0, :], mm[c][:, j, 0, :], mask_c[c][:, j, 1:2], first_sum[:, 0, :], ALU.mult, ALU.add))
                    do.wait(do.n - 1)
                    v.tensor_tensor(gat[c][:, :, :], run[c][:, :, :], mm[c][:, :, 1, :], ALU.add).then_inc(gat_ready, 1)

                def selu_residual(i, c, x1_to, k=CT):
                    dve.wait_ge(gat_act, 4 * i + 2 * c + 1)
                    n = do.mark(v.tensor_scalar(gexp[c][:, 0:k, :], gexp[c][:, 0:k, :], 1.0, SELU_L * SELU_A, ALU.min, ALU.mult))
                    do.wait(n)
                    wait_from(dve, x1_ready, 2 * i + c)
                    dve.wait_ge(xrow_ready[c], 16 * (i + 1) + (16 if k < CT else 0))
                    n = do.mark(v.scalar_tensor_tensor(half[:, 0:k, :], gexp[c][:, 0:k, :], -SELU_L * SELU_A, xrow[c][:, 0:k, :], ALU.add, ALU.add))
                    do.wait(n)
                    dve.wait_ge(gat_act, 4 * i + 2 * c + 2)
                    wait_from(dve, h1_ready, 2 * i + (c - 1))
                    if k == CT:
                        wait_from(dve, x1_stored[c], 16 * i)
                    v.tensor_tensor(x1_to, half[:, 0:k, :], grelu[c][:, 0:k, :], ALU.add).then_inc(x1_ready, 1)
                    dve.wait_ge(x1_ready, kth(i, c))
                    for r in range(k):
                        ins = v.bn_stats(stats[c][:, r, :], x1_to[:, r, :])
                    do.step(ins)
                    st, sq, df, dd, va = stats[c][:, 0:k, :], sumq[c][:, 0:k, :], diff[c][:, 0:k], sqd[c][:, 0:k], var[c][:, 0:k]
                    nd = do.mark(v.tensor_tensor(df, st[:, :, 1], st[:, :, 4], ALU.subtract))
                    do.mark(v.tensor_tensor(sq, st[:, :, 1:3], st[:, :, 4:6], ALU.add))
                    do.wait(nd)
                    do.step(v.scalar_tensor_tensor(dd, df, D / 4.0, df, ALU.mult, ALU.mult))
                    v.tensor_tensor(va, dd, sq[:, :, 1], ALU.add).then_inc(var_ready, 1)

                def apply(i, c, x1_from, h1_to, k=CT):
                    wait_from(dve, h1_ready, 2 * i + c)
                    n = do.mark(v.scalar_tensor_tensor(cen[:, 0:k, :], mid(sumq[c][:, 0:k, 0], k), -0.5, x1_from, ALU.mult, ALU.add))
                    do.wait(n)
                    dve.wait_ge(rstd_ready, kth(i, c))
                    if k == CT:
                        wait_from(dve, scattered[c], 16 * CT * i)
                        wait_from(dve, h1_stored[c], 16 * i)
                    v.scalar_tensor_tensor(h1_to, cen[:, 0:k, :], 0.0, mid(rstd[c][:, 0:k], k), ALU.max, ALU.mult).then_inc(h1_ready, 1)

                def turn(i):
                    for c in range(2):
                        if exists(*ago(i, c, 1)):
                            running_sums(*ago(i, c, 1))
                        if exists(*ago(i, c, 2)):
                            apply(i - 1, c, x1[c][:, :, :], h1[c][:, :, :])
                        if exists(*ago(i, c, -1)):
                            weigh(*ago(i, c, -1))
                        if exists(*ago(i, c, 1)):
                            j, d = ago(i, c, 1)
                            selu_residual(j, d, x1[d][:, :, :])

                do.step(v.memset(run[1][:, :, :], 0.0))
                weigh(0, 0)
                turn(0)
                do.enter()
                with dve.Fori(1, TURNS - 1) as i:
                    do.turn(i - 1, 34)
                    turn(i)
                do.leave(TURNS - 2)
                turn(TURNS - 1)
                turn(TURNS)
                dve.wait_ge(border_sum, 1)
                do.step(v.tensor_tensor(border[:, 0, :], first_sum[:, 0, :], ext_ps[:, 0, :], ALU.add))
                do.step(v.tensor_tensor(border[:, 1, :], run[1][:, CT - 1, :], ext_ps[:, 1, :], ALU.add))
                v.tensor_tensor(gat[0][:, 0:2, :], border[:, :, :], mm[0][:, 0:2, 1, :], ALU.add).then_inc(gat_ready, 1)
                selu_residual(TURNS, 0, border_x1[:, :, :], 2)
                apply(TURNS, 0, border_x1[:, :, :], border_h1[:, :, :], 2)

        with ExitStack() as own:
            def tmp(name, shape, dt=F32):
                return sb(name, shape, dt, own)

            def pair(name, shape, dt=F32):
                return [tmp(f"n_{name}{c}", shape, dt) for c in range(2)]

            gidx = pair("gidx", [P, CT, 2], U32)
            sidx = pair("sidx", [P, CT], U32)
            mask_c = pair("mask", [P, CT, 2])
            grow = pair("grow", [P, CT, KW])
            hrow = pair("hrow", [P, CT * D])
            xrow = pair("xrow", [P, CT, D])
            growT = pair("growT", [KW, CT * P])
            hrowT = pair("hrowT", [P, CT * D])
            run = pair("run", [P, CT, D])
            pre = pair("pre", [P, CT, D])
            res = pair("res", [P, CT, D])
            border = tmp("n_border", [P, 2, D])
            ea_p = edge_attr[0:FULL * T, :].rearrange("(p t) w -> p t w", t=T)
            tr_g = [own.enter_context(nc.psum_tensor(f"n_trg{k}", [KW, CT * P], F32)) for k in range(2)]
            tr_h = [own.enter_context(nc.psum_tensor(f"n_trh{k}", [P, CT * D], F32)) for k in range(2)]
            mm = [own.enter_context(nc.psum_tensor(f"n_mm{k}", [P, 2, CT, D], F32)) for k in range(2)]
            ext_ps = own.enter_context(nc.psum_tensor("n_ext", [P, 2, D], F32))
            gidx_ready, sidx_ready, gathered, attr_ready, rows_ready, scattered = (
                [sem(f"n_{n}{c}") for c in range(2)] for n in
                ("gidx_ready", "sidx_ready", "gathered", "attr_ready", "rows_ready", "scattered"))
            (tr_ready, copied, mm_ready, sum_ready, res_ready, dve_step, border_sum, border_scattered, attr_zeroed) = (
                sem(f"n_{n}") for n in ("tr_ready", "copied", "mm_ready", "sum_ready", "res_ready", "dve_step",
                                        "border_sum", "border_scattered", "attr_zeroed"))
            block = own.enter_context(nc.Block())

            @block.gpsimd
            def _(pool):
                last_row[0] = pool.to_reg(N - 1)

                def gathers(i, c):
                    pool.wait_ge(gidx_ready[c], 16 * (i + 1))
                    pool.sem_inc(admitted, 1)
                    for j in range(CT):
                        nc.gpsimd.indirect_dma_start(
                            grow[c][:, j, 0:D], None, h1_table,
                            bass.IndirectOffsetOnAxis(ap=gidx[c][:, j, 0:1], axis=0),
                            bounds_check=last_row[0], oob_is_err=False).then_inc(gathered[c], 16)

                def scatters(i, c):
                    pool.wait_ge(sidx_ready[c], 16 * (i + 1))
                    pool.wait_ge(res_ready, kth(i, c))
                    pool.sem_inc(admitted, 1)
                    for j in range(CT):
                        scatter(out, sidx[c][:, j:j + 1], res[c][:, j, :], scattered[c])

                for c in range(2):
                    gathers(0, c)
                with pool.Fori(1, TURNS) as i:
                    for c in range(2):
                        pool.wait_ge(tr_ready, 2 * i + (c - 1))
                        gathers(i, c)
                        scatters(i - 1, c)
                for c in range(2):
                    scatters(TURNS - 1, c)
                pool.wait_ge(res_ready, 2 * TURNS + 1)
                for k in range(2):
                    scatter(out, border_idx[:, k:k + 1], res[0][:, k, :], border_scattered)
                for c in range(2):
                    pool.wait_ge(scattered[c], 16 * CT * TURNS)
                pool.wait_ge(border_scattered, 32)

            @block.sync
            def _(sp):
                def load_gidx(i, c):
                    sp.dma_start(gidx[c][:, :, :], gather_idx[:, cols(i, c), :]).then_inc(gidx_ready[c], 16)

                def load_sidx(i, c):
                    sp.dma_start(sidx[c][:, :], scatter_idx[:, cols(i, c)]).then_inc(sidx_ready[c], 16)

                def load_attr(i, c):
                    sp.dma_start(grow[c][0:FULL, :, D:KW], ea_p[:, cols(i, c), :]).then_inc(attr_ready[c], 16)
                    lo = i * PER + CT * c
                    start = lo * 1 if isinstance(i, int) else lo
                    sp.dma_start(grow[c][FULL:P, :, D:KW],
                                 edge_attr[bass.ds(start + FULL * T, CT), :].rearrange("(p t) w -> p t w", p=1)).then_inc(attr_ready[c], 16)

                def load_rows(i, c):
                    sp.dma_start(r3(hrow[c][:, :], D), h1_edges[:, cols(i, c), :]).then_inc(rows_ready[c], 16)
                    sp.dma_start(xrow[c][:, :, :], x1_edges[:, cols(i, c), :]).then_inc(rows_ready[c], 16)

                REAL = REST // PER
                assert REST % PER == 0

                def load_attr_full(i, c):
                    sp.dma_start(grow[c][0:FULL, :, D:KW], ea_p[:, cols(i, c), :]).then_inc(attr_ready[c], 16)

                def turn(i, attr, more=True):
                    for c in range(2):
                        sp.wait_ge(gathered[c], 16 * CT * (i + 1))
                        if more:
                            load_gidx(i + 1, c)
                        sp.wait_ge(tr_ready, kth(i, c))
                        if more:
                            attr(i + 1, c)
                        sp.wait_ge(res_ready, kth(i, c))
                        if more:
                            load_rows(i + 1, c)
                        sp.wait_ge(scattered[c], 16 * CT * i)
                        load_sidx(i, c)

                for c in range(2):
                    load_gidx(0, c)
                    load_attr(0, c)
                    load_rows(0, c)
                with sp.Fori(0, REAL - 1) as i:
                    turn(i, load_attr)
                with sp.Fori(REAL - 1, TURNS - 1) as i:
                    turn(i, load_attr_full)
                turn(TURNS - 1, None, False)

            @block.tensor
            def _(pe):
                t = nc.tensor

                def products_h(lhs, ps, pairs):
                    for j in range(pairs):
                        ins = t.matmul(ps[:, 1, 2 * j:2 * j + 2, :], lhs[:, j * P:(j + 1) * P], w1_blk[:, :], start=True, stop=True)
                    return ins

                def turn(i, attr_incs):
                    for c in range(2):
                        pe.wait_ge(gathered[c], 16 * CT * (i + 1))
                        pe.wait_ge(attr_ready[c], attr_incs)
                        pe.wait_ge(rows_ready[c], 32 * (i + 1))
                        pe.wait_ge(copied, 4 * i + 2 * c)
                        for j in range(CT):
                            t.transpose(tr_g[c][:, j * P:(j + 1) * P], grow[c][:, j, :], ident[:, :])
                        for j in range(CT // 2):
                            ins = t.transpose(tr_h[c][:, j * P:(j + 1) * P], hrow[c][:, j * P:(j + 1) * P], ident[:, :])
                        ins.then_inc(tr_ready, 1)
                        pe.wait_ge(copied, 4 * i + 2 * c + 2)
                        pe.wait_ge(sum_ready, 2 * i + c)
                        for j in range(CT):
                            t.matmul(mm[c][:, 0, j, :], growT[c][:, j * P:(j + 1) * P], w1_all[:, :], start=True, stop=True)
                        products_h(hrowT[c], mm[c], CT // 2).then_inc(mm_ready, 1)

                REAL = REST // PER
                with pe.Fori(0, REAL) as i:
                    turn(i, 32 * (i + 1))
                with pe.Fori(REAL, TURNS) as i:
                    turn(i, 16 * (i + 1) + 16 * REAL)
                pe.wait_ge(sum_ready, 2 * TURNS)
                t.transpose(tr_h[0][:, 0:P], border_h1[:, :, :].rearrange("p k f -> p (k f)"), ident[:, :]).then_inc(tr_ready, 1)
                pe.wait_ge(copied, 4 * TURNS + 1)
                products_h(hrowT[0], mm[0], 1)
                for k, (from_first, from_last) in enumerate(((same_aa, same_ba), (same_ab, same_bb))):
                    t.matmul(ext_ps[:, k, :], from_first[:, :], first_sum[:, 1, :], start=True, stop=False)
                    ins = t.matmul(ext_ps[:, k, :], from_last[:, :], run[1][:, CT - 1, :], start=False, stop=True)
                ins.then_inc(border_sum, 1)

            @block.scalar
            def _(act):
                a = nc.scalar
                with act.Fori(0, TURNS) as i:
                    for c in range(2):
                        act.wait_ge(tr_ready, kth(i, c))
                        act.wait_ge(mm_ready, 2 * i + c)
                        a.activation(growT[c][:, :], tr_g[c][:, :], ACT.Copy).then_inc(copied, 1)
                        a.activation(hrowT[c][:, :], tr_h[c][:, :], ACT.Copy).then_inc(copied, 1)
                act.wait_ge(tr_ready, 2 * TURNS + 1)
                act.wait_ge(mm_ready, 2 * TURNS)
                a.activation(hrowT[0][:, 0:P], tr_h[0][:, 0:P], ACT.Copy).then_inc(copied, 1)

            @block.vector
            def _(dve):
                v = nc.vector
                do = Chain(dve, dve_step)

                def close(pre_ap, sum_ap, h_ap, x_ap, res_ap, k):
                    dve.wait_ge(res_ready_now[0], res_ready_now[1])
                    v.tensor_tensor(pre_ap, sum_ap, h_ap, ALU.add).then_inc(sum_ready, 1)
                    dve.wait_ge(sum_ready, res_ready_now[1] + 1)
                    do.step(v.tensor_tensor(pre_ap, pre_ap, bias1_b[:, :].unsqueeze(1).to_broadcast([P, k, D]), ALU.add))
                    v.scalar_tensor_tensor(res_ap, pre_ap, 0.0, x_ap, ALU.max, ALU.add).then_inc(res_ready, 1)

                res_ready_now = [res_ready, 0]
                do.step(v.memset(run[1][:, :, :], 0.0))
                do.enter()
                with dve.Fori(0, TURNS) as i:
                    do.turn(i, 2 * (2 * CT + 2))
                    for c in range(2):
                        do.step(v.tensor_copy(mask_c[c][:, :, :], masks[:, cols(i, c), :]))
                        dve.wait_ge(mm_ready, kth(i, c))
                        for j in range(CT):
                            before = run[c][:, j - 1, :] if j else run[1 - c][:, CT - 1, :]
                            if j:
                                do.wait(do.n - 1)
                            do.mark(v.scalar_tensor_tensor(run[c][:, j, :], before, mask_c[c][:, j, 0:1], mm[c][:, 0, j, :], ALU.mult, ALU.add))
                            if j:
                                do.wait(do.n - 1)
                            do.mark(v.scalar_tensor_tensor(first_sum[:, 1, :], mm[c][:, 0, j, :], mask_c[c][:, j, 1:2], first_sum[:, 1, :], ALU.mult, ALU.add))
                        do.wait(do.n - 1)
                        dve.wait_ge(rows_ready[c], 32 * (i + 1))
                        dve.wait_ge(scattered[c], 16 * CT * i)
                        res_ready_now[1] = 2 * i + c
                        close(pre[c][:, :, :], run[c][:, :, :], mm[c][:, 1, :, :], xrow[c][:, :, :], res[c][:, :, :], CT)
                do.leave(TURNS)
                dve.wait_ge(border_sum, 1)
                do.step(v.tensor_tensor(border[:, 0, :], first_sum[:, 1, :], ext_ps[:, 0, :], ALU.add))
                do.step(v.tensor_tensor(border[:, 1, :], run[1][:, CT - 1, :], ext_ps[:, 1, :], ALU.add))
                dve.wait_ge(scattered[0], 16 * CT * TURNS)
                res_ready_now[1] = 2 * TURNS
                close(pre[0][:, 0:2, :], border[:, :, :], mm[0][:, 1, 0:2, :], border_x1[:, :, :], res[0][:, 0:2, :], 2)





def kernel(x, src, dst, edge_attr_16, L0_gnn_W_l, L0_gnn_W_r, L0_gnn_att, L0_gnn_bias, L1_gnn_W, L1_gnn_b):
    import numpy as np
    import concourse.bacc as bacc
    from concourse.bass_utils import run_bass_kernel_spmd

    nc = bacc.Bacc("TRN2", target_bir_lowering=False, num_devices=1)
    named = dict(x=x, src=src, dst=dst, edge_attr=edge_attr_16, w_l=L0_gnn_W_l, w_r=L0_gnn_W_r, att=L0_gnn_att,
                 bias0=L0_gnn_bias, w1=L1_gnn_W, bias1=L1_gnn_b)
    arrays, args = {}, {}
    for name, a in named.items():
        a = np.ascontiguousarray(a)
        arrays[f"in_{name}"] = a
        args[name] = nc.dram_tensor(f"in_{name}", a.shape, mybir.dt.from_np(a.dtype), kind="ExternalInput").ap()
    out = nc.dram_tensor("out_x", tuple(x.shape), F32, kind="ExternalOutput").ap()
    gnn_program(nc, out=out, **args)
    result = run_bass_kernel_spmd(nc, [arrays], core_ids=[0])
    return result.results[0]["out_x"]
```

```python
from contextlib import ExitStack

import concourse.bass as bass
from concourse import mybir

F32 = mybir.dt.float32
BF16 = mybir.dt.bfloat16
I32 = mybir.dt.int32
U32 = mybir.dt.uint32
ALU = mybir.AluOpType
ACT = mybir.ActivationFunctionType
AX = mybir.AxisListType

P = 128
EPS = 1e-5
BIG = 1e30
SELU_L = 1.0507009873554805
SELU_A = 1.6732632423543772
SELU_LA = SELU_L * SELU_A
LN_EXP_SET = 6


class Chain:

    def __init__(self, eng, sem):
        self.eng, self.sem, self.start, self.n = eng, sem, 0, 0

    def turn(self, i, per_loop):
        self.start, self.n, self.per_loop = self.base + i * per_loop, 0, per_loop

    def enter(self):
        self.base = self.start + self.n

    def leave(self, turns):
        assert self.n == self.per_loop, (self.n, self.per_loop)
        self.start, self.n = self.base + turns * self.per_loop, 0

    def mark(self, ins):
        ins.then_inc(self.sem, 1)
        self.n += 1
        return self.n

    def wait(self, n):
        self.eng.wait_ge(self.sem, self.start + n)

    def step(self, ins):
        self.wait(self.mark(ins))


def gnn_program(nc, x, src, dst, edge_attr, w_l, w_r, att, bias0, w1, bias1, out):
    N, D = x.shape
    E = src.shape[0]
    H = att.shape[0]
    EW = edge_attr.shape[1]
    KW = D + EW
    CT = 4
    PER = 2 * CT
    TURNS = -(-E // (P * PER))
    T = TURNS * PER
    FULL = E // T
    REST = E - FULL * T
    HD = H * D
    NZ = HD // P
    ROWS = 8
    BLOCK = 2 * ROWS * P
    LAST = N - BLOCK
    assert (TURNS - 1) * BLOCK < N <= TURNS * BLOCK and NZ == 3 and FULL == P - 1

    h1_table = nc.dram_tensor("h1_table", (N, D), F32).ap()
    stash = nc.dram_tensor("stash", (P, T, 3 * D), F32).ap()
    x1_edges = nc.dram_tensor("x1_edges", (P, T, D), F32).ap()
    h1_edges = nc.dram_tensor("h1_edges", (P, T, D), F32).ap()

    keep = ExitStack()
    last_row = [N - 1]

    def sb(name, shape, dt=F32, ctx=keep):
        return ctx.enter_context(nc.sbuf_tensor(name, shape, dt))

    def sem(name):
        return keep.enter_context(nc.semaphore(name))

    def exists(i, c):
        return not isinstance(i, int) or 0 <= 2 * i + c < 2 * TURNS

    def ago(i, c, k):
        return i + (c - k) // 2, (c - k) % 2

    def wait_from(eng, semaphore, value):
        if not isinstance(value, int) or value > 0:
            eng.wait_ge(semaphore, value)

    def r3(ap, f):
        return ap.rearrange("p (r f) -> p r f", f=f)

    with keep:
        gather_idx = sb("gather_idx", [P, T + PER, 2], U32)
        scatter_idx = sb("scatter_idx", [P, T], U32)
        border_idx = sb("border_idx", [P, 2], U32)
        masks = sb("masks", [P, T, 2])
        same_next = sb("same_next", [P, T])
        is_last = sb("is_last", [P, T])
        is_first = sb("is_first", [P, T])
        ident = sb("ident", [P, P])
        ones = sb("ones", [P, P])
        eps = sb("eps", [P, 1])
        w_edge = sb("w_edge", [P, HD])
        w_self = sb("w_self", [P, HD])
        att_blk = sb("att_blk", [P, NZ, 32])
        lin_e = sb("lin_e", [P, 32])
        lin_s = sb("lin_s", [P, 32])
        select = sb("select", [P, 2 * H])
        mean_blk = sb("mean_blk", [P, P])
        w_msg = sb("w_msg", [P, NZ, D])
        base_w = sb("base_w", [P, D])
        w1_blk = sb("w1_blk", [P, P])
        w1_all = sb("w1_all", [KW, D])
        ones16 = sb("ones16", [3 * 32, P], BF16)
        bias_parts = sb("bias_parts", [3 * 32, 2, ROWS * D], BF16)
        selu_la = sb("selu_la", [P, 1])
        bias0_b = sb("bias0_b", [P, D])
        bias1_b = sb("bias1_b", [P, D])
        same_aa = sb("same_aa", [P, P])
        same_ba = sb("same_ba", [P, P])
        same_ab = sb("same_ab", [P, P])
        same_bb = sb("same_bb", [P, P])
        pen_a = sb("pen_a", [P, 2, P])
        pen_b = sb("pen_b", [P, 2, P])
        scores = sb("scores", [P, 2 * H, T])
        alpha = sb("alpha", [P, T, H])
        first_sum = sb("first_sum", [P, 2, D])
        border_x1 = sb("border_x1", [P, 2, D])
        border_h1 = sb("border_h1", [P, 2, D])
        admitted = sem("admitted")

        with ExitStack() as own:
            def tmp(name, shape, dt=F32):
                return sb(name, shape, dt, own)

            src_i = tmp("src_i", [P, T], I32)
            dst_i = tmp("dst_i", [P, T], I32)
            dstf = tmp("dstf", [P, T])
            work = tmp("work", [P, T])
            endm = tmp("endm", [P, T])
            notab = tmp("notab", [P, 1])
            cnt = tmp("cnt", [P, 2])
            bidf = tmp("bidf", [P, 2])
            before = tmp("before", [P, P])
            dg = tmp("dg", [P, 2, P])
            eq = tmp("eq", [P, P])
            att_b = tmp("att_b", [P, HD])
            prod = tmp("prod", [P, HD])
            wl_lo = tmp("wl_lo", [P, HD])
            wl_sum = tmp("wl_sum", [P, D])
            part = tmp("part", [P, 3, D], BF16)
            rest = tmp("rest", [P, 2, D])
            rows_ps = own.enter_context(nc.psum_tensor("rows_ps", [P, 2, P], F32))
            zeroed, loaded_e, loaded_w, pooled, diag, rowed, step = (
                sem(n) for n in ("zeroed", "loaded_edges", "loaded_weights", "pool_consts", "diag_ready",
                                 "rows_ready", "setup_step"))
            n_w = [0]
            block = own.enter_context(nc.Block())

            @block.gpsimd
            def _(pool):
                nc.gpsimd.memset(src_i[:, :], 0).then_inc(zeroed, 1)
                nc.gpsimd.memset(dst_i[:, :], N).then_inc(zeroed, 1)
                for t in (att_blk[:, :, :], base_w[:, :], w1_blk[:, :]):
                    nc.gpsimd.memset(t, 0.0).then_inc(zeroed, 1)
                nc.gpsimd.memset(ident[:, :], 0.0).then_inc(pooled, 1)
                nc.gpsimd.memset(before[:, :], 1.0).then_inc(pooled, 1)
                pool.wait_ge(pooled, 2)
                nc.gpsimd.affine_select(out=ident[:, :], in_=ident[:, :], compare_op=ALU.not_equal, fill=1.0,
                                        base=0, pattern=[[-1, P]], channel_multiplier=1).then_inc(pooled, 1)
                nc.gpsimd.affine_select(out=before[:, :], in_=before[:, :], compare_op=ALU.is_gt, fill=0.0,
                                        base=0, pattern=[[-1, P]], channel_multiplier=1).then_inc(pooled, 1)

            @block.sync
            def _(sp):
                sp.wait_ge(zeroed, 2)
                for tile, dram in ((src_i, src), (dst_i, dst)):
                    sp.dma_start(tile[0:FULL, :], dram[0:FULL * T].rearrange("(p t) -> p t", t=T)).then_inc(loaded_e, 16)
                    sp.dma_start(tile[FULL:P, 0:REST], dram[FULL * T:E].rearrange("(p t) -> p t", p=1)).then_inc(loaded_e, 16)
                sp.wait_ge(zeroed, 5)

                def load(to, what):
                    sp.dma_start(to, what).then_inc(loaded_w, 16)
                    n_w[0] += 16

                load(w_edge[0:D, :], w_l)
                load(w_edge[D:P, :], w_r)
                load(wl_lo[0:D, :], w_l)
                load(wl_lo[D:P, :], w_l)
                for h in range(H):
                    rows = slice((h % 2) * D, (h % 2) * D + D)
                    load(att_blk[rows, h // 2, h:h + 1], att[h, :].rearrange("(f o) -> f o", o=1))
                load(att_b[:, :], att.rearrange("h f -> (h f)").partition_broadcast(P))
                load(bias0_b[:, :], bias0.partition_broadcast(P))
                load(bias1_b[:, :], bias1.partition_broadcast(P))
                load(base_w[D:D + 1, :], bias0.rearrange("(o f) -> o f", o=1))
                load(w1_all[:, :], w1)
                load(w1_blk[0:D, 0:D], w1[0:D, :])
                load(w1_blk[D:P, D:P], w1[0:D, :])

            @block.tensor
            def _(pe):
                pe.wait_ge(diag, 1)
                nc.tensor.matmul(rows_ps[:, :, :], ones[:, :], dg[:, :, :], start=True, stop=True).then_inc(rowed, 1)

            @block.vector
            def _(dve):
                v = nc.vector
                do = Chain(dve, step)
                do.step(v.memset(ones[:, :], 1.0))
                do.step(v.memset(eps[:, :], EPS))
                do.step(v.memset(selu_la[:, :], SELU_LA))
                do.step(v.memset(ones16[:, :], 1.0))
                do.step(v.memset(bias_parts[:, :, :], 0.0))
                for t in (w_self[:, :], lin_e[:, :], lin_s[:, :], select[:, :], mean_blk[:, :]):
                    do.step(v.memset(t, 0.0))
                do.step(v.memset(first_sum[:, :, :], 0.0))
                do.step(v.memset(gather_idx[:, :, :], 0))
                dve.wait_ge(loaded_e, 64)
                do.step(v.tensor_copy(dstf[:, :], dst_i[:, :]))
                do.step(v.tensor_copy(gather_idx[:, 0:T, 0], src_i[:, :]))
                do.step(v.tensor_scalar(gather_idx[:, 0:T, 1], dstf[:, :], float(N - 1), None, ALU.min))
                a, b = dstf[:, 0:1], dstf[:, T - 1:T]
                dve.wait_ge(pooled, 4)
                do.step(v.tensor_scalar(dg[:, 0, :], ident[:, :], a, None, ALU.mult))
                v.tensor_scalar(dg[:, 1, :], ident[:, :], b, None, ALU.mult).then_inc(diag, 1)
                do.step(v.memset(masks[:, 0:1, 0:1], 0.0))
                do.step(v.memset(same_next[:, T - 1:T], 0.0))
                do.step(v.tensor_tensor(masks[:, 1:T, 0], dstf[:, 1:T], dstf[:, 0:T - 1], ALU.is_equal))
                do.step(v.tensor_copy(same_next[:, 0:T - 1], masks[:, 1:T, 0]))
                do.step(v.tensor_scalar(is_first[:, :], dstf[:, :], a, None, ALU.is_equal))
                do.step(v.tensor_copy(masks[:, :, 1], is_first[:, :]))
                do.step(v.tensor_tensor(notab[:, :], a, b, ALU.not_equal))
                do.step(v.tensor_scalar(is_last[:, :], dstf[:, :], b, notab[:, :], ALU.is_equal, ALU.mult))
                do.step(v.tensor_tensor(work[:, :], is_first[:, :], is_last[:, :], ALU.add))
                do.step(v.tensor_tensor(work[:, :], work[:, :], same_next[:, :], ALU.add))
                do.step(v.tensor_scalar(endm[:, :], work[:, :], 0.0, None, ALU.is_equal))
                do.step(v.tensor_scalar(work[:, :], dstf[:, :], float(N), None, ALU.subtract))
                do.step(v.tensor_tensor(work[:, :], work[:, :], endm[:, :], ALU.mult))
                do.step(v.tensor_scalar(scatter_idx[:, :], work[:, :], float(N), None, ALU.add))
                dve.wait_ge(rowed, 1)
                row_a, row_b = rows_ps[:, 0, :], rows_ps[:, 1, :]
                for pen, k, row, own_node in ((pen_a, 0, row_a, a), (pen_a, 1, row_b, a),
                                              (pen_b, 0, row_a, b), (pen_b, 1, row_b, b)):
                    do.step(v.tensor_scalar(eq[:, :], row, own_node, None, ALU.is_equal))
                    do.step(v.tensor_scalar(pen[:, k, :], eq[:, :], 1.0, BIG, ALU.subtract, ALU.mult))
                    if pen is pen_a and k == 0:
                        do.step(v.tensor_tensor(same_aa[:, :], eq[:, :], ident[:, :], ALU.subtract))
                        do.step(v.tensor_tensor(eq[:, :], eq[:, :], before[:, :], ALU.mult))
                        do.step(v.tensor_reduce(cnt[:, 0:1], eq[:, :], AX.X, ALU.add))
                    if pen is pen_b and k == 0:
                        do.step(v.tensor_reduce(cnt[:, 1:2], eq[:, :], AX.X, ALU.add))
                do.step(v.tensor_scalar(same_ba[:, :], row_a, b, notab[:, :], ALU.is_equal, ALU.mult))
                do.step(v.tensor_scalar(same_ab[:, :], row_b, a, None, ALU.is_equal))
                do.step(v.tensor_scalar(eq[:, :], row_b, b, None, ALU.is_equal))
                do.step(v.tensor_tensor(eq[:, :], eq[:, :], ident[:, :], ALU.subtract))
                do.step(v.tensor_scalar(same_bb[:, :], eq[:, :], notab[:, :], None, ALU.mult))
                for k, node in ((0, a), (1, b)):
                    do.step(v.tensor_scalar(cnt[:, k:k + 1], cnt[:, k:k + 1], 0.0, None, ALU.is_equal))
                    do.step(v.tensor_scalar(bidf[:, k:k + 1], node, float(N), None, ALU.subtract))
                do.step(v.tensor_tensor(bidf[:, :], bidf[:, :], cnt[:, :], ALU.mult))
                do.step(v.tensor_scalar(border_idx[:, :], bidf[:, :], float(N), None, ALU.add))
                dve.wait_ge(loaded_w, n_w[0])
                do.step(v.tensor_tensor(w_self[D:P, :], wl_lo[D:P, :], w_edge[D:P, :], ALU.add))
                for w, lin in ((w_edge, lin_e), (w_self, lin_s)):
                    do.step(v.tensor_tensor(prod[:, :], w[:, :], att_b[:, :], ALU.mult))
                    do.step(v.tensor_reduce(lin[:, 0:H], r3(prod[:, :], D), AX.X, ALU.add))
                    do.step(v.tensor_scalar(lin[:, 0:H], lin[:, 0:H], 0.2, None, ALU.mult))
                do.step(v.tensor_scalar(prod[:, :], wl_lo[:, :], 1.0 / H, None, ALU.mult))
                do.step(v.tensor_reduce(wl_sum[:, :], prod[:, :].rearrange("p (h f) -> p f h", f=D), AX.X, ALU.add))
                do.step(v.tensor_copy(mean_blk[0:D, 0:D], wl_sum[0:D, :]))
                do.step(v.tensor_copy(mean_blk[D:P, D:P], wl_sum[D:P, :]))
                do.step(v.tensor_copy(base_w[0:D, :], wl_sum[0:D, :]))
                for h in range(H):
                    rows = slice((h % 2) * D, (h % 2) * D + D)
                    do.step(v.tensor_copy(w_msg[rows, h // 2, :], prod[rows, h * D:(h + 1) * D]))
                for layer, bias in enumerate((bias0_b, bias1_b)):
                    left = bias[:, :]
                    for k in range(3):
                        do.step(v.tensor_copy(part[:, k, :], left))
                        row = slice(32 * k, 32 * k + 1)
                        do.step(v.tensor_copy(bias_parts[row, layer, :].rearrange("p (r f) -> p r f", f=D),
                                              part[row, k, :].unsqueeze(1).to_broadcast([1, ROWS, D])))
                        if k < 2:
                            do.step(v.tensor_tensor(rest[:, k, :], left, part[:, k, :], ALU.subtract))
                            left = rest[:, k, :]
                for g in range(4):
                    do.step(v.tensor_copy(select[32 * g:32 * g + H, H * (g // 2):H * (g // 2) + H],
                                          ident[32 * g:32 * g + H, 32 * g:32 * g + H]))

        with ExitStack() as own:
            def tmp(name, shape, dt=F32):
                return sb(name, shape, dt, own)

            def pair(name, shape, dt=F32):
                return [tmp(f"{name}{c}", shape, dt) for c in range(2)]

            R2 = 2 * ROWS
            idx_c = pair("idx_c", [P, CT, 2], U32)
            xe = pair("xe", [P, CT, 2, D])
            xd = pair("xd", [P, ROWS, D])
            he = pair("he", [P, CT * 2 * D])
            hd = pair("hd", [P, ROWS * D])
            h1 = pair("h1", [P, ROWS * D])
            stats = pair("stats", [P, R2, 6])
            sumq = pair("sumq", [P, R2, 2])
            diff = pair("diff", [P, R2])
            var = pair("var", [P, R2])
            lnv = pair("lnv", [P, R2])
            rstd = pair("rstd", [P, R2])
            stats1 = pair("stats1", [P, ROWS, 6])
            sumq1 = pair("sumq1", [P, ROWS, 2])
            diff1 = pair("diff1", [P, ROWS])
            var1 = pair("var1", [P, ROWS])
            lnv1 = pair("lnv1", [P, ROWS])
            rstd1 = pair("rstd1", [P, ROWS])
            xc = [tmp(f"xc{k}", [P, ROWS, D]) for k in range(4)]
            heT = pair("heT", [P, CT * P])
            hdT = pair("hdT", [P, ROWS * D])
            relu_z = pair("relu_z", [P, 2 * NZ, CT * P])
            scoreT = pair("scoreT", [P, CT * P])
            gexp = pair("gexp", [P, ROWS * D])
            grelu = pair("grelu", [P, ROWS * D])
            x1 = pair("x1", [P, ROWS, D])
            res = pair("res", [P, ROWS * D])

            def ps(name, shape):
                return own.enter_context(nc.psum_tensor(name, shape, F32))

            tr_e = ps("tr_e", [P, CT * P])
            tr_d = ps("tr_d", [P, CT * P])
            z_ps = [ps(f"z_ps{k}", [P, CT * P]) for k in range(3)]
            sc_ps = ps("sc_ps", [P, CT * P])
            sel_ps = ps("sel_ps", [P, CT, 2 * H])
            mm_d = ps("mm_d", [P, ROWS * D])

            idx_ready, gathered, x_ready, x_stashed, h_stashed, h1_stored, out_stored = (
                [sem(f"{n}{c}") for c in range(2)] for n in
                ("idx_ready", "gathered", "x_ready", "x_stashed", "h_stashed", "h1_stored", "out_stored"))
            hd_tr, hd_T, mm_ready = (
                [sem(f"{n}{layer}") for layer in range(2)] for n in ("hd_transposed", "hdT_ready", "mm_ready"))
            (mm_read, var_ready, rstd_ready, h_ready, he_tr, he_T, z_ready, relu_ready, round_ready, scoreT_ready,
             sel_ready, scores_done, gat_act, x1_ready, var1_ready,
             rstd1_ready, h1_ready, res_ready, dve_step, act_step) = (sem(n) for n in (
                 "mm_read", "var_ready", "rstd_ready", "h_ready", "he_transposed", "heT_ready", "z_ready", "relu_ready",
                 "round_ready", "scoreT_ready", "sel_ready", "scores_done",
                 "gat_act", "x1_ready", "var1_ready", "rstd1_ready", "h1_ready",
                 "res_ready", "dve_step", "act_step"))
            block = own.enter_context(nc.Block())
            LASTI = TURNS - 1

            def kth(i, c):
                return 2 * i + (c + 1)

            def nodes(i):
                return LAST if isinstance(i, int) and i == LASTI else i * BLOCK

            def dense_rows(dram, i, c):
                return dram[bass.ds(nodes(i), BLOCK), :].rearrange("(p u) f -> p u f", u=2 * ROWS)[:, c * ROWS:(c + 1) * ROWS, :]

            @block.gpsimd
            def _(pool):
                last_row[0] = pool.to_reg(N - 1)

                def gathers(i, c):
                    pool.wait_ge(idx_ready[c], 16 * (i + 1))
                    pool.sem_inc(admitted, 1)
                    for j in range(CT):
                        for s in range(2):
                            nc.gpsimd.indirect_dma_start(
                                xe[c][:, j, s, :], None, x,
                                bass.IndirectOffsetOnAxis(ap=idx_c[c][:, j, s:s + 1], axis=0),
                                bounds_check=last_row[0], oob_is_err=False).then_inc(gathered[c], 16)

                for c in range(2):
                    gathers(0, c)
                with pool.Fori(1, TURNS) as i:
                    for c in range(2):
                        pool.wait_ge(h_ready, 2 * i + (c - 1))
                        pool.wait_ge(x_stashed[c], 16 * i)
                        gathers(i, c)

            @block.sync
            def _(sp):
                def load_idx(i, c):
                    sp.dma_start(idx_c[c][:, :, :], gather_idx[:, bass.ds(i * PER + CT * c, CT), :]).then_inc(idx_ready[c], 16)

                def load_x(i, c):
                    sp.dma_start(xd[c][:, :, :], dense_rows(x, i, c)).then_inc(x_ready[c], 16)

                def stashes(i, c):
                    sp.wait_ge(h_ready, kth(i, c))
                    sp.dma_start(stash[:, bass.ds(i * PER + CT * c, CT), 0:2 * D], r3(he[c][:, :], 2 * D)).then_inc(h_stashed[c], 16)
                    sp.dma_start(stash[:, bass.ds(i * PER + CT * c, CT), 2 * D:3 * D], xe[c][:, :, 1, :]).then_inc(x_stashed[c], 16)

                def store(i, c, ready, dram, rows, stored):
                    sp.wait_ge(ready, kth(i, c))
                    if isinstance(i, int) and i == LASTI:
                        for k in range(2):
                            sp.wait_ge(stored[k], 16 * LASTI)
                    sp.dma_start(dense_rows(dram, i, c), r3(rows[c][:, :], D)).then_inc(stored[c], 16)

                def turn(i):
                    for c in range(2):
                        j, d = ago(i, c, -3)
                        if exists(j, d):
                            wait_from(sp, gathered[d], 32 * CT * j)
                            load_idx(j, d)
                        if exists(*ago(i, c, 2)):
                            store(i - 1, c, res_ready, out, res, out_stored)
                        if exists(*ago(i, c, -2)):
                            sp.wait_ge(x1_ready, kth(i, c))
                            load_x(i + 1, c)
                        if exists(*ago(i, c, -1)):
                            stashes(*ago(i, c, -1))
                        if exists(*ago(i, c, 1)):
                            store(*ago(i, c, 1), h1_ready, h1_table, h1, h1_stored)

                for c in range(2):
                    load_idx(0, c)
                    load_x(0, c)
                wait_from(sp, gathered[0], 32 * CT)
                load_idx(1, 0)
                stashes(0, 0)
                turn(0)
                with sp.Fori(1, LASTI - 1) as i:
                    turn(i)
                turn(LASTI - 1)
                turn(LASTI)
                turn(TURNS)
                for c in range(2):
                    for s in (x_stashed, h_stashed, h1_stored, out_stored):
                        sp.wait_ge(s[c], 16 * TURNS)

            @block.tensor
            def _(pe):
                t = nc.tensor

                def transpose_e(i, c):
                    pe.wait_ge(h_ready, kth(i, c))
                    wait_from(pe, he_T, 2 * i + c)
                    for j in range(CT):
                        ins = t.transpose(tr_e[:, j * P:(j + 1) * P], he[c][:, j * P:(j + 1) * P], ident[:, :])
                    ins.then_inc(he_tr, 1)

                def before_this(i, c, layer, done):
                    if layer == 0:
                        wait_from(pe, done[1], 2 * i + (c - 2))
                    elif exists(*ago(i, c, -2)):
                        pe.wait_ge(done[0], 2 * i + (c + 3))
                    else:
                        pe.wait_ge(done[0], 2 * TURNS)
                        pe.wait_ge(done[1], 2 * i + c)

                def transpose_d(i, c, layer):
                    if layer == 0:
                        pe.wait_ge(h_ready, kth(i, c))
                    else:
                        pe.wait_ge(h1_ready, kth(i, c))
                    before_this(i, c, layer, hd_T)
                    h = (hd, h1)[layer][c]
                    for j in range(ROWS // 2):
                        ins = t.transpose(tr_d[:, j * P:(j + 1) * P], h[:, j * P:(j + 1) * P], ident[:, :])
                    ins.then_inc(hd_tr[layer], 1)

                def dense_mm(i, c, layer):
                    pe.wait_ge(hd_T[layer], kth(i, c))
                    before_this(i, c, layer, (mm_read, res_ready))
                    t.matmul(mm_d[:, :], ones16[:, :], bias_parts[:, layer, :], start=True, stop=False)
                    for j in range(ROWS // 2):
                        ins = t.matmul(mm_d[:, j * P:(j + 1) * P], hdT[c][:, j * P:(j + 1) * P],
                                       (mean_blk, w1_blk)[layer][:, :], start=False, stop=(j == ROWS // 2 - 1))
                    ins.then_inc(mm_ready[layer], 1)

                ORDER = [(0, 0), (0, 2), (1, 0), (1, 2), (0, 1), (1, 1)]

                def project(i, c, part):
                    if part == 0:
                        pe.wait_ge(he_T, kth(i, c))
                    for n in range(3 * part, 3 * part + 3):
                        kind, z = ORDER[n]
                        pe.wait_ge(relu_ready, 12 * i + 6 * c + n + 1)
                        t.matmul(z_ps[n % 3][:, :], (w_edge, w_self)[kind][:, z * P:(z + 1) * P], heT[c][:, :],
                                 start=True, stop=True).then_inc(z_ready, 1)

                def rounds(i, c):
                    pe.wait_ge(relu_ready, 12 * i + 6 * c + 6 + 3)
                    for g, (n, z) in enumerate(((0, 0), (1, 2), (2, 0), (3, 2))):
                        t.matmul(sc_ps[32 * g:32 * g + 32, :], att_blk[:, z, :], relu_z[c][:, n, :], start=True, stop=False)
                    t.matmul(sc_ps[0:32, :], att_blk[:, 1, :], relu_z[c][:, 4, :], start=False, stop=True)
                    t.matmul(sc_ps[32:64, :], lin_e[:, :], heT[c][:, :], start=False, stop=True)
                    t.matmul(sc_ps[64:96, :], att_blk[:, 1, :], relu_z[c][:, 5, :], start=False, stop=True)
                    t.matmul(sc_ps[96:128, :], lin_s[:, :], heT[c][:, :], start=False, stop=True).then_inc(round_ready, 1)

                def select_scores(i, c):
                    pe.wait_ge(scoreT_ready, kth(i, c))
                    wait_from(pe, scores_done, 2 * i + c)
                    for j in range(CT):
                        ins = t.matmul(sel_ps[:, j, :], scoreT[c][:, j * P:(j + 1) * P], select[:, :], start=True, stop=True)
                    ins.then_inc(sel_ready, 1)

                def turn(i):
                    for c in range(2):
                        now, previous, older = (exists(*ago(i, c, k)) for k in range(3))
                        if now:
                            transpose_d(i, c, 0)
                            transpose_e(i, c)
                        if previous:
                            rounds(*ago(i, c, 1))
                        if now:
                            project(i, c, 0)
                            dense_mm(i, c, 0)
                        if older:
                            transpose_d(i - 1, c, 1)
                        if now:
                            project(i, c, 1)
                        if previous:
                            select_scores(*ago(i, c, 1))
                        if older:
                            dense_mm(i - 1, c, 1)

                turn(0)
                with pe.Fori(1, TURNS) as i:
                    turn(i)
                turn(TURNS)

            @block.scalar
            def _(act):
                a = nc.scalar
                own_step = Chain(act, act_step)

                def rstds(i, c, layer):
                    v, l, r = ((var, lnv, rstd), (var1, lnv1, rstd1))[layer]
                    act.wait_ge((var_ready, var1_ready)[layer], kth(i, c))
                    n = own_step.mark(a.activation(l[c][:, :], v[c][:, :], ACT.Ln, bias=eps[:, :], scale=1.0 / D))
                    own_step.wait(n)
                    a.activation(r[c][:, :], l[c][:, :], ACT.Exp, scale=-0.5).then_inc((rstd_ready, rstd1_ready)[layer], 1)

                def copy_e(i, c):
                    act.wait_ge(he_tr, kth(i, c))
                    a.activation(heT[c][:, :], tr_e[:, :], ACT.Copy).then_inc(he_T, 1)

                def copy_d(i, c, layer):
                    act.wait_ge(hd_tr[layer], kth(i, c))
                    a.activation(hdT[c][:, :], tr_d[:, :], ACT.Copy).then_inc(hd_T[layer], 1)

                def relus(i, c, which):
                    for n in which:
                        act.wait_ge(z_ready, 12 * i + 6 * c + n + 1)
                        a.activation(relu_z[c][:, n, :], z_ps[n % 3][:, :], ACT.Relu, scale=0.8).then_inc(relu_ready, 1)

                def copy_scores(i, c):
                    act.wait_ge(round_ready, kth(i, c))
                    a.activation(scoreT[c][:, :], sc_ps[:, :], ACT.Copy).then_inc(scoreT_ready, 1)

                def selu_parts(i, c):
                    act.wait_ge(mm_ready[0], kth(i, c))
                    n = own_step.mark(a.activation(gexp[c][:, :], mm_d[:, :], ACT.Exp))
                    a.activation(grelu[c][:, :], mm_d[:, :], ACT.Relu, scale=SELU_L).then_inc(mm_read, 1)
                    own_step.wait(n)
                    a.activation(gexp[c][:, :], gexp[c][:, :], ACT.Relu, scale=-SELU_LA, bias=selu_la[:, :]).then_inc(gat_act, 1)

                def turn(i):
                    for c in range(2):
                        now, previous, following = exists(i, c), exists(*ago(i, c, 1)), exists(*ago(i, c, -1))
                        if now:
                            copy_d(i, c, 0)
                            copy_e(i, c)
                        if previous:
                            copy_scores(*ago(i, c, 1))
                        if now:
                            relus(i, c, (0, 1, 2))
                        if previous:
                            rstds(*ago(i, c, 1), 1)
                        if now:
                            selu_parts(i, c)
                        if exists(*ago(i, c, 2)):
                            copy_d(i - 1, c, 1)
                        if now:
                            relus(i, c, (3, 4))
                        if following:
                            rstds(*ago(i, c, -1), 0)
                        if now:
                            relus(i, c, (5,))

                act.add_instruction(mybir.InstLoadActFuncSet(
                    name=nc.get_next_instruction_name(), act_func_set_id=LN_EXP_SET, ins=[], outs=[]))
                act.sem_inc(relu_ready, 3)
                rstds(0, 0, 0)
                turn(0)
                own_step.enter()
                with act.Fori(1, LASTI) as i:
                    own_step.turn(i - 1, 6)
                    turn(i)
                own_step.leave(LASTI - 1)
                turn(LASTI)
                turn(TURNS)

            @block.vector
            def _(dve):
                v = nc.vector
                do = Chain(dve, dve_step)

                def mid(ap):
                    return ap.unsqueeze(2).to_broadcast([P, ROWS, D])

                def centre(to, sq, rows):
                    return do.mark(v.scalar_tensor_tensor(to, mid(sq), -0.5, rows, ALU.mult, ALU.add))

                def scale(to, cen, r):
                    return v.scalar_tensor_tensor(to, cen, 0.0, mid(r), ALU.max, ALU.mult)

                def halves(st, sq, df):
                    do.wait(do.n)
                    nd = do.mark(v.tensor_tensor(df[:, :], st[:, :, 1], st[:, :, 4], ALU.subtract))
                    do.mark(v.tensor_tensor(sq[:, :, :], st[:, :, 1:3], st[:, :, 4:6], ALU.add))
                    return nd

                def between(nd, df, va):
                    do.wait(nd)
                    return do.mark(v.scalar_tensor_tensor(va[:, :], df[:, :], D / 4.0, df[:, :], ALU.mult, ALU.mult))

                def total(n, sq, va, signal):
                    do.wait(n)
                    v.tensor_tensor(va[:, :], va[:, :], sq[:, :, 1], ALU.add).then_inc(signal, 1)

                def dense_stats(i, c):
                    dve.wait_ge(x_ready[c], 16 * (i + 1))
                    for r in range(ROWS):
                        v.bn_stats(stats[c][:, r, :], xd[c][:, r, :])

                def edge_stats(i, c):
                    dve.wait_ge(gathered[c], 32 * CT * (i + 1))
                    for r in range(ROWS):
                        ins = v.bn_stats(stats[c][:, ROWS + r, :], xe[c][:, r // 2, r % 2, :])
                    do.mark(ins)
                    return halves(stats[c], sumq[c], diff[c])

                def norm_between(i, c, nd):
                    n = between(nd, diff[c], var[c])
                    wait_from(dve, h_ready, 2 * i + c)
                    do.wait(n - 1)
                    nx = centre(xc[0][:, :, :], sumq[c][:, 0:ROWS, 0], xd[c][:, :, :])
                    total(n, sumq[c], var[c], var_ready)
                    centre(xc[1][:, :, :], sumq[c][:, ROWS:R2, 0], xe[c][:, :, :, :].rearrange("p j s f -> p (j s) f"))
                    return nx

                def norm_dense(i, c, nx):
                    do.wait(nx)
                    dve.wait_ge(rstd_ready, kth(i, c))
                    scale(r3(hd[c][:, :], D), xc[0][:, :, :], rstd[c][:, 0:ROWS])

                def norm_edges(i, c, nx):
                    do.wait(nx + 1)
                    wait_from(dve, h_stashed[c], 16 * i)
                    scale(r3(he[c][:, :], D), xc[1][:, :, :], rstd[c][:, ROWS:R2]).then_inc(h_ready, 1)

                def residual(i, c):
                    dve.wait_ge(mm_read, kth(i, c))
                    return do.mark(v.tensor_tensor(xc[2][:, :, :], xd[c][:, :, :], r3(grelu[c][:, :], D), ALU.add))

                def add_selu(i, c, n):
                    do.wait(n)
                    dve.wait_ge(gat_act, kth(i, c))
                    wait_from(dve, res_ready, 2 * i + (c - 1))
                    v.tensor_tensor(x1[c][:, :, :], xc[2][:, :, :], r3(gexp[c][:, :], D), ALU.subtract).then_inc(x1_ready, 1)

                def x1_stats(i, c):
                    dve.wait_ge(x1_ready, kth(i, c))
                    for r in range(ROWS):
                        ins = v.bn_stats(stats1[c][:, r, :], x1[c][:, r, :])
                    do.mark(ins)
                    return halves(stats1[c], sumq1[c], diff1[c])

                def norm1_between(i, c, nd):
                    n = between(nd, diff1[c], var1[c])
                    do.wait(nd + 1)
                    wait_from(dve, h1_ready, 2 * i + c)
                    centre(xc[3][:, :, :], sumq1[c][:, :, 0], x1[c][:, :, :])
                    total(n, sumq1[c], var1[c], var1_ready)

                def norm1_apply(i, c):
                    do.wait(do.n)
                    dve.wait_ge(rstd1_ready, kth(i, c))
                    wait_from(dve, h1_stored[c], 16 * i)
                    scale(r3(h1[c][:, :], D), xc[3][:, :, :], rstd1[c][:, :]).then_inc(h1_ready, 1)

                def keep_scores(i, c):
                    dve.wait_ge(sel_ready, kth(i, c))
                    v.tensor_copy(scores[:, :, bass.ds(i * PER + CT * c, CT)].rearrange("p g t -> p t g"), sel_ps[:, :, :]).then_inc(scores_done, 1)

                def dense_out(i, c):
                    dve.wait_ge(mm_ready[1], kth(i, c))
                    wait_from(dve, out_stored[c], 16 * i)
                    v.scalar_tensor_tensor(r3(res[c][:, :], D), r3(mm_d[:, :], D), 0.0, x1[c][:, :, :], ALU.max, ALU.add).then_inc(res_ready, 1)

                def turn(i):
                    for c in range(2):
                        now, previous, following = exists(i, c), exists(*ago(i, c, 1)), exists(*ago(i, c, -1))
                        before, after = ago(i, c, 1), ago(i, c, -1)
                        if following:
                            dense_stats(*after)
                            nx = norm_between(*after, edge_stats(*after))
                        if previous:
                            norm1_apply(*before)
                        if following:
                            norm_dense(*after, nx)
                            norm_edges(*after, nx)
                        if now:
                            n = residual(i, c)
                        if previous:
                            keep_scores(*before)
                        if exists(*ago(i, c, 2)):
                            dense_out(i - 1, c)
                        if now:
                            add_selu(i, c, n)
                            norm1_between(i, c, x1_stats(i, c))

                dense_stats(0, 0)
                nx = norm_between(0, 0, edge_stats(0, 0))
                norm_dense(0, 0, nx)
                norm_edges(0, 0, nx)
                turn(0)
                do.enter()
                with dve.Fori(1, LASTI) as i:
                    do.turn(i - 1, 24)
                    turn(i)
                do.leave(LASTI - 1)
                turn(LASTI)
                turn(TURNS)

        with ExitStack() as own:
            def tmp(name, shape, dt=F32):
                return sb(name, shape, dt, own)

            HT = H * T
            pen_same = tmp("pen_same", [P, H, T])
            pen_next = tmp("pen_next", [P, H, T])
            one_same = tmp("one_same", [P, H, T])
            one_next = tmp("one_next", [P, H, T])
            pen_first = tmp("pen_first", [P, T])
            pen_last = tmp("pen_last", [P, T])
            top = tmp("top", [P, H, T])
            fwd = tmp("fwd", [P, H, T])
            bwd = tmp("bwd", [P, H, T])
            ends = tmp("ends", [P, 2, H])
            spread = tmp("spread", [P, 2 * H, P])
            cand = tmp("cand", [P, 2, H, P])
            best2 = tmp("best2", [P, 2, H])
            border_best = tmp("border_best", [P, 2, H])
            border_more = tmp("border_more", [P, 2, H])
            spread_ps = own.enter_context(nc.psum_tensor("spread_ps", [P, 4, 4, P], F32))
            sums_ps = own.enter_context(nc.psum_tensor("sums_ps", [P, 2, H], F32))
            step, spread_ready, rows_ready, shifted, exp_ready, ends_ready, sums_ready = (
                sem(n) for n in ("softmax_step", "spread_ready", "best_rows_ready", "shifted", "exp_ready",
                                 "ends_ready", "border_sums_ready"))
            block = own.enter_context(nc.Block())

            def flat(t):
                return t[:, :, :].rearrange("p h t -> p (h t)")

            def back(t):
                return flat(t)[:, ::-1]

            @block.tensor
            def _(pe):
                pe.wait_ge(spread_ready, 1)
                for k in range(3):
                    ins = nc.tensor.matmul(spread_ps[:, k, :, :], ones[:, :], spread[:, 4 * k:4 * k + 4, :], start=True, stop=True)
                ins.then_inc(rows_ready, 1)
                pe.wait_ge(ends_ready, 1)
                for k, (from_first, from_last) in enumerate(((same_aa, same_ba), (same_ab, same_bb))):
                    nc.tensor.matmul(sums_ps[:, k, :], from_first[:, :], ends[:, 0, :], start=True, stop=False)
                    ins = nc.tensor.matmul(sums_ps[:, k, :], from_last[:, :], ends[:, 1, :], start=False, stop=True)
                ins.then_inc(sums_ready, 1)

            @block.scalar
            def _(act):
                act.wait_ge(shifted, 1)
                nc.scalar.activation(scores[:, :, :], scores[:, :, :], ACT.Exp).then_inc(exp_ready, 1)

            @block.vector
            def _(dve):
                v = nc.vector
                do = Chain(dve, step)

                def heads(ap):
                    return ap.unsqueeze(1).to_broadcast([P, H, T])

                edge_s, self_s = scores[:, 0:H, :], scores[:, H:2 * H, :]
                v.tensor_scalar(pen_same[:, :, :], heads(masks[:, :, 0]), 1.0, BIG, ALU.subtract, ALU.mult)
                v.tensor_scalar(pen_next[:, :, :], heads(same_next[:, :]), 1.0, BIG, ALU.subtract, ALU.mult)
                v.tensor_copy(one_same[:, :, :], heads(masks[:, :, 0]))
                v.tensor_copy(one_next[:, :, :], heads(same_next[:, :]))
                v.tensor_scalar(pen_first[:, :], is_first[:, :], 1.0, BIG, ALU.subtract, ALU.mult)
                v.tensor_scalar(pen_last[:, :], is_last[:, :], 1.0, BIG, ALU.subtract, ALU.mult)
                do.step(v.tensor_tensor(top[:, :, :], edge_s, self_s, ALU.max))
                v.tensor_tensor_scan(flat(fwd), flat(pen_same), flat(top), -BIG, ALU.add, ALU.max)
                do.step(v.tensor_tensor_scan(back(bwd), back(pen_next), back(top), -BIG, ALU.add, ALU.max))
                v.tensor_copy(ends[:, 0, :], bwd[:, :, 0])
                do.step(v.tensor_copy(ends[:, 1, :], fwd[:, :, T - 1]))
                v.tensor_tensor(spread[:, :, :], ident[:, :].unsqueeze(1).to_broadcast([P, 2 * H, P]),
                                ends[:, :, :].rearrange("p k h -> p (k h)").unsqueeze(2).to_broadcast([P, 2 * H, P]),
                                ALU.mult).then_inc(spread_ready, 1)
                do.step(v.tensor_tensor(top[:, :, :], fwd[:, :, :], bwd[:, :, :], ALU.max))
                dve.wait_ge(rows_ready, 1)
                for k, pen in enumerate((pen_a, pen_b)):
                    for piece in range(2):
                        for h in range(H):
                            row = piece * H + h
                            ins = v.tensor_tensor(cand[:, piece, h, :], spread_ps[:, row // 4, row % 4, :], pen[:, piece, :], ALU.add)
                    do.step(ins)
                    do.step(v.tensor_reduce(best2[:, :, :], cand[:, :, :, :], AX.X, ALU.max))
                    do.step(v.tensor_tensor(border_best[:, k, :], best2[:, 0, :], best2[:, 1, :], ALU.max))
                for k, pen in enumerate((pen_first, pen_last)):
                    for h in range(H):
                        ins = v.scalar_tensor_tensor(top[:, h, :], pen[:, :], border_best[:, k, h:h + 1], top[:, h, :], ALU.add, ALU.max)
                    do.step(ins)
                v.tensor_tensor(edge_s, edge_s, top[:, :, :], ALU.subtract)
                v.tensor_tensor(self_s, self_s, top[:, :, :], ALU.subtract).then_inc(shifted, 1)
                dve.wait_ge(exp_ready, 1)
                v.tensor_tensor_scan(flat(fwd), flat(one_same), edge_s.rearrange("p h t -> p (h t)"), 0.0, ALU.mult, ALU.add)
                do.step(v.tensor_tensor_scan(back(bwd), back(one_next), edge_s.rearrange("p h t -> p (h t)")[:, ::-1], 0.0, ALU.mult, ALU.add))
                v.tensor_copy(ends[:, 0, :], bwd[:, :, 0])
                v.tensor_copy(ends[:, 1, :], fwd[:, :, T - 1]).then_inc(ends_ready, 1)
                do.step(v.tensor_tensor(top[:, :, :], fwd[:, :, :], bwd[:, :, :], ALU.add))
                do.step(v.tensor_tensor(top[:, :, :], top[:, :, :], edge_s, ALU.subtract))
                do.step(v.tensor_tensor(top[:, :, :], top[:, :, :], self_s, ALU.add))
                dve.wait_ge(sums_ready, 1)
                do.step(v.tensor_copy(border_more[:, :, :], sums_ps[:, :, :]))
                for k, mask in enumerate((is_first, is_last)):
                    for h in range(H):
                        ins = v.scalar_tensor_tensor(top[:, h, :], mask[:, :], border_more[:, k, h:h + 1], top[:, h, :], ALU.mult, ALU.add)
                    do.step(ins)
                do.step(v.tensor_scalar(top[:, :, :], top[:, :, :], 1e-16, None, ALU.add))
                do.step(v.reciprocal(top[:, :, :], top[:, :, :]))
                do.step(v.tensor_tensor(alpha[:, :, :].rearrange("p t h -> p h t"), edge_s, top[:, :, :], ALU.mult))

        with ExitStack() as own:
            def tmp(name, shape, dt=F32):
                return sb(name, shape, dt, own)

            def pair(name, shape, dt=F32):
                return [tmp(f"m_{name}{c}", shape, dt) for c in range(2)]

            hrow = pair("hrow", [P, CT, 3 * D])
            xrow = pair("xrow", [P, CT, D])
            idx_c = pair("idx", [P, CT], U32)
            mask_c = pair("mask", [P, CT, 2])
            hdiff = pair("hdiff", [P, CT, D])
            wdiff = pair("wdiff", [P, CT, H, D])
            parts = [tmp(f"m_parts{k}", [P, (NZ + 1) * P]) for k in range(4)]
            run = pair("run", [P, CT, D])
            gat = pair("gat", [P, CT, D])
            gexp = pair("gexp", [P, CT, D])
            grelu = pair("grelu", [P, CT, D])
            half = tmp("m_half", [P, CT, D])
            cen = tmp("m_cen", [P, CT, D])
            border = tmp("m_border", [P, 2, D])
            x1 = pair("x1", [P, CT, D])
            stats = pair("stats", [P, CT, 6])
            sumq = pair("sumq", [P, CT, 2])
            diff = pair("diff", [P, CT])
            sqd = pair("sqd", [P, CT])
            var = pair("var", [P, CT])
            lnv = pair("lnv", [P, CT])
            rstd = pair("rstd", [P, CT])
            h1 = pair("h1", [P, CT, D])
            tr = [own.enter_context(nc.psum_tensor(f"m_tr{k}", [P, (NZ + 1) * P], F32)) for k in range(4)]
            mm = [own.enter_context(nc.psum_tensor(f"m_mm{k}", [P, CT, 2, D], F32)) for k in range(2)]
            ext_ps = own.enter_context(nc.psum_tensor("m_ext", [P, 2, D], F32))
            hrow_ready, xrow_ready, sidx_ready, x1_stored, h1_stored, scattered = (
                [sem(f"m_{n}{c}") for c in range(2)] for n in
                ("hrow_ready", "xrow_ready", "sidx_ready", "x1_stored", "h1_stored", "scattered"))
            (row_consts, wdiff_ready, tr_ready, parts_ready, mm_ready, gat_ready, gat_act, x1_ready, var_ready,
             rstd_ready, h1_ready, dve_step, act_step, border_sum, border_scattered) = (sem(f"m_{n}") for n in (
                 "row_consts", "wdiff_ready", "tr_ready", "parts_ready", "mm_ready", "gat_ready", "gat_act",
                 "x1_ready", "var_ready", "rstd_ready", "h1_ready", "dve_step", "act_step", "border_sum",
                 "border_scattered"))
            block = own.enter_context(nc.Block())

            def kth(i, c):
                return 2 * i + (c + 1)

            def cols(i, c):
                return bass.ds(i * PER + CT * c, CT)

            def scatter(table, idx, rows_ap, done):
                nc.gpsimd.indirect_dma_start(table, bass.IndirectOffsetOnAxis(ap=idx, axis=0), rows_ap, None,
                                             bounds_check=last_row[0], oob_is_err=False).then_inc(done, 16)

            @block.gpsimd
            def _(pool):
                last_row[0] = pool.to_reg(N - 1)
                for c in range(2):
                    nc.gpsimd.memset(hrow[c][:, :, 2 * D:3 * D], 0.0).then_inc(row_consts, 1)
                pool.wait_ge(row_consts, 2)
                for c in range(2):
                    nc.gpsimd.memset(hrow[c][:, :, 2 * D:2 * D + 1], 1.0).then_inc(row_consts, 1)
                with pool.Fori(0, TURNS) as i:
                    for c in range(2):
                        pool.wait_ge(sidx_ready[c], 16 * (i + 1))
                        pool.wait_ge(h1_ready, kth(i, c))
                        pool.sem_inc(admitted, 1)
                        for j in range(CT):
                            scatter(h1_table, idx_c[c][:, j:j + 1], h1[c][:, j, :], scattered[c])
                pool.wait_ge(h1_ready, 2 * TURNS + 1)
                for k in range(2):
                    scatter(h1_table, border_idx[:, k:k + 1], border_h1[:, k, :], border_scattered)
                for c in range(2):
                    pool.wait_ge(scattered[c], 16 * CT * TURNS)
                pool.wait_ge(border_scattered, 32)

            @block.sync
            def _(sp):
                def load_h(i, c):
                    sp.dma_start(hrow[c][:, :, 0:2 * D], stash[:, cols(i, c), 0:2 * D]).then_inc(hrow_ready[c], 16)

                def load_x(i, c):
                    sp.dma_start(xrow[c][:, :, :], stash[:, cols(i, c), 2 * D:3 * D]).then_inc(xrow_ready[c], 16)

                def load_idx(i, c):
                    sp.dma_start(idx_c[c][:, :], scatter_idx[:, cols(i, c)]).then_inc(sidx_ready[c], 16)

                def store_x1(i, c):
                    sp.wait_ge(x1_ready, kth(i, c))
                    sp.dma_start(x1_edges[:, cols(i, c), :], x1[c][:, :, :]).then_inc(x1_stored[c], 16)

                def store_h1(i, c):
                    sp.wait_ge(h1_ready, kth(i, c))
                    sp.dma_start(h1_edges[:, cols(i, c), :], h1[c][:, :, :]).then_inc(h1_stored[c], 16)

                def turn(i):
                    for c in range(2):
                        if exists(*ago(i, c, -1)):
                            n, m = ago(i, c, 1), ago(i, c, -1)
                            wait_from(sp, tr_ready, 8 * n[0] + CT * (n[1] + 1))
                            load_h(*m)
                        if exists(*ago(i, c, 2)):
                            store_x1(i - 1, c)
                        if exists(i, c):
                            load_x(i, c)
                        j, d = ago(i, c, 3)
                        if exists(j, d):
                            store_h1(j, d)
                        j, d = ago(i, c, 1)
                        if exists(j, d):
                            wait_from(sp, scattered[d], 16 * CT * j)
                            load_idx(j, d)

                load_h(0, 0)
                turn(0)
                turn(1)
                with sp.Fori(2, TURNS - 1) as i:
                    turn(i)
                turn(TURNS - 1)
                turn(TURNS)
                store_h1(TURNS - 1, 1)
                for k, t in ((0, 0), (1, T - 1)):
                    sp.dma_start(hrow[0][:, k, 0:2 * D], stash[:, t, 0:2 * D]).then_inc(hrow_ready[0], 16)
                    sp.dma_start(xrow[0][:, k, :], stash[:, t, 2 * D:3 * D]).then_inc(xrow_ready[0], 16)
                for c in range(2):
                    sp.wait_ge(x1_stored[c], 16 * TURNS)
                    sp.wait_ge(h1_stored[c], 16 * TURNS)

            @block.tensor
            def _(pe):
                t = nc.tensor

                def transposes(i, n):
                    c, j = divmod(n, CT)
                    if j == 0:
                        pe.wait_ge(hrow_ready[c], 16 * (i + 1))
                        pe.wait_ge(wdiff_ready, kth(i, c))
                    wd = wdiff[c][:, j, :, :].rearrange("p h f -> p (h f)")
                    for z in range(NZ):
                        t.transpose(tr[n % 4][:, z * P:(z + 1) * P], wd[:, z * P:(z + 1) * P], ident[:, :])
                    t.transpose(tr[n % 4][:, NZ * P:], hrow[c][:, j, D:3 * D], ident[:, :]).then_inc(tr_ready, 1)

                def products(i, n):
                    c, j = divmod(n, CT)
                    pe.wait_ge(parts_ready, 8 * i + n + 1)
                    for z in range(NZ):
                        t.matmul(mm[c][:, j, 0, :], parts[n % 4][:, z * P:(z + 1) * P], w_msg[:, z, :],
                                 start=(z == 0), stop=(z == NZ - 1))
                    t.matmul(mm[c][:, j, 1, :], parts[n % 4][:, NZ * P:], base_w[:, :],
                             start=True, stop=True).then_inc(mm_ready, 1)

                pe.wait_ge(row_consts, 4)
                with pe.Fori(0, TURNS) as i:
                    for c in range(2):
                        for j in range(CT):
                            transposes(i, CT * c + j)
                        for j in range(CT):
                            products(i, CT * c + j)
                pe.wait_ge(hrow_ready[0], 16 * TURNS + 32)
                pe.wait_ge(gat_ready, 2 * TURNS)
                for k in range(2):
                    t.transpose(tr[k][:, NZ * P:], hrow[0][:, k, D:3 * D], ident[:, :]).then_inc(tr_ready, 1)
                for k in range(2):
                    pe.wait_ge(parts_ready, 8 * TURNS + k + 1)
                    t.matmul(mm[0][:, k, 1, :], parts[k][:, NZ * P:], base_w[:, :], start=True, stop=True)
                for k, (from_first, from_last) in enumerate(((same_aa, same_ba), (same_ab, same_bb))):
                    t.matmul(ext_ps[:, k, :], from_first[:, :], first_sum[:, 0, :], start=True, stop=False)
                    ins = t.matmul(ext_ps[:, k, :], from_last[:, :], run[1][:, CT - 1, :], start=False, stop=True)
                ins.then_inc(border_sum, 1)

            @block.scalar
            def _(act):
                a = nc.scalar
                own_step = Chain(act, act_step)

                def copies(i, n):
                    act.wait_ge(tr_ready, 8 * i + n + 1)
                    a.activation(parts[n % 4][:, :], tr[n % 4][:, :], ACT.Copy).then_inc(parts_ready, 1)

                def selu_parts(i, c, k=CT):
                    act.wait_ge(gat_ready, kth(i, c))
                    n = own_step.mark(a.activation(gexp[c][:, 0:k, :], gat[c][:, 0:k, :], ACT.Exp))
                    a.activation(grelu[c][:, 0:k, :], gat[c][:, 0:k, :], ACT.Relu, scale=SELU_L).then_inc(gat_act, 1)
                    own_step.wait(n)
                    a.activation(gexp[c][:, 0:k, :], gexp[c][:, 0:k, :], ACT.Relu, scale=-SELU_LA, bias=selu_la[:, :]).then_inc(gat_act, 1)

                def rstds(i, c, k=CT):
                    act.wait_ge(var_ready, kth(i, c))
                    own_step.step(a.activation(lnv[c][:, 0:k], var[c][:, 0:k], ACT.Ln, bias=eps[:, :], scale=1.0 / D))
                    a.activation(rstd[c][:, 0:k], lnv[c][:, 0:k], ACT.Exp, scale=-0.5).then_inc(rstd_ready, 1)

                def turn(i):
                    for c in range(2):
                        if exists(i, c):
                            copies(i, CT * c)
                        if exists(*ago(i, c, 2)):
                            rstds(*ago(i, c, 2))
                        if exists(i, c):
                            copies(i, CT * c + 1)
                        if exists(*ago(i, c, 1)):
                            selu_parts(*ago(i, c, 1))
                        if exists(i, c):
                            copies(i, CT * c + 2)
                            copies(i, CT * c + 3)

                turn(0)
                own_step.enter()
                with act.Fori(1, TURNS) as i:
                    own_step.turn(i - 1, 4)
                    turn(i)
                own_step.leave(TURNS - 1)
                turn(TURNS)
                for k in range(2):
                    act.wait_ge(tr_ready, 8 * TURNS + k + 1)
                    a.activation(parts[k][:, NZ * P:], tr[k][:, NZ * P:], ACT.Copy).then_inc(parts_ready, 1)
                selu_parts(TURNS, 0, 2)
                rstds(TURNS, 0, 2)

            @block.vector
            def _(dve):
                v = nc.vector
                do = Chain(dve, dve_step)

                def mid(ap, k):
                    return ap.unsqueeze(2).to_broadcast([P, k, D])

                def subtract(i, c):
                    dve.wait_ge(hrow_ready[c], 16 * (i + 1))
                    n = do.mark(v.tensor_tensor(hdiff[c][:, :, :], hrow[c][:, :, 0:D], hrow[c][:, :, D:2 * D], ALU.subtract))
                    wait_from(dve, gat_ready, 2 * i + (c - 1))
                    do.mark(v.tensor_copy(mask_c[c][:, :, :], masks[:, cols(i, c), :]))
                    return n

                def weigh(i, c, n):
                    do.wait(n)
                    v.tensor_tensor(wdiff[c][:, :, :, :], hdiff[c][:, :, :].unsqueeze(2).to_broadcast([P, CT, H, D]),
                                    alpha[:, cols(i, c), :].unsqueeze(3).to_broadcast([P, CT, H, D]), ALU.mult).then_inc(wdiff_ready, 1)

                def running_sums(i, c):
                    do.wait(do.n)
                    dve.wait_ge(mm_ready, 8 * i + CT * (c + 1))
                    for j in range(CT):
                        before = run[c][:, j - 1, :] if j else run[1 - c][:, CT - 1, :]
                        if j:
                            do.wait(do.n - 1)
                        do.mark(v.scalar_tensor_tensor(run[c][:, j, :], before, mask_c[c][:, j, 0:1], mm[c][:, j, 0, :], ALU.mult, ALU.add))
                        if j:
                            do.wait(do.n - 1)
                        do.mark(v.scalar_tensor_tensor(first_sum[:, 0, :], mm[c][:, j, 0, :], mask_c[c][:, j, 1:2], first_sum[:, 0, :], ALU.mult, ALU.add))
                    do.wait(do.n - 1)
                    v.tensor_tensor(gat[c][:, :, :], run[c][:, :, :], mm[c][:, :, 1, :], ALU.add).then_inc(gat_ready, 1)

                def residual(i, c, k=CT):
                    dve.wait_ge(gat_act, 4 * i + 2 * c + 1)
                    dve.wait_ge(xrow_ready[c], 16 * (i + 1) + (16 if k < CT else 0))
                    return do.mark(v.tensor_tensor(half[:, 0:k, :], xrow[c][:, 0:k, :], grelu[c][:, 0:k, :], ALU.add))

                def add_selu(i, c, n, x1_to, k=CT):
                    do.wait(n)
                    dve.wait_ge(gat_act, 4 * i + 2 * c + 2)
                    if k == CT:
                        wait_from(dve, x1_stored[c], 16 * i)
                    v.tensor_tensor(x1_to, half[:, 0:k, :], gexp[c][:, 0:k, :], ALU.subtract).then_inc(x1_ready, 1)

                def x1_norm(i, c, x1_from, k=CT):
                    dve.wait_ge(x1_ready, kth(i, c))
                    for r in range(k):
                        ins = v.bn_stats(stats[c][:, r, :], x1_from[:, r, :])
                    do.step(ins)
                    st, sq, df, dd, va = stats[c][:, 0:k, :], sumq[c][:, 0:k, :], diff[c][:, 0:k], sqd[c][:, 0:k], var[c][:, 0:k]
                    nd = do.mark(v.tensor_tensor(df, st[:, :, 1], st[:, :, 4], ALU.subtract))
                    do.mark(v.tensor_tensor(sq, st[:, :, 1:3], st[:, :, 4:6], ALU.add))
                    do.wait(nd)
                    n = do.mark(v.scalar_tensor_tensor(dd, df, D / 4.0, df, ALU.mult, ALU.mult))
                    do.wait(n - 1)
                    wait_from(dve, h1_ready, 2 * i + c)
                    do.mark(v.scalar_tensor_tensor(cen[:, 0:k, :], mid(sumq[c][:, 0:k, 0], k), -0.5, x1_from, ALU.mult, ALU.add))
                    do.wait(n)
                    v.tensor_tensor(va, dd, sq[:, :, 1], ALU.add).then_inc(var_ready, 1)

                def apply(i, c, h1_to, k=CT):
                    do.wait(do.n)
                    dve.wait_ge(rstd_ready, kth(i, c))
                    if k == CT:
                        wait_from(dve, scattered[c], 16 * CT * i)
                        wait_from(dve, h1_stored[c], 16 * i)
                    v.scalar_tensor_tensor(h1_to, cen[:, 0:k, :], 0.0, mid(rstd[c][:, 0:k], k), ALU.max, ALU.mult).then_inc(h1_ready, 1)

                def turn(i):
                    for c in range(2):
                        previous, following = exists(*ago(i, c, 1)), exists(*ago(i, c, -1))
                        j, d = ago(i, c, 1)
                        if previous:
                            running_sums(j, d)
                        if exists(*ago(i, c, 2)):
                            apply(i - 1, c, h1[c][:, :, :])
                        if following:
                            n = subtract(*ago(i, c, -1))
                            weigh(*ago(i, c, -1), n)
                        if previous:
                            n = residual(j, d)
                            add_selu(j, d, n, x1[d][:, :, :])
                            x1_norm(j, d, x1[d][:, :, :])

                do.step(v.memset(run[1][:, :, :], 0.0))
                weigh(0, 0, subtract(0, 0))
                turn(0)
                do.enter()
                with dve.Fori(1, TURNS - 1) as i:
                    do.turn(i - 1, 32)
                    turn(i)
                do.leave(TURNS - 2)
                turn(TURNS - 1)
                turn(TURNS)
                dve.wait_ge(border_sum, 1)
                do.step(v.tensor_tensor(border[:, 0, :], first_sum[:, 0, :], ext_ps[:, 0, :], ALU.add))
                do.step(v.tensor_tensor(border[:, 1, :], run[1][:, CT - 1, :], ext_ps[:, 1, :], ALU.add))
                v.tensor_tensor(gat[0][:, 0:2, :], border[:, :, :], mm[0][:, 0:2, 1, :], ALU.add).then_inc(gat_ready, 1)
                add_selu(TURNS, 0, residual(TURNS, 0, 2), border_x1[:, :, :], 2)
                x1_norm(TURNS, 0, border_x1[:, :, :], 2)
                apply(TURNS, 0, border_h1[:, :, :], 2)

        with ExitStack() as own:
            def tmp(name, shape, dt=F32):
                return sb(name, shape, dt, own)

            def pair(name, shape, dt=F32):
                return [tmp(f"n_{name}{c}", shape, dt) for c in range(2)]

            gidx = pair("gidx", [P, CT, 2], U32)
            sidx = pair("sidx", [P, CT], U32)
            mask_c = pair("mask", [P, CT, 2])
            grow = pair("grow", [P, CT, KW])
            hrow = pair("hrow", [P, CT * D])
            xrow = pair("xrow", [P, CT, D])
            growT = pair("growT", [KW, CT * P])
            hrowT = pair("hrowT", [P, CT * D])
            run = pair("run", [P, CT, D])
            pre = pair("pre", [P, CT, D])
            res = pair("res", [P, CT, D])
            border = tmp("n_border", [P, 2, D])
            ea_p = edge_attr[0:FULL * T, :].rearrange("(p t) w -> p t w", t=T)
            tr_g = [own.enter_context(nc.psum_tensor(f"n_trg{k}", [KW, CT * P], F32)) for k in range(2)]
            tr_h = [own.enter_context(nc.psum_tensor(f"n_trh{k}", [P, CT * D], F32)) for k in range(2)]
            mm = [own.enter_context(nc.psum_tensor(f"n_mm{k}", [P, 2, CT, D], F32)) for k in range(2)]
            ext_ps = own.enter_context(nc.psum_tensor("n_ext", [P, 2, D], F32))
            gidx_ready, sidx_ready, gathered, attr_ready, rows_ready, scattered = (
                [sem(f"n_{n}{c}") for c in range(2)] for n in
                ("gidx_ready", "sidx_ready", "gathered", "attr_ready", "rows_ready", "scattered"))
            (tr_ready, copied, mm_ready, sum_ready, res_ready, dve_step, border_sum, border_scattered, attr_zeroed) = (
                sem(f"n_{n}") for n in ("tr_ready", "copied", "mm_ready", "sum_ready", "res_ready", "dve_step",
                                        "border_sum", "border_scattered", "attr_zeroed"))
            block = own.enter_context(nc.Block())

            @block.gpsimd
            def _(pool):
                last_row[0] = pool.to_reg(N - 1)

                def gathers(i, c):
                    pool.wait_ge(gidx_ready[c], 16 * (i + 1))
                    pool.sem_inc(admitted, 1)
                    for j in range(CT):
                        nc.gpsimd.indirect_dma_start(
                            grow[c][:, j, 0:D], None, h1_table,
                            bass.IndirectOffsetOnAxis(ap=gidx[c][:, j, 0:1], axis=0),
                            bounds_check=last_row[0], oob_is_err=False).then_inc(gathered[c], 16)

                def scatters(i, c):
                    pool.wait_ge(sidx_ready[c], 16 * (i + 1))
                    pool.wait_ge(res_ready, kth(i, c))
                    pool.sem_inc(admitted, 1)
                    for j in range(CT):
                        scatter(out, sidx[c][:, j:j + 1], res[c][:, j, :], scattered[c])

                for c in range(2):
                    gathers(0, c)
                with pool.Fori(1, TURNS) as i:
                    for c in range(2):
                        pool.wait_ge(tr_ready, 2 * i + (c - 1))
                        gathers(i, c)
                        scatters(i - 1, c)
                for c in range(2):
                    scatters(TURNS - 1, c)
                pool.wait_ge(res_ready, 2 * TURNS + 1)
                for k in range(2):
                    scatter(out, border_idx[:, k:k + 1], res[0][:, k, :], border_scattered)
                for c in range(2):
                    pool.wait_ge(scattered[c], 16 * CT * TURNS)
                pool.wait_ge(border_scattered, 32)

            @block.sync
            def _(sp):
                def load_gidx(i, c):
                    sp.dma_start(gidx[c][:, :, :], gather_idx[:, cols(i, c), :]).then_inc(gidx_ready[c], 16)

                def load_sidx(i, c):
                    sp.dma_start(sidx[c][:, :], scatter_idx[:, cols(i, c)]).then_inc(sidx_ready[c], 16)

                def load_attr(i, c):
                    sp.dma_start(grow[c][0:FULL, :, D:KW], ea_p[:, cols(i, c), :]).then_inc(attr_ready[c], 16)
                    lo = i * PER + CT * c
                    start = lo * 1 if isinstance(i, int) else lo
                    sp.dma_start(grow[c][FULL:P, :, D:KW],
                                 edge_attr[bass.ds(start + FULL * T, CT), :].rearrange("(p t) w -> p t w", p=1)).then_inc(attr_ready[c], 16)

                def load_rows(i, c):
                    sp.dma_start(r3(hrow[c][:, :], D), h1_edges[:, cols(i, c), :]).then_inc(rows_ready[c], 16)
                    sp.dma_start(xrow[c][:, :, :], x1_edges[:, cols(i, c), :]).then_inc(rows_ready[c], 16)

                REAL = REST // PER
                assert REST % PER == 0

                def load_attr_full(i, c):
                    sp.dma_start(grow[c][0:FULL, :, D:KW], ea_p[:, cols(i, c), :]).then_inc(attr_ready[c], 16)

                def turn(i, attr, more=True):
                    for c in range(2):
                        sp.wait_ge(gathered[c], 16 * CT * (i + 1))
                        if more:
                            load_gidx(i + 1, c)
                        sp.wait_ge(tr_ready, kth(i, c))
                        if more:
                            attr(i + 1, c)
                        sp.wait_ge(res_ready, kth(i, c))
                        if more:
                            load_rows(i + 1, c)
                        sp.wait_ge(scattered[c], 16 * CT * i)
                        load_sidx(i, c)

                for c in range(2):
                    load_gidx(0, c)
                    load_attr(0, c)
                    load_rows(0, c)
                with sp.Fori(0, REAL - 1) as i:
                    turn(i, load_attr)
                with sp.Fori(REAL - 1, TURNS - 1) as i:
                    turn(i, load_attr_full)
                turn(TURNS - 1, None, False)

            @block.tensor
            def _(pe):
                t = nc.tensor

                def products_h(lhs, ps, pairs):
                    for j in range(pairs):
                        ins = t.matmul(ps[:, 1, 2 * j:2 * j + 2, :], lhs[:, j * P:(j + 1) * P], w1_blk[:, :], start=True, stop=True)
                    return ins

                def turn(i, attr_incs):
                    for c in range(2):
                        pe.wait_ge(gathered[c], 16 * CT * (i + 1))
                        pe.wait_ge(attr_ready[c], attr_incs)
                        pe.wait_ge(rows_ready[c], 32 * (i + 1))
                        pe.wait_ge(copied, 4 * i + 2 * c)
                        for j in range(CT):
                            t.transpose(tr_g[c][:, j * P:(j + 1) * P], grow[c][:, j, :], ident[:, :])
                        for j in range(CT // 2):
                            ins = t.transpose(tr_h[c][:, j * P:(j + 1) * P], hrow[c][:, j * P:(j + 1) * P], ident[:, :])
                        ins.then_inc(tr_ready, 1)
                        pe.wait_ge(copied, 4 * i + 2 * c + 2)
                        pe.wait_ge(sum_ready, 2 * i + c)
                        for j in range(CT):
                            t.matmul(mm[c][:, 0, j, :], growT[c][:, j * P:(j + 1) * P], w1_all[:, :], start=True, stop=True)
                        products_h(hrowT[c], mm[c], CT // 2).then_inc(mm_ready, 1)

                REAL = REST // PER
                with pe.Fori(0, REAL) as i:
                    turn(i, 32 * (i + 1))
                with pe.Fori(REAL, TURNS) as i:
                    turn(i, 16 * (i + 1) + 16 * REAL)
                pe.wait_ge(sum_ready, 2 * TURNS)
                t.transpose(tr_h[0][:, 0:P], border_h1[:, :, :].rearrange("p k f -> p (k f)"), ident[:, :]).then_inc(tr_ready, 1)
                pe.wait_ge(copied, 4 * TURNS + 1)
                products_h(hrowT[0], mm[0], 1)
                for k, (from_first, from_last) in enumerate(((same_aa, same_ba), (same_ab, same_bb))):
                    t.matmul(ext_ps[:, k, :], from_first[:, :], first_sum[:, 1, :], start=True, stop=False)
                    ins = t.matmul(ext_ps[:, k, :], from_last[:, :], run[1][:, CT - 1, :], start=False, stop=True)
                ins.then_inc(border_sum, 1)

            @block.scalar
            def _(act):
                a = nc.scalar
                with act.Fori(0, TURNS) as i:
                    for c in range(2):
                        act.wait_ge(tr_ready, kth(i, c))
                        act.wait_ge(mm_ready, 2 * i + c)
                        a.activation(growT[c][:, :], tr_g[c][:, :], ACT.Copy).then_inc(copied, 1)
                        a.activation(hrowT[c][:, :], tr_h[c][:, :], ACT.Copy).then_inc(copied, 1)
                act.wait_ge(tr_ready, 2 * TURNS + 1)
                act.wait_ge(mm_ready, 2 * TURNS)
                a.activation(hrowT[0][:, 0:P], tr_h[0][:, 0:P], ACT.Copy).then_inc(copied, 1)

            @block.vector
            def _(dve):
                v = nc.vector
                do = Chain(dve, dve_step)

                def close(pre_ap, sum_ap, h_ap, x_ap, res_ap, k):
                    dve.wait_ge(res_ready_now[0], res_ready_now[1])
                    v.tensor_tensor(pre_ap, sum_ap, h_ap, ALU.add).then_inc(sum_ready, 1)
                    dve.wait_ge(sum_ready, res_ready_now[1] + 1)
                    do.step(v.tensor_tensor(pre_ap, pre_ap, bias1_b[:, :].unsqueeze(1).to_broadcast([P, k, D]), ALU.add))
                    v.scalar_tensor_tensor(res_ap, pre_ap, 0.0, x_ap, ALU.max, ALU.add).then_inc(res_ready, 1)

                res_ready_now = [res_ready, 0]
                do.step(v.memset(run[1][:, :, :], 0.0))
                do.enter()
                with dve.Fori(0, TURNS) as i:
                    do.turn(i, 2 * (2 * CT + 2))
                    for c in range(2):
                        do.step(v.tensor_copy(mask_c[c][:, :, :], masks[:, cols(i, c), :]))
                        dve.wait_ge(mm_ready, kth(i, c))
                        for j in range(CT):
                            before = run[c][:, j - 1, :] if j else run[1 - c][:, CT - 1, :]
                            if j:
                                do.wait(do.n - 1)
                            do.mark(v.scalar_tensor_tensor(run[c][:, j, :], before, mask_c[c][:, j, 0:1], mm[c][:, 0, j, :], ALU.mult, ALU.add))
                            if j:
                                do.wait(do.n - 1)
                            do.mark(v.scalar_tensor_tensor(first_sum[:, 1, :], mm[c][:, 0, j, :], mask_c[c][:, j, 1:2], first_sum[:, 1, :], ALU.mult, ALU.add))
                        do.wait(do.n - 1)
                        dve.wait_ge(rows_ready[c], 32 * (i + 1))
                        dve.wait_ge(scattered[c], 16 * CT * i)
                        res_ready_now[1] = 2 * i + c
                        close(pre[c][:, :, :], run[c][:, :, :], mm[c][:, 1, :, :], xrow[c][:, :, :], res[c][:, :, :], CT)
                do.leave(TURNS)
                dve.wait_ge(border_sum, 1)
                do.step(v.tensor_tensor(border[:, 0, :], first_sum[:, 1, :], ext_ps[:, 0, :], ALU.add))
                do.step(v.tensor_tensor(border[:, 1, :], run[1][:, CT - 1, :], ext_ps[:, 1, :], ALU.add))
                dve.wait_ge(scattered[0], 16 * CT * TURNS)
                res_ready_now[1] = 2 * TURNS
                close(pre[0][:, 0:2, :], border[:, :, :], mm[0][:, 1, 0:2, :], border_x1[:, :, :], res[0][:, 0:2, :], 2)





def kernel(x, src, dst, edge_attr_16, L0_gnn_W_l, L0_gnn_W_r, L0_gnn_att, L0_gnn_bias, L1_gnn_W, L1_gnn_b):
    import numpy as np
    import concourse.bacc as bacc
    from concourse.bass_utils import run_bass_kernel_spmd

    nc = bacc.Bacc("TRN2", target_bir_lowering=False, num_devices=1)
    named = dict(x=x, src=src, dst=dst, edge_attr=edge_attr_16, w_l=L0_gnn_W_l, w_r=L0_gnn_W_r, att=L0_gnn_att,
                 bias0=L0_gnn_bias, w1=L1_gnn_W, bias1=L1_gnn_b)
    arrays, args = {}, {}
    for name, a in named.items():
        a = np.ascontiguousarray(a)
        arrays[f"in_{name}"] = a
        args[name] = nc.dram_tensor(f"in_{name}", a.shape, mybir.dt.from_np(a.dtype), kind="ExternalInput").ap()
    out = nc.dram_tensor("out_x", tuple(x.shape), F32, kind="ExternalOutput").ap()
    gnn_program(nc, out=out, **args)
    result = run_bass_kernel_spmd(nc, [arrays], core_ids=[0])
    return result.results[0]["out_x"]
```

```python
from contextlib import ExitStack

import concourse.bass as bass
from concourse import mybir

F32 = mybir.dt.float32
BF16 = mybir.dt.bfloat16
I32 = mybir.dt.int32
U32 = mybir.dt.uint32
ALU = mybir.AluOpType
ACT = mybir.ActivationFunctionType
AX = mybir.AxisListType

P = 128
EPS = 1e-5
BIG = 1e30
SELU_L = 1.0507009873554805
SELU_A = 1.6732632423543772
SELU_LA = SELU_L * SELU_A
LN_EXP_SET = 6


class Chain:

    def __init__(self, eng, sem):
        self.eng, self.sem, self.start, self.n = eng, sem, 0, 0

    def turn(self, i, per_loop):
        self.start, self.n, self.per_loop = self.base + i * per_loop, 0, per_loop

    def enter(self):
        self.base = self.start + self.n

    def leave(self, turns):
        assert self.n == self.per_loop, (self.n, self.per_loop)
        self.start, self.n = self.base + turns * self.per_loop, 0

    def mark(self, ins):
        ins.then_inc(self.sem, 1)
        self.n += 1
        return self.n

    def wait(self, n):
        self.eng.wait_ge(self.sem, self.start + n)

    def step(self, ins):
        self.wait(self.mark(ins))


def gnn_program(nc, x, src, dst, edge_attr, w_l, w_r, att, bias0, w1, bias1, out):
    N, D = x.shape
    E = src.shape[0]
    H = att.shape[0]
    EW = edge_attr.shape[1]
    KW = D + EW
    CT = 4
    PER = 2 * CT
    TURNS = -(-E // (P * PER))
    T = TURNS * PER
    FULL = E // T
    REST = E - FULL * T
    FULL_PARTS = (slice(0, FULL // 16 * 16), slice(FULL // 16 * 16, FULL))
    REAL = REST // PER
    HD = H * D
    NZ = HD // P
    ROWS = 8
    BLOCK = 2 * ROWS * P
    LAST = N - BLOCK
    assert (TURNS - 1) * BLOCK < N <= TURNS * BLOCK and NZ == 3 and FULL == P - 1 and REST % PER == 0

    x1_table = nc.dram_tensor("x1_table", (N, D), F32).ap()
    stash = nc.dram_tensor("stash", (P, T, 3 * D), F32).ap()
    x1_edges = nc.dram_tensor("x1_edges", (P, T, D), F32).ap()

    keep = ExitStack()
    last_row = [N - 1]

    def sb(name, shape, dt=F32, ctx=keep):
        return ctx.enter_context(nc.sbuf_tensor(name, shape, dt))

    def sem(name):
        return keep.enter_context(nc.semaphore(name))

    def exists(i, c):
        return not isinstance(i, int) or 0 <= 2 * i + c < 2 * TURNS

    def ago(i, c, k):
        return i + (c - k) // 2, (c - k) % 2

    def wait_from(eng, semaphore, value):
        if not isinstance(value, int) or value > 0:
            eng.wait_ge(semaphore, value)

    def r3(ap, f):
        return ap.rearrange("p (r f) -> p r f", f=f)

    with keep:
        gather_idx = sb("gather_idx", [P, T + PER, 2], U32)
        scatter_idx = sb("scatter_idx", [P, T], U32)
        border_idx = sb("border_idx", [P, 2], U32)
        masks = sb("masks", [P, T, 2])
        same_next = sb("same_next", [P, T])
        is_last = sb("is_last", [P, T])
        is_first = sb("is_first", [P, T])
        ident = sb("ident", [P, P])
        ones = sb("ones", [P, P])
        eps = sb("eps", [P, 1])
        w_edge = sb("w_edge", [P, HD])
        w_self = sb("w_self", [P, HD])
        att_blk = sb("att_blk", [P, NZ, 32])
        lin_e = sb("lin_e", [P, 32])
        lin_s = sb("lin_s", [P, 32])
        select = sb("select", [P, 2 * H])
        mean_blk = sb("mean_blk", [P, P])
        w_msg = sb("w_msg", [P, NZ, D])
        base_w = sb("base_w", [P, D])
        w1_blk = sb("w1_blk", [P, P])
        w1_all = sb("w1_all", [KW, D])
        ones16 = sb("ones16", [3 * 32, P], BF16)
        bias_parts = sb("bias_parts", [3 * 32, 2, ROWS * D], BF16)
        selu_la = sb("selu_la", [P, 1])
        bias0_b = sb("bias0_b", [P, D])
        bias1_b = sb("bias1_b", [P, D])
        same_aa = sb("same_aa", [P, P])
        same_ba = sb("same_ba", [P, P])
        same_ab = sb("same_ab", [P, P])
        same_bb = sb("same_bb", [P, P])
        pen_a = sb("pen_a", [P, 2, P])
        pen_b = sb("pen_b", [P, 2, P])
        scores = sb("scores", [P, 2 * H, T])
        alpha = sb("alpha", [P, T, H])
        first_sum = sb("first_sum", [P, 2, D])
        border_x1 = sb("border_x1", [P, 2, D])
        border_h1 = sb("border_h1", [P, 2, D])
        admitted = sem("admitted")

        with ExitStack() as own:
            def tmp(name, shape, dt=F32):
                return sb(name, shape, dt, own)

            src_i = tmp("src_i", [P, T], I32)
            dst_i = tmp("dst_i", [P, T], I32)
            dstf = tmp("dstf", [P, T])
            work = tmp("work", [P, T])
            endm = tmp("endm", [P, T])
            notab = tmp("notab", [P, 1])
            cnt = tmp("cnt", [P, 2])
            bidf = tmp("bidf", [P, 2])
            before = tmp("before", [P, P])
            dg = tmp("dg", [P, 2, P])
            eq = tmp("eq", [P, P])
            att_b = tmp("att_b", [P, HD])
            prod = tmp("prod", [P, HD])
            wl_lo = tmp("wl_lo", [P, HD])
            wl_sum = tmp("wl_sum", [P, D])
            part = tmp("part", [P, 3, D], BF16)
            rest = tmp("rest", [P, 2, D])
            rows_ps = own.enter_context(nc.psum_tensor("rows_ps", [P, 2, P], F32))
            zeroed, loaded_e, loaded_w, pooled, diag, rowed, step = (
                sem(n) for n in ("zeroed", "loaded_edges", "loaded_weights", "pool_consts", "diag_ready",
                                 "rows_ready", "setup_step"))
            n_w = [0]
            block = own.enter_context(nc.Block())

            @block.gpsimd
            def _(pool):
                nc.gpsimd.memset(src_i[:, :], 0).then_inc(zeroed, 1)
                nc.gpsimd.memset(dst_i[:, :], N).then_inc(zeroed, 1)
                for t in (att_blk[:, :, :], base_w[:, :], w1_blk[:, :]):
                    nc.gpsimd.memset(t, 0.0).then_inc(zeroed, 1)
                nc.gpsimd.memset(ident[:, :], 0.0).then_inc(pooled, 1)
                nc.gpsimd.memset(before[:, :], 1.0).then_inc(pooled, 1)
                pool.wait_ge(pooled, 2)
                nc.gpsimd.affine_select(out=ident[:, :], in_=ident[:, :], compare_op=ALU.not_equal, fill=1.0,
                                        base=0, pattern=[[-1, P]], channel_multiplier=1).then_inc(pooled, 1)
                nc.gpsimd.affine_select(out=before[:, :], in_=before[:, :], compare_op=ALU.is_gt, fill=0.0,
                                        base=0, pattern=[[-1, P]], channel_multiplier=1).then_inc(pooled, 1)

            @block.sync
            def _(sp):
                sp.wait_ge(zeroed, 2)
                for tile, dram in ((src_i, src), (dst_i, dst)):
                    for rows in FULL_PARTS:
                        sp.dma_start(tile[rows, :], dram[0:FULL * T].rearrange("(p t) -> p t", t=T)[rows, :]).then_inc(loaded_e, 16)
                    sp.dma_start(tile[FULL:P, 0:REST], dram[FULL * T:E].rearrange("(p t) -> p t", p=1)).then_inc(loaded_e, 16)
                sp.wait_ge(zeroed, 5)

                def load(to, what):
                    sp.dma_start(to, what).then_inc(loaded_w, 16)
                    n_w[0] += 16

                load(w_edge[0:D, :], w_l)
                load(w_edge[D:P, :], w_r)
                load(wl_lo[0:D, :], w_l)
                load(wl_lo[D:P, :], w_l)
                for h in range(H):
                    rows = slice((h % 2) * D, (h % 2) * D + D)
                    load(att_blk[rows, h // 2, h:h + 1], att[h, :].rearrange("(f o) -> f o", o=1))
                load(att_b[:, :], att.rearrange("h f -> (h f)").partition_broadcast(P))
                load(bias0_b[:, :], bias0.partition_broadcast(P))
                load(bias1_b[:, :], bias1.partition_broadcast(P))
                load(base_w[D:D + 1, :], bias0.rearrange("(o f) -> o f", o=1))
                load(w1_all[:, :], w1)
                load(w1_blk[0:D, 0:D], w1[0:D, :])
                load(w1_blk[D:P, D:P], w1[0:D, :])

            @block.tensor
            def _(pe):
                pe.wait_ge(diag, 1)
                nc.tensor.matmul(rows_ps[:, :, :], ones[:, :], dg[:, :, :], start=True, stop=True).then_inc(rowed, 1)

            @block.vector
            def _(dve):
                v = nc.vector
                do = Chain(dve, step)
                do.step(v.memset(ones[:, :], 1.0))
                do.step(v.memset(eps[:, :], EPS))
                do.step(v.memset(selu_la[:, :], SELU_LA))
                do.step(v.memset(ones16[:, :], 1.0))
                do.step(v.memset(bias_parts[:, :, :], 0.0))
                for t in (w_self[:, :], lin_e[:, :], lin_s[:, :], select[:, :], mean_blk[:, :]):
                    do.step(v.memset(t, 0.0))
                do.step(v.memset(first_sum[:, :, :], 0.0))
                do.step(v.memset(gather_idx[:, :, :], 0))
                dve.wait_ge(loaded_e, 96)
                do.step(v.tensor_copy(dstf[:, :], dst_i[:, :]))
                do.step(v.tensor_copy(gather_idx[:, 0:T, 0], src_i[:, :]))
                do.step(v.tensor_scalar(gather_idx[:, 0:T, 1], dstf[:, :], float(N - 1), None, ALU.min))
                a, b = dstf[:, 0:1], dstf[:, T - 1:T]
                dve.wait_ge(pooled, 4)
                do.step(v.tensor_scalar(dg[:, 0, :], ident[:, :], a, None, ALU.mult))
                v.tensor_scalar(dg[:, 1, :], ident[:, :], b, None, ALU.mult).then_inc(diag, 1)
                do.step(v.memset(masks[:, 0:1, 0:1], 0.0))
                do.step(v.memset(same_next[:, T - 1:T], 0.0))
                do.step(v.tensor_tensor(masks[:, 1:T, 0], dstf[:, 1:T], dstf[:, 0:T - 1], ALU.is_equal))
                do.step(v.tensor_copy(same_next[:, 0:T - 1], masks[:, 1:T, 0]))
                do.step(v.tensor_scalar(is_first[:, :], dstf[:, :], a, None, ALU.is_equal))
                do.step(v.tensor_copy(masks[:, :, 1], is_first[:, :]))
                do.step(v.tensor_tensor(notab[:, :], a, b, ALU.not_equal))
                do.step(v.tensor_scalar(is_last[:, :], dstf[:, :], b, notab[:, :], ALU.is_equal, ALU.mult))
                do.step(v.tensor_tensor(work[:, :], is_first[:, :], is_last[:, :], ALU.add))
                do.step(v.tensor_tensor(work[:, :], work[:, :], same_next[:, :], ALU.add))
                do.step(v.tensor_scalar(endm[:, :], work[:, :], 0.0, None, ALU.is_equal))
                do.step(v.tensor_scalar(work[:, :], dstf[:, :], float(N), None, ALU.subtract))
                do.step(v.tensor_tensor(work[:, :], work[:, :], endm[:, :], ALU.mult))
                do.step(v.tensor_scalar(scatter_idx[:, :], work[:, :], float(N), None, ALU.add))
                dve.wait_ge(rowed, 1)
                row_a, row_b = rows_ps[:, 0, :], rows_ps[:, 1, :]
                for pen, k, row, own_node in ((pen_a, 0, row_a, a), (pen_a, 1, row_b, a),
                                              (pen_b, 0, row_a, b), (pen_b, 1, row_b, b)):
                    do.step(v.tensor_scalar(eq[:, :], row, own_node, None, ALU.is_equal))
                    do.step(v.tensor_scalar(pen[:, k, :], eq[:, :], 1.0, BIG, ALU.subtract, ALU.mult))
                    if pen is pen_a and k == 0:
                        do.step(v.tensor_tensor(same_aa[:, :], eq[:, :], ident[:, :], ALU.subtract))
                        do.step(v.tensor_tensor(eq[:, :], eq[:, :], before[:, :], ALU.mult))
                        do.step(v.tensor_reduce(cnt[:, 0:1], eq[:, :], AX.X, ALU.add))
                    if pen is pen_b and k == 0:
                        do.step(v.tensor_reduce(cnt[:, 1:2], eq[:, :], AX.X, ALU.add))
                do.step(v.tensor_scalar(same_ba[:, :], row_a, b, notab[:, :], ALU.is_equal, ALU.mult))
                do.step(v.tensor_scalar(same_ab[:, :], row_b, a, None, ALU.is_equal))
                do.step(v.tensor_scalar(eq[:, :], row_b, b, None, ALU.is_equal))
                do.step(v.tensor_tensor(eq[:, :], eq[:, :], ident[:, :], ALU.subtract))
                do.step(v.tensor_scalar(same_bb[:, :], eq[:, :], notab[:, :], None, ALU.mult))
                for k, node in ((0, a), (1, b)):
                    do.step(v.tensor_scalar(cnt[:, k:k + 1], cnt[:, k:k + 1], 0.0, None, ALU.is_equal))
                    do.step(v.tensor_scalar(bidf[:, k:k + 1], node, float(N), None, ALU.subtract))
                do.step(v.tensor_tensor(bidf[:, :], bidf[:, :], cnt[:, :], ALU.mult))
                do.step(v.tensor_scalar(border_idx[:, :], bidf[:, :], float(N), None, ALU.add))
                dve.wait_ge(loaded_w, n_w[0])
                do.step(v.tensor_tensor(w_self[D:P, :], wl_lo[D:P, :], w_edge[D:P, :], ALU.add))
                for w, lin in ((w_edge, lin_e), (w_self, lin_s)):
                    do.step(v.tensor_tensor(prod[:, :], w[:, :], att_b[:, :], ALU.mult))
                    do.step(v.tensor_reduce(lin[:, 0:H], r3(prod[:, :], D), AX.X, ALU.add))
                    do.step(v.tensor_scalar(lin[:, 0:H], lin[:, 0:H], 0.2, None, ALU.mult))
                do.step(v.tensor_scalar(prod[:, :], wl_lo[:, :], 1.0 / H, None, ALU.mult))
                do.step(v.tensor_reduce(wl_sum[:, :], prod[:, :].rearrange("p (h f) -> p f h", f=D), AX.X, ALU.add))
                do.step(v.tensor_copy(mean_blk[0:D, 0:D], wl_sum[0:D, :]))
                do.step(v.tensor_copy(mean_blk[D:P, D:P], wl_sum[D:P, :]))
                do.step(v.tensor_copy(base_w[0:D, :], wl_sum[0:D, :]))
                for h in range(H):
                    rows = slice((h % 2) * D, (h % 2) * D + D)
                    do.step(v.tensor_copy(w_msg[rows, h // 2, :], prod[rows, h * D:(h + 1) * D]))
                for layer, bias in enumerate((bias0_b, bias1_b)):
                    left = bias[:, :]
                    for k in range(3):
                        do.step(v.tensor_copy(part[:, k, :], left))
                        row = slice(32 * k, 32 * k + 1)
                        do.step(v.tensor_copy(bias_parts[row, layer, :].rearrange("p (r f) -> p r f", f=D),
                                              part[row, k, :].unsqueeze(1).to_broadcast([1, ROWS, D])))
                        if k < 2:
                            do.step(v.tensor_tensor(rest[:, k, :], left, part[:, k, :], ALU.subtract))
                            left = rest[:, k, :]
                for g in range(4):
                    do.step(v.tensor_copy(select[32 * g:32 * g + H, H * (g // 2):H * (g // 2) + H],
                                          ident[32 * g:32 * g + H, 32 * g:32 * g + H]))

        with ExitStack() as own:
            def tmp(name, shape, dt=F32):
                return sb(name, shape, dt, own)

            def pair(name, shape, dt=F32):
                return [tmp(f"{name}{c}", shape, dt) for c in range(2)]

            R2 = 2 * ROWS
            idx_c = pair("idx_c", [P, CT, 2], U32)
            xe = pair("xe", [P, CT, 2, D])
            xd = pair("xd", [P, ROWS, D])
            he = pair("he", [P, CT * 2 * D])
            hd = pair("hd", [P, ROWS * D])
            h1 = pair("h1", [P, ROWS * D])
            stats = pair("stats", [P, R2, 6])
            sumq = pair("sumq", [P, R2, 2])
            diff = pair("diff", [P, R2])
            var = pair("var", [P, R2])
            lnv = pair("lnv", [P, R2])
            rstd = pair("rstd", [P, R2])
            stats1 = pair("stats1", [P, ROWS, 6])
            sumq1 = pair("sumq1", [P, ROWS, 2])
            diff1 = pair("diff1", [P, ROWS])
            var1 = pair("var1", [P, ROWS])
            lnv1 = pair("lnv1", [P, ROWS])
            rstd1 = pair("rstd1", [P, ROWS])
            xc = [tmp(f"xc{k}", [P, ROWS, D]) for k in range(4)]
            hdiff = pair("hdiff", [P, CT, D])
            heT = pair("heT", [P, CT * P])
            hdT = pair("hdT", [P, ROWS * D])
            relu_z = pair("relu_z", [P, 2 * NZ, CT * P])
            scoreT = pair("scoreT", [P, CT * P])
            gexp = pair("gexp", [P, ROWS * D])
            grelu = pair("grelu", [P, ROWS * D])
            x1 = pair("x1", [P, ROWS, D])
            res = pair("res", [P, ROWS, D])

            def ps(name, shape):
                return own.enter_context(nc.psum_tensor(name, shape, F32))

            tr_e = ps("tr_e", [P, CT * P])
            tr_d = ps("tr_d", [P, CT * P])
            z_ps = [ps(f"z_ps{k}", [P, CT * P]) for k in range(3)]
            sc_ps = ps("sc_ps", [P, CT * P])
            sel_ps = ps("sel_ps", [P, CT, 2 * H])
            mm_d = ps("mm_d", [P, ROWS * D])

            idx_ready, gathered, x_ready, x_stashed, h_stashed, diff_stashed, x1_stored, out_stored = (
                [sem(f"{n}{c}") for c in range(2)] for n in
                ("idx_ready", "gathered", "x_ready", "x_stashed", "h_stashed", "diff_stashed", "x1_stored", "out_stored"))
            diff_ready = sem("diff_ready")
            hd_tr, hd_T, mm_ready = (
                [sem(f"{n}{layer}") for layer in range(2)] for n in ("hd_transposed", "hdT_ready", "mm_ready"))
            (mm_read, var_ready, rstd_ready, h_ready, he_tr, he_T, z_ready, relu_ready, round_ready, scoreT_ready,
             sel_ready, scores_done, gat_act, x1_ready, var1_ready,
             rstd1_ready, h1_ready, res_ready, dve_step, act_step) = (sem(n) for n in (
                 "mm_read", "var_ready", "rstd_ready", "h_ready", "he_transposed", "heT_ready", "z_ready", "relu_ready",
                 "round_ready", "scoreT_ready", "sel_ready", "scores_done",
                 "gat_act", "x1_ready", "var1_ready", "rstd1_ready", "h1_ready",
                 "res_ready", "dve_step", "act_step"))
            block = own.enter_context(nc.Block())
            LASTI = TURNS - 1

            def kth(i, c):
                return 2 * i + (c + 1)

            def nodes(i):
                return LAST if isinstance(i, int) and i == LASTI else i * BLOCK

            def dense_rows(dram, i, c):
                return dram[bass.ds(nodes(i), BLOCK), :].rearrange("(p u) f -> p u f", u=2 * ROWS)[:, c * ROWS:(c + 1) * ROWS, :]

            @block.gpsimd
            def _(pool):
                last_row[0] = pool.to_reg(N - 1)

                def gathers(i, c):
                    pool.wait_ge(idx_ready[c], 16 * (i + 1))
                    pool.sem_inc(admitted, 1)
                    for j in range(CT):
                        for s in range(2):
                            nc.gpsimd.indirect_dma_start(
                                xe[c][:, j, s, :], None, x,
                                bass.IndirectOffsetOnAxis(ap=idx_c[c][:, j, s:s + 1], axis=0),
                                bounds_check=last_row[0], oob_is_err=False).then_inc(gathered[c], 16)

                for c in range(2):
                    gathers(0, c)
                with pool.Fori(1, TURNS) as i:
                    for c in range(2):
                        pool.wait_ge(h_ready, 2 * i + (c - 1))
                        pool.wait_ge(x_stashed[c], 16 * i)
                        gathers(i, c)

            @block.sync
            def _(sp):
                def load_idx(i, c):
                    sp.dma_start(idx_c[c][:, :, :], gather_idx[:, bass.ds(i * PER + CT * c, CT), :]).then_inc(idx_ready[c], 16)

                def load_x(i, c):
                    sp.dma_start(xd[c][:, :, :], dense_rows(x, i, c)).then_inc(x_ready[c], 16)

                def stashes(i, c):
                    sp.wait_ge(diff_ready, kth(i, c))
                    sp.dma_start(stash[:, bass.ds(i * PER + CT * c, CT), 2 * D:3 * D], xe[c][:, :, 1, :]).then_inc(x_stashed[c], 16)
                    sp.dma_start(stash[:, bass.ds(i * PER + CT * c, CT), D:2 * D], r3(he[c][:, :], 2 * D)[:, :, D:2 * D]).then_inc(h_stashed[c], 16)
                    sp.dma_start(stash[:, bass.ds(i * PER + CT * c, CT), 0:D], hdiff[c][:, :, :]).then_inc(diff_stashed[c], 16)

                def store(i, c, ready, dram, rows, stored):
                    sp.wait_ge(ready, kth(i, c))
                    if isinstance(i, int) and i == LASTI:
                        for k in range(2):
                            sp.wait_ge(stored[k], 16 * LASTI)
                    sp.dma_start(dense_rows(dram, i, c), rows[c][:, :, :]).then_inc(stored[c], 16)

                def turn(i):
                    for c in range(2):
                        j, d = ago(i, c, -3)
                        if exists(j, d):
                            wait_from(sp, gathered[d], 32 * CT * j)
                            load_idx(j, d)
                        if exists(*ago(i, c, -1)):
                            stashes(*ago(i, c, -1))
                        if exists(*ago(i, c, 2)):
                            store(i - 1, c, res_ready, out, res, out_stored)
                        if exists(*ago(i, c, -2)):
                            sp.wait_ge(x1_ready, kth(i, c))
                            load_x(i + 1, c)
                        if exists(i, c):
                            store(i, c, x1_ready, x1_table, x1, x1_stored)

                for c in range(2):
                    load_idx(0, c)
                    load_x(0, c)
                wait_from(sp, gathered[0], 32 * CT)
                load_idx(1, 0)
                stashes(0, 0)
                turn(0)
                with sp.Fori(1, LASTI - 1) as i:
                    turn(i)
                turn(LASTI - 1)
                turn(LASTI)
                turn(TURNS)
                for c in range(2):
                    for s in (x_stashed, h_stashed, diff_stashed, x1_stored, out_stored):
                        sp.wait_ge(s[c], 16 * TURNS)

            @block.tensor
            def _(pe):
                t = nc.tensor

                def transpose_e(i, c):
                    pe.wait_ge(h_ready, kth(i, c))
                    wait_from(pe, he_T, 2 * i + c)
                    for j in range(CT):
                        ins = t.transpose(tr_e[:, j * P:(j + 1) * P], he[c][:, j * P:(j + 1) * P], ident[:, :])
                    ins.then_inc(he_tr, 1)

                def before_this(i, c, layer, done):
                    if layer == 0:
                        wait_from(pe, done[1], 2 * i + (c - 2))
                    elif exists(*ago(i, c, -2)):
                        pe.wait_ge(done[0], 2 * i + (c + 3))
                    else:
                        pe.wait_ge(done[0], 2 * TURNS)
                        pe.wait_ge(done[1], 2 * i + c)

                def transpose_d(i, c, layer):
                    if layer == 0:
                        pe.wait_ge(h_ready, kth(i, c))
                    else:
                        pe.wait_ge(h1_ready, kth(i, c))
                    before_this(i, c, layer, hd_T)
                    h = (hd, h1)[layer][c]
                    for j in range(ROWS // 2):
                        ins = t.transpose(tr_d[:, j * P:(j + 1) * P], h[:, j * P:(j + 1) * P], ident[:, :])
                    ins.then_inc(hd_tr[layer], 1)

                def dense_mm(i, c, layer):
                    pe.wait_ge(hd_T[layer], kth(i, c))
                    before_this(i, c, layer, (mm_read, res_ready))
                    t.matmul(mm_d[:, :], ones16[:, :], bias_parts[:, layer, :], start=True, stop=False)
                    for j in range(ROWS // 2):
                        ins = t.matmul(mm_d[:, j * P:(j + 1) * P], hdT[c][:, j * P:(j + 1) * P],
                                       (mean_blk, w1_blk)[layer][:, :], start=False, stop=(j == ROWS // 2 - 1))
                    ins.then_inc(mm_ready[layer], 1)

                ORDER = [(0, 0), (0, 2), (1, 0), (1, 2), (0, 1), (1, 1)]

                def project(i, c, part):
                    if part == 0:
                        pe.wait_ge(he_T, kth(i, c))
                    for n in range(3 * part, 3 * part + 3):
                        kind, z = ORDER[n]
                        pe.wait_ge(relu_ready, 12 * i + 6 * c + n + 1)
                        t.matmul(z_ps[n % 3][:, :], (w_edge, w_self)[kind][:, z * P:(z + 1) * P], heT[c][:, :],
                                 start=True, stop=True).then_inc(z_ready, 1)

                def rounds(i, c):
                    pe.wait_ge(relu_ready, 12 * i + 6 * c + 6 + 3)
                    for g, (n, z) in enumerate(((0, 0), (1, 2), (2, 0), (3, 2))):
                        t.matmul(sc_ps[32 * g:32 * g + 32, :], att_blk[:, z, :], relu_z[c][:, n, :], start=True, stop=False)
                    t.matmul(sc_ps[0:32, :], att_blk[:, 1, :], relu_z[c][:, 4, :], start=False, stop=True)
                    t.matmul(sc_ps[32:64, :], lin_e[:, :], heT[c][:, :], start=False, stop=True)
                    t.matmul(sc_ps[64:96, :], att_blk[:, 1, :], relu_z[c][:, 5, :], start=False, stop=True)
                    t.matmul(sc_ps[96:128, :], lin_s[:, :], heT[c][:, :], start=False, stop=True).then_inc(round_ready, 1)

                def select_scores(i, c):
                    pe.wait_ge(scoreT_ready, kth(i, c))
                    wait_from(pe, scores_done, 2 * i + c)
                    for j in range(CT):
                        ins = t.matmul(sel_ps[:, j, :], scoreT[c][:, j * P:(j + 1) * P], select[:, :], start=True, stop=True)
                    ins.then_inc(sel_ready, 1)

                def turn(i):
                    for c in range(2):
                        now, previous, older = (exists(*ago(i, c, k)) for k in range(3))
                        if now:
                            transpose_e(i, c)
                            transpose_d(i, c, 0)
                        if previous:
                            rounds(*ago(i, c, 1))
                        if now:
                            project(i, c, 0)
                            dense_mm(i, c, 0)
                        if older:
                            transpose_d(i - 1, c, 1)
                        if now:
                            project(i, c, 1)
                        if previous:
                            select_scores(*ago(i, c, 1))
                        if older:
                            dense_mm(i - 1, c, 1)

                turn(0)
                with pe.Fori(1, TURNS) as i:
                    turn(i)
                turn(TURNS)

            @block.scalar
            def _(act):
                a = nc.scalar
                own_step = Chain(act, act_step)

                def rstds(i, c, layer):
                    v, l, r = ((var, lnv, rstd), (var1, lnv1, rstd1))[layer]
                    act.wait_ge((var_ready, var1_ready)[layer], kth(i, c))
                    n = own_step.mark(a.activation(l[c][:, :], v[c][:, :], ACT.Ln, bias=eps[:, :], scale=1.0 / D))
                    own_step.wait(n)
                    a.activation(r[c][:, :], l[c][:, :], ACT.Exp, scale=-0.5).then_inc((rstd_ready, rstd1_ready)[layer], 1)

                def copy_e(i, c):
                    act.wait_ge(he_tr, kth(i, c))
                    a.activation(heT[c][:, :], tr_e[:, :], ACT.Copy).then_inc(he_T, 1)

                def copy_d(i, c, layer):
                    act.wait_ge(hd_tr[layer], kth(i, c))
                    a.activation(hdT[c][:, :], tr_d[:, :], ACT.Copy).then_inc(hd_T[layer], 1)

                def relus(i, c, which):
                    for n in which:
                        act.wait_ge(z_ready, 12 * i + 6 * c + n + 1)
                        a.activation(relu_z[c][:, n, :], z_ps[n % 3][:, :], ACT.Relu, scale=0.8).then_inc(relu_ready, 1)

                def copy_scores(i, c):
                    act.wait_ge(round_ready, kth(i, c))
                    a.activation(scoreT[c][:, :], sc_ps[:, :], ACT.Copy).then_inc(scoreT_ready, 1)

                def selu_parts(i, c):
                    act.wait_ge(mm_ready[0], kth(i, c))
                    n = own_step.mark(a.activation(gexp[c][:, :], mm_d[:, :], ACT.Exp))
                    a.activation(grelu[c][:, :], mm_d[:, :], ACT.Relu, scale=SELU_L).then_inc(mm_read, 1)
                    own_step.wait(n)
                    a.activation(gexp[c][:, :], gexp[c][:, :], ACT.Relu, scale=-SELU_LA, bias=selu_la[:, :]).then_inc(gat_act, 1)

                def turn(i):
                    for c in range(2):
                        now, previous, following = exists(i, c), exists(*ago(i, c, 1)), exists(*ago(i, c, -1))
                        if now:
                            copy_e(i, c)
                            copy_d(i, c, 0)
                        if previous:
                            copy_scores(*ago(i, c, 1))
                        if now:
                            relus(i, c, (0, 1, 2))
                        if previous:
                            rstds(*ago(i, c, 1), 1)
                        if now:
                            selu_parts(i, c)
                        if exists(*ago(i, c, 2)):
                            copy_d(i - 1, c, 1)
                        if now:
                            relus(i, c, (3,))
                        if following:
                            rstds(*ago(i, c, -1), 0)
                        if now:
                            relus(i, c, (4, 5))

                act.add_instruction(mybir.InstLoadActFuncSet(
                    name=nc.get_next_instruction_name(), act_func_set_id=LN_EXP_SET, ins=[], outs=[]))
                act.sem_inc(relu_ready, 3)
                rstds(0, 0, 0)
                turn(0)
                own_step.enter()
                with act.Fori(1, LASTI) as i:
                    own_step.turn(i - 1, 6)
                    turn(i)
                own_step.leave(LASTI - 1)
                turn(LASTI)
                turn(TURNS)

            @block.vector
            def _(dve):
                v = nc.vector
                do = Chain(dve, dve_step)

                def mid(ap):
                    return ap.unsqueeze(2).to_broadcast([P, ROWS, D])

                def centre(to, sq, rows):
                    return do.mark(v.scalar_tensor_tensor(to, mid(sq), -0.5, rows, ALU.mult, ALU.add))

                def scale(to, cen, r):
                    return v.scalar_tensor_tensor(to, cen, 0.0, mid(r), ALU.max, ALU.mult)

                def halves(st, sq, df):
                    do.wait(do.n)
                    nd = do.mark(v.tensor_tensor(df[:, :], st[:, :, 1], st[:, :, 4], ALU.subtract))
                    do.mark(v.tensor_tensor(sq[:, :, :], st[:, :, 1:3], st[:, :, 4:6], ALU.add))
                    return nd

                def between(nd, df, va):
                    do.wait(nd)
                    return do.mark(v.scalar_tensor_tensor(va[:, :], df[:, :], D / 4.0, df[:, :], ALU.mult, ALU.mult))

                def total(n, sq, va, signal):
                    do.wait(n)
                    v.tensor_tensor(va[:, :], va[:, :], sq[:, :, 1], ALU.add).then_inc(signal, 1)

                def norm_stats(i, c):
                    dve.wait_ge(gathered[c], 32 * CT * (i + 1))
                    for r in range(ROWS):
                        v.bn_stats(stats[c][:, ROWS + r, :], xe[c][:, r // 2, r % 2, :])
                    dve.wait_ge(x_ready[c], 16 * (i + 1))
                    for r in range(ROWS):
                        ins = v.bn_stats(stats[c][:, r, :], xd[c][:, r, :])
                    do.mark(ins)
                    return halves(stats[c], sumq[c], diff[c])

                def norm_between(i, c, nd):
                    n = between(nd, diff[c], var[c])
                    wait_from(dve, h_ready, 2 * i + c)
                    do.wait(n - 1)
                    nx = centre(xc[0][:, :, :], sumq[c][:, 0:ROWS, 0], xd[c][:, :, :])
                    total(n, sumq[c], var[c], var_ready)
                    centre(xc[1][:, :, :], sumq[c][:, ROWS:R2, 0], xe[c][:, :, :, :].rearrange("p j s f -> p (j s) f"))
                    return nx

                def norm_dense(i, c, nx):
                    do.wait(nx)
                    dve.wait_ge(rstd_ready, kth(i, c))
                    scale(r3(hd[c][:, :], D), xc[0][:, :, :], rstd[c][:, 0:ROWS])

                def norm_edges(i, c, nx):
                    do.wait(nx + 1)
                    wait_from(dve, h_stashed[c], 16 * i)
                    scale(r3(he[c][:, :], D), xc[1][:, :, :], rstd[c][:, ROWS:R2]).then_inc(h_ready, 1)

                def subtract(i, c):
                    dve.wait_ge(h_ready, kth(i, c))
                    wait_from(dve, diff_stashed[c], 16 * i)
                    h = r3(he[c][:, :], 2 * D)
                    v.tensor_tensor(hdiff[c][:, :, :], h[:, :, 0:D], h[:, :, D:2 * D], ALU.subtract).then_inc(diff_ready, 1)

                def residual(i, c):
                    dve.wait_ge(mm_read, kth(i, c))
                    return do.mark(v.tensor_tensor(xc[2][:, :, :], xd[c][:, :, :], r3(grelu[c][:, :], D), ALU.add))

                def add_selu(i, c, n):
                    do.wait(n)
                    dve.wait_ge(gat_act, kth(i, c))
                    wait_from(dve, res_ready, 2 * i + (c - 1))
                    wait_from(dve, x1_stored[c], 16 * i)
                    v.tensor_tensor(x1[c][:, :, :], xc[2][:, :, :], r3(gexp[c][:, :], D), ALU.subtract).then_inc(x1_ready, 1)

                def x1_stats(i, c):
                    dve.wait_ge(x1_ready, kth(i, c))
                    for r in range(ROWS):
                        ins = v.bn_stats(stats1[c][:, r, :], x1[c][:, r, :])
                    do.mark(ins)
                    return halves(stats1[c], sumq1[c], diff1[c])

                def norm1_between(i, c, nd):
                    n = between(nd, diff1[c], var1[c])
                    do.wait(nd + 1)
                    wait_from(dve, h1_ready, 2 * i + c)
                    centre(xc[3][:, :, :], sumq1[c][:, :, 0], x1[c][:, :, :])
                    total(n, sumq1[c], var1[c], var1_ready)

                def norm1_apply(i, c):
                    do.wait(do.n)
                    dve.wait_ge(rstd1_ready, kth(i, c))
                    scale(r3(h1[c][:, :], D), xc[3][:, :, :], rstd1[c][:, :]).then_inc(h1_ready, 1)

                def keep_scores(i, c):
                    dve.wait_ge(sel_ready, kth(i, c))
                    v.tensor_copy(scores[:, :, bass.ds(i * PER + CT * c, CT)].rearrange("p g t -> p t g"), sel_ps[:, :, :]).then_inc(scores_done, 1)

                def dense_out(i, c):
                    dve.wait_ge(mm_ready[1], kth(i, c))
                    wait_from(dve, out_stored[c], 16 * i)
                    v.scalar_tensor_tensor(res[c][:, :, :], r3(mm_d[:, :], D), 0.0, x1[c][:, :, :], ALU.max, ALU.add).then_inc(res_ready, 1)

                def turn(i):
                    for c in range(2):
                        now, previous, following = exists(i, c), exists(*ago(i, c, 1)), exists(*ago(i, c, -1))
                        before, after = ago(i, c, 1), ago(i, c, -1)
                        if following:
                            nx = norm_between(*after, norm_stats(*after))
                        if previous:
                            norm1_apply(*before)
                        if following:
                            norm_dense(*after, nx)
                            norm_edges(*after, nx)
                        if following:
                            subtract(*after)
                        if now:
                            n = residual(i, c)
                        if previous:
                            keep_scores(*before)
                        if exists(*ago(i, c, 2)):
                            dense_out(i - 1, c)
                        if now:
                            add_selu(i, c, n)
                            norm1_between(i, c, x1_stats(i, c))

                nx = norm_between(0, 0, norm_stats(0, 0))
                norm_dense(0, 0, nx)
                norm_edges(0, 0, nx)
                subtract(0, 0)
                turn(0)
                do.enter()
                with dve.Fori(1, LASTI) as i:
                    do.turn(i - 1, 24)
                    turn(i)
                do.leave(LASTI - 1)
                turn(LASTI)
                turn(TURNS)

        with ExitStack() as own:
            def tmp(name, shape, dt=F32):
                return sb(name, shape, dt, own)

            HT = H * T
            pen_same = tmp("pen_same", [P, H, T])
            pen_next = tmp("pen_next", [P, H, T])
            one_same = tmp("one_same", [P, H, T])
            one_next = tmp("one_next", [P, H, T])
            pen_first = tmp("pen_first", [P, T])
            pen_last = tmp("pen_last", [P, T])
            top = tmp("top", [P, H, T])
            fwd = tmp("fwd", [P, H, T])
            bwd = tmp("bwd", [P, H, T])
            ends = tmp("ends", [P, 2, H])
            spread = tmp("spread", [P, 2 * H, P])
            cand = tmp("cand", [P, 2, H, P])
            best2 = tmp("best2", [P, 2, H])
            border_best = tmp("border_best", [P, 2, H])
            border_more = tmp("border_more", [P, 2, H])
            spread_ps = own.enter_context(nc.psum_tensor("spread_ps", [P, 4, 4, P], F32))
            sums_ps = own.enter_context(nc.psum_tensor("sums_ps", [P, 2, H], F32))
            pen_ready = sem("pen_ready")
            step, spread_ready, rows_ready, shifted, exp_ready, ends_ready, sums_ready = (
                sem(n) for n in ("softmax_step", "spread_ready", "best_rows_ready", "shifted", "exp_ready",
                                 "ends_ready", "border_sums_ready"))
            block = own.enter_context(nc.Block())

            def flat(t):
                return t[:, :, :].rearrange("p h t -> p (h t)")

            def back(t):
                return flat(t)[:, ::-1]

            @block.tensor
            def _(pe):
                pe.wait_ge(spread_ready, 1)
                for k in range(3):
                    ins = nc.tensor.matmul(spread_ps[:, k, :, :], ones[:, :], spread[:, 4 * k:4 * k + 4, :], start=True, stop=True)
                ins.then_inc(rows_ready, 1)
                pe.wait_ge(ends_ready, 1)
                for k, (from_first, from_last) in enumerate(((same_aa, same_ba), (same_ab, same_bb))):
                    nc.tensor.matmul(sums_ps[:, k, :], from_first[:, :], ends[:, 0, :], start=True, stop=False)
                    ins = nc.tensor.matmul(sums_ps[:, k, :], from_last[:, :], ends[:, 1, :], start=False, stop=True)
                ins.then_inc(sums_ready, 1)

            @block.scalar
            def _(act):
                a = nc.scalar

                def per_head(ap):
                    return ap.unsqueeze(1).to_broadcast([P, H, T])

                a.activation(pen_same[:, :, :], per_head(masks[:, :, 0]), ACT.Copy, scale=BIG, bias=-BIG).then_inc(pen_ready, 1)
                a.activation(pen_next[:, :, :], per_head(same_next[:, :]), ACT.Copy, scale=BIG, bias=-BIG).then_inc(pen_ready, 1)
                a.activation(one_same[:, :, :], per_head(masks[:, :, 0]), ACT.Copy)
                a.activation(one_next[:, :, :], per_head(same_next[:, :]), ACT.Copy)
                for k, kind in enumerate((slice(0, H), slice(H, 2 * H))):
                    act.wait_ge(shifted, k + 1)
                    a.activation(scores[:, kind, :], scores[:, kind, :], ACT.Exp).then_inc(exp_ready, 1)

            @block.vector
            def _(dve):
                v = nc.vector
                do = Chain(dve, step)

                edge_s, self_s = scores[:, 0:H, :], scores[:, H:2 * H, :]
                v.tensor_scalar(pen_first[:, :], is_first[:, :], 1.0, BIG, ALU.subtract, ALU.mult)
                v.tensor_scalar(pen_last[:, :], is_last[:, :], 1.0, BIG, ALU.subtract, ALU.mult)
                do.step(v.tensor_tensor(top[:, :, :], edge_s, self_s, ALU.max))
                dve.wait_ge(pen_ready, 1)
                v.tensor_tensor_scan(flat(fwd), flat(pen_same), flat(top), -BIG, ALU.add, ALU.max)
                dve.wait_ge(pen_ready, 2)
                do.step(v.tensor_tensor_scan(back(bwd), back(pen_next), back(top), -BIG, ALU.add, ALU.max))
                v.tensor_copy(ends[:, 0, :], bwd[:, :, 0])
                do.step(v.tensor_copy(ends[:, 1, :], fwd[:, :, T - 1]))
                v.tensor_tensor(spread[:, :, :], ident[:, :].unsqueeze(1).to_broadcast([P, 2 * H, P]),
                                ends[:, :, :].rearrange("p k h -> p (k h)").unsqueeze(2).to_broadcast([P, 2 * H, P]),
                                ALU.mult).then_inc(spread_ready, 1)
                do.step(v.tensor_tensor(top[:, :, :], fwd[:, :, :], bwd[:, :, :], ALU.max))
                dve.wait_ge(rows_ready, 1)
                for k, pen in enumerate((pen_a, pen_b)):
                    for piece in range(2):
                        for h in range(H):
                            row = piece * H + h
                            ins = v.tensor_tensor(cand[:, piece, h, :], spread_ps[:, row // 4, row % 4, :], pen[:, piece, :], ALU.add)
                    do.step(ins)
                    do.step(v.tensor_reduce(best2[:, :, :], cand[:, :, :, :], AX.X, ALU.max))
                    do.step(v.tensor_tensor(border_best[:, k, :], best2[:, 0, :], best2[:, 1, :], ALU.max))
                for k, pen in enumerate((pen_first, pen_last)):
                    for h in range(H):
                        ins = v.scalar_tensor_tensor(top[:, h, :], pen[:, :], border_best[:, k, h:h + 1], top[:, h, :], ALU.add, ALU.max)
                    do.step(ins)
                v.tensor_tensor(edge_s, edge_s, top[:, :, :], ALU.subtract).then_inc(shifted, 1)
                v.tensor_tensor(self_s, self_s, top[:, :, :], ALU.subtract).then_inc(shifted, 1)
                dve.wait_ge(exp_ready, 1)
                v.tensor_tensor_scan(flat(fwd), flat(one_same), edge_s.rearrange("p h t -> p (h t)"), 0.0, ALU.mult, ALU.add)
                do.step(v.tensor_tensor_scan(back(bwd), back(one_next), edge_s.rearrange("p h t -> p (h t)")[:, ::-1], 0.0, ALU.mult, ALU.add))
                v.tensor_copy(ends[:, 0, :], bwd[:, :, 0])
                v.tensor_copy(ends[:, 1, :], fwd[:, :, T - 1]).then_inc(ends_ready, 1)
                do.step(v.scalar_tensor_tensor(top[:, :, :], fwd[:, :, :], 1e-16, bwd[:, :, :], ALU.add, ALU.add))
                do.step(v.tensor_tensor(top[:, :, :], top[:, :, :], edge_s, ALU.subtract))
                dve.wait_ge(exp_ready, 2)
                do.step(v.tensor_tensor(top[:, :, :], top[:, :, :], self_s, ALU.add))
                dve.wait_ge(sums_ready, 1)
                do.step(v.tensor_copy(border_more[:, :, :], sums_ps[:, :, :]))
                for k, mask in enumerate((is_first, is_last)):
                    for h in range(H):
                        ins = v.scalar_tensor_tensor(top[:, h, :], mask[:, :], border_more[:, k, h:h + 1], top[:, h, :], ALU.mult, ALU.add)
                    do.step(ins)
                do.step(v.reciprocal(top[:, :, :], top[:, :, :]))
                do.step(v.tensor_tensor(alpha[:, :, :].rearrange("p t h -> p h t"), edge_s, top[:, :, :], ALU.mult))

        with ExitStack() as own:
            def tmp(name, shape, dt=F32):
                return sb(name, shape, dt, own)

            def pair(name, shape, dt=F32):
                return [tmp(f"m_{name}{c}", shape, dt) for c in range(2)]

            hrow = pair("hrow", [P, CT, 3 * D])
            xrow = pair("xrow", [P, CT, D])
            idx_c = pair("idx", [P, CT], U32)
            mask_c = pair("mask", [P, CT, 2])
            wdiff = pair("wdiff", [P, CT, H, D])
            parts = [tmp(f"m_parts{k}", [P, (NZ + 1) * P]) for k in range(4)]
            run = pair("run", [P, CT, D])
            gat = pair("gat", [P, CT, D])
            gexp = pair("gexp", [P, CT, D])
            grelu = pair("grelu", [P, CT, D])
            half = tmp("m_half", [P, CT, D])
            border = tmp("m_border", [P, 2, D])
            x1 = pair("x1", [P, CT, D])
            tr = [own.enter_context(nc.psum_tensor(f"m_tr{k}", [P, (NZ + 1) * P], F32)) for k in range(4)]
            mm = [own.enter_context(nc.psum_tensor(f"m_mm{k}", [P, CT, 2, D], F32)) for k in range(2)]
            ext_ps = own.enter_context(nc.psum_tensor("m_ext", [P, 2, D], F32))
            hrow_ready, xrow_ready, sidx_ready, x1_stored, scattered = (
                [sem(f"m_{n}{c}") for c in range(2)] for n in
                ("hrow_ready", "xrow_ready", "sidx_ready", "x1_stored", "scattered"))
            (row_consts, wdiff_ready, tr_ready, parts_ready, mm_ready, gat_ready, gat_act, x1_ready,
             dve_step, act_step, border_sum, border_scattered) = (sem(f"m_{n}") for n in (
                 "row_consts", "wdiff_ready", "tr_ready", "parts_ready", "mm_ready", "gat_ready", "gat_act",
                 "x1_ready", "dve_step", "act_step", "border_sum", "border_scattered"))
            block = own.enter_context(nc.Block())

            def kth(i, c):
                return 2 * i + (c + 1)

            def cols(i, c):
                return bass.ds(i * PER + CT * c, CT)

            def scatter(table, idx, rows_ap, done):
                nc.gpsimd.indirect_dma_start(table, bass.IndirectOffsetOnAxis(ap=idx, axis=0), rows_ap, None,
                                             bounds_check=last_row[0], oob_is_err=False).then_inc(done, 16)

            @block.gpsimd
            def _(pool):
                last_row[0] = pool.to_reg(N - 1)
                for c in range(2):
                    nc.gpsimd.memset(hrow[c][:, :, 2 * D:3 * D], 0.0).then_inc(row_consts, 1)
                pool.wait_ge(row_consts, 2)
                for c in range(2):
                    nc.gpsimd.memset(hrow[c][:, :, 2 * D:2 * D + 1], 1.0).then_inc(row_consts, 1)
                with pool.Fori(0, TURNS) as i:
                    for c in range(2):
                        pool.wait_ge(sidx_ready[c], 16 * (i + 1))
                        pool.wait_ge(x1_ready, kth(i, c))
                        pool.sem_inc(admitted, 1)
                        for j in range(CT):
                            scatter(x1_table, idx_c[c][:, j:j + 1], x1[c][:, j, :], scattered[c])
                pool.wait_ge(x1_ready, 2 * TURNS + 1)
                for k in range(2):
                    scatter(x1_table, border_idx[:, k:k + 1], border_x1[:, k, :], border_scattered)
                for c in range(2):
                    pool.wait_ge(scattered[c], 16 * CT * TURNS)
                pool.wait_ge(border_scattered, 32)

            @block.sync
            def _(sp):
                def load_h(i, c):
                    sp.dma_start(hrow[c][:, :, 0:2 * D], stash[:, cols(i, c), 0:2 * D]).then_inc(hrow_ready[c], 16)

                def load_x(i, c):
                    sp.dma_start(xrow[c][:, :, :], stash[:, cols(i, c), 2 * D:3 * D]).then_inc(xrow_ready[c], 16)

                def load_idx(i, c):
                    sp.dma_start(idx_c[c][:, :], scatter_idx[:, cols(i, c)]).then_inc(sidx_ready[c], 16)

                def store_x1(i, c):
                    sp.wait_ge(x1_ready, kth(i, c))
                    sp.dma_start(x1_edges[:, cols(i, c), :], x1[c][:, :, :]).then_inc(x1_stored[c], 16)

                def turn(i):
                    for c in range(2):
                        if exists(*ago(i, c, -1)):
                            n, m = ago(i, c, 1), ago(i, c, -1)
                            wait_from(sp, tr_ready, 8 * n[0] + CT * (n[1] + 1))
                            load_h(*m)
                        if exists(*ago(i, c, 2)):
                            store_x1(i - 1, c)
                        if exists(i, c):
                            load_x(i, c)
                        j, d = ago(i, c, 1)
                        if exists(j, d):
                            wait_from(sp, scattered[d], 16 * CT * j)
                            load_idx(j, d)

                load_h(0, 0)
                turn(0)
                turn(1)
                with sp.Fori(2, TURNS - 1) as i:
                    turn(i)
                turn(TURNS - 1)
                turn(TURNS)
                for k, t in ((0, 0), (1, T - 1)):
                    sp.dma_start(hrow[0][:, k, 0:2 * D], stash[:, t, 0:2 * D]).then_inc(hrow_ready[0], 16)
                    sp.dma_start(xrow[0][:, k, :], stash[:, t, 2 * D:3 * D]).then_inc(xrow_ready[0], 16)
                for c in range(2):
                    sp.wait_ge(x1_stored[c], 16 * TURNS)

            @block.tensor
            def _(pe):
                t = nc.tensor

                def transposes(i, n):
                    c, j = divmod(n, CT)
                    if j == 0:
                        pe.wait_ge(hrow_ready[c], 16 * (i + 1))
                        pe.wait_ge(wdiff_ready, kth(i, c))
                    wd = wdiff[c][:, j, :, :].rearrange("p h f -> p (h f)")
                    for z in range(NZ):
                        t.transpose(tr[n % 4][:, z * P:(z + 1) * P], wd[:, z * P:(z + 1) * P], ident[:, :])
                    t.transpose(tr[n % 4][:, NZ * P:], hrow[c][:, j, D:3 * D], ident[:, :]).then_inc(tr_ready, 1)

                def products(i, n):
                    c, j = divmod(n, CT)
                    pe.wait_ge(parts_ready, 8 * i + n + 1)
                    for z in range(NZ):
                        t.matmul(mm[c][:, j, 0, :], parts[n % 4][:, z * P:(z + 1) * P], w_msg[:, z, :],
                                 start=(z == 0), stop=(z == NZ - 1))
                    t.matmul(mm[c][:, j, 1, :], parts[n % 4][:, NZ * P:], base_w[:, :],
                             start=True, stop=True).then_inc(mm_ready, 1)

                pe.wait_ge(row_consts, 4)
                with pe.Fori(0, TURNS) as i:
                    for c in range(2):
                        for j in range(CT):
                            transposes(i, CT * c + j)
                        for j in range(CT):
                            products(i, CT * c + j)
                pe.wait_ge(hrow_ready[0], 16 * TURNS + 32)
                pe.wait_ge(gat_ready, 2 * TURNS)
                for k in range(2):
                    t.transpose(tr[k][:, NZ * P:], hrow[0][:, k, D:3 * D], ident[:, :]).then_inc(tr_ready, 1)
                for k in range(2):
                    pe.wait_ge(parts_ready, 8 * TURNS + k + 1)
                    t.matmul(mm[0][:, k, 1, :], parts[k][:, NZ * P:], base_w[:, :], start=True, stop=True)
                for k, (from_first, from_last) in enumerate(((same_aa, same_ba), (same_ab, same_bb))):
                    t.matmul(ext_ps[:, k, :], from_first[:, :], first_sum[:, 0, :], start=True, stop=False)
                    ins = t.matmul(ext_ps[:, k, :], from_last[:, :], run[1][:, CT - 1, :], start=False, stop=True)
                ins.then_inc(border_sum, 1)

            @block.scalar
            def _(act):
                a = nc.scalar
                own_step = Chain(act, act_step)

                def copies(i, n):
                    act.wait_ge(tr_ready, 8 * i + n + 1)
                    a.activation(parts[n % 4][:, :], tr[n % 4][:, :], ACT.Copy).then_inc(parts_ready, 1)

                def selu_parts(i, c, k=CT):
                    act.wait_ge(gat_ready, kth(i, c))
                    n = own_step.mark(a.activation(gexp[c][:, 0:k, :], gat[c][:, 0:k, :], ACT.Exp))
                    a.activation(grelu[c][:, 0:k, :], gat[c][:, 0:k, :], ACT.Relu, scale=SELU_L).then_inc(gat_act, 1)
                    own_step.wait(n)
                    a.activation(gexp[c][:, 0:k, :], gexp[c][:, 0:k, :], ACT.Relu, scale=-SELU_LA, bias=selu_la[:, :]).then_inc(gat_act, 1)

                def turn(i):
                    for c in range(2):
                        if exists(i, c):
                            copies(i, CT * c)
                        if exists(i, c):
                            copies(i, CT * c + 1)
                            copies(i, CT * c + 2)
                            copies(i, CT * c + 3)
                        if exists(*ago(i, c, 1)):
                            selu_parts(*ago(i, c, 1))

                turn(0)
                own_step.enter()
                with act.Fori(1, TURNS) as i:
                    own_step.turn(i - 1, 2)
                    turn(i)
                own_step.leave(TURNS - 1)
                turn(TURNS)
                for k in range(2):
                    act.wait_ge(tr_ready, 8 * TURNS + k + 1)
                    a.activation(parts[k][:, NZ * P:], tr[k][:, NZ * P:], ACT.Copy).then_inc(parts_ready, 1)
                selu_parts(TURNS, 0, 2)

            @block.vector
            def _(dve):
                v = nc.vector
                do = Chain(dve, dve_step)

                def mid(ap, k):
                    return ap.unsqueeze(2).to_broadcast([P, k, D])

                def take_masks(i, c):
                    wait_from(dve, gat_ready, 2 * i + (c - 1))
                    do.mark(v.tensor_copy(mask_c[c][:, :, :], masks[:, cols(i, c), :]))

                def weigh(i, c):
                    dve.wait_ge(hrow_ready[c], 16 * (i + 1))
                    v.tensor_tensor(wdiff[c][:, :, :, :], hrow[c][:, :, 0:D].unsqueeze(2).to_broadcast([P, CT, H, D]),
                                    alpha[:, cols(i, c), :].unsqueeze(3).to_broadcast([P, CT, H, D]), ALU.mult).then_inc(wdiff_ready, 1)

                def running_sums(i, c):
                    do.wait(do.n)
                    dve.wait_ge(mm_ready, 8 * i + CT * (c + 1))
                    for j in range(CT):
                        before = run[c][:, j - 1, :] if j else run[1 - c][:, CT - 1, :]
                        if j:
                            do.wait(do.n - 1)
                        do.mark(v.scalar_tensor_tensor(run[c][:, j, :], before, mask_c[c][:, j, 0:1], mm[c][:, j, 0, :], ALU.mult, ALU.add))
                        if j:
                            do.wait(do.n - 1)
                        do.mark(v.scalar_tensor_tensor(first_sum[:, 0, :], mm[c][:, j, 0, :], mask_c[c][:, j, 1:2], first_sum[:, 0, :], ALU.mult, ALU.add))
                    do.wait(do.n - 1)
                    v.tensor_tensor(gat[c][:, :, :], run[c][:, :, :], mm[c][:, :, 1, :], ALU.add).then_inc(gat_ready, 1)

                def residual(i, c, k=CT):
                    wait_from(dve, x1_ready, 2 * i + c)
                    dve.wait_ge(gat_act, 4 * i + 2 * c + 1)
                    dve.wait_ge(xrow_ready[c], 16 * (i + 1) + (16 if k < CT else 0))
                    return do.mark(v.tensor_tensor(half[:, 0:k, :], xrow[c][:, 0:k, :], grelu[c][:, 0:k, :], ALU.add))

                def add_selu(i, c, n, x1_to, k=CT):
                    do.wait(n)
                    dve.wait_ge(gat_act, 4 * i + 2 * c + 2)
                    if k == CT:
                        wait_from(dve, x1_stored[c], 16 * i)
                        wait_from(dve, scattered[c], 16 * CT * i)
                    v.tensor_tensor(x1_to, half[:, 0:k, :], gexp[c][:, 0:k, :], ALU.subtract).then_inc(x1_ready, 1)

                def turn(i):
                    for c in range(2):
                        previous, following = exists(*ago(i, c, 1)), exists(*ago(i, c, -1))
                        j, d = ago(i, c, 1)
                        if previous:
                            running_sums(j, d)
                        if following:
                            weigh(*ago(i, c, -1))
                            take_masks(*ago(i, c, -1))
                        if previous:
                            n = residual(j, d)
                            add_selu(j, d, n, x1[d][:, :, :])

                do.step(v.memset(run[1][:, :, :], 0.0))
                weigh(0, 0)
                take_masks(0, 0)
                turn(0)
                do.enter()
                with dve.Fori(1, TURNS - 1) as i:
                    do.turn(i - 1, 20)
                    turn(i)
                do.leave(TURNS - 2)
                turn(TURNS - 1)
                turn(TURNS)
                dve.wait_ge(border_sum, 1)
                do.step(v.tensor_tensor(border[:, 0, :], first_sum[:, 0, :], ext_ps[:, 0, :], ALU.add))
                do.step(v.tensor_tensor(border[:, 1, :], run[1][:, CT - 1, :], ext_ps[:, 1, :], ALU.add))
                v.tensor_tensor(gat[0][:, 0:2, :], border[:, :, :], mm[0][:, 0:2, 1, :], ALU.add).then_inc(gat_ready, 1)
                add_selu(TURNS, 0, residual(TURNS, 0, 2), border_x1[:, :, :], 2)

        with ExitStack() as own:
            def tmp(name, shape, dt=F32):
                return sb(name, shape, dt, own)

            def pair(name, shape, dt=F32):
                return [tmp(f"n_{name}{c}", shape, dt) for c in range(2)]

            gidx = pair("gidx", [P, CT, 2], U32)
            sidx = pair("sidx", [P, CT], U32)
            mask_c = pair("mask", [P, CT, 2])
            grow = pair("grow", [P, CT, KW])
            hrow = pair("hrow", [P, CT * D])
            xrow = pair("xrow", [P, CT, D])
            growT = pair("growT", [KW, CT * P])
            hrowT = pair("hrowT", [P, CT * D])
            run = pair("run", [P, CT, D])
            pre = pair("pre", [P, CT, D])
            res = pair("res", [P, CT, D])
            border = tmp("n_border", [P, 2, D])
            R = 2 * CT
            cen = tmp("n_cen", [P, R, D])
            stats = pair("stats", [P, R, 6])
            sumq = pair("sumq", [P, R, 2])
            diff = pair("diff", [P, R])
            var = pair("var", [P, R])
            lnv = pair("lnv", [P, R])
            rstd = pair("rstd", [P, R])
            ea_p = edge_attr[0:FULL * T, :].rearrange("(p t) w -> p t w", t=T)
            tr_g = [own.enter_context(nc.psum_tensor(f"n_trg{k}", [KW, CT * P], F32)) for k in range(2)]
            tr_h = [own.enter_context(nc.psum_tensor(f"n_trh{k}", [P, CT * D], F32)) for k in range(2)]
            mm = [own.enter_context(nc.psum_tensor(f"n_mm{k}", [P, 2, CT, D], F32)) for k in range(2)]
            ext_ps = own.enter_context(nc.psum_tensor("n_ext", [P, 2, D], F32))
            gidx_ready, sidx_ready, gathered, attr_ready, rows_ready, scattered = (
                [sem(f"n_{n}{c}") for c in range(2)] for n in
                ("gidx_ready", "sidx_ready", "gathered", "attr_ready", "rows_ready", "scattered"))
            (tr_ready, copied, mm_ready, sum_ready, res_ready, dve_step, border_sum, border_scattered) = (
                sem(f"n_{n}") for n in ("tr_ready", "copied", "mm_ready", "sum_ready", "res_ready", "dve_step",
                                        "border_sum", "border_scattered"))
            var_ready, rstd_ready, h_ready, border_var, border_rstd, act_step = (
                sem(f"n_{n}") for n in ("var_ready", "rstd_ready", "h_ready", "border_var", "border_rstd", "act_step"))
            block = own.enter_context(nc.Block())

            @block.gpsimd
            def _(pool):
                last_row[0] = pool.to_reg(N - 1)

                def gathers(i, c):
                    pool.wait_ge(gidx_ready[c], 16 * (i + 1))
                    pool.sem_inc(admitted, 1)
                    for j in range(CT):
                        nc.gpsimd.indirect_dma_start(
                            grow[c][:, j, 0:D], None, x1_table,
                            bass.IndirectOffsetOnAxis(ap=gidx[c][:, j, 0:1], axis=0),
                            bounds_check=last_row[0], oob_is_err=False).then_inc(gathered[c], 16)

                def scatters(i, c):
                    pool.wait_ge(sidx_ready[c], 16 * (i + 1))
                    pool.wait_ge(res_ready, kth(i, c))
                    pool.sem_inc(admitted, 1)
                    for j in range(CT):
                        scatter(out, sidx[c][:, j:j + 1], res[c][:, j, :], scattered[c])

                for c in range(2):
                    gathers(0, c)
                with pool.Fori(1, TURNS) as i:
                    for c in range(2):
                        pool.wait_ge(tr_ready, 2 * i + (c - 1))
                        gathers(i, c)
                        scatters(i - 1, c)
                for c in range(2):
                    scatters(TURNS - 1, c)
                pool.wait_ge(res_ready, 2 * TURNS + 1)
                for k in range(2):
                    scatter(out, border_idx[:, k:k + 1], res[0][:, k, :], border_scattered)
                for c in range(2):
                    pool.wait_ge(scattered[c], 16 * CT * TURNS)
                pool.wait_ge(border_scattered, 32)

            @block.sync
            def _(sp):
                def load_gidx(i, c):
                    sp.dma_start(gidx[c][:, :, :], gather_idx[:, cols(i, c), :]).then_inc(gidx_ready[c], 16)

                def load_sidx(i, c):
                    sp.dma_start(sidx[c][:, :], scatter_idx[:, cols(i, c)]).then_inc(sidx_ready[c], 16)

                def load_attr_full(i, c):
                    for rows in FULL_PARTS:
                        sp.dma_start(grow[c][rows, :, D:KW], ea_p[rows, cols(i, c), :]).then_inc(attr_ready[c], 16)

                def load_attr(i, c):
                    load_attr_full(i, c)
                    sp.dma_start(grow[c][FULL:P, :, D:KW],
                                 edge_attr[bass.ds(i * PER + (CT * c + FULL * T), CT), :].rearrange("(p t) w -> p t w", p=1)).then_inc(attr_ready[c], 16)

                def load_rows(i, c):
                    sp.dma_start(xrow[c][:, :, :], x1_edges[:, cols(i, c), :]).then_inc(rows_ready[c], 16)

                def turn(i, attr, more=True):
                    for c in range(2):
                        sp.wait_ge(gathered[c], 16 * CT * (i + 1))
                        if more:
                            load_gidx(i + 1, c)
                        sp.wait_ge(tr_ready, kth(i, c))
                        if more:
                            attr(i + 1, c)
                        sp.wait_ge(scattered[c], 16 * CT * i)
                        load_sidx(i, c)
                        sp.wait_ge(res_ready, kth(i, c))
                        if more:
                            load_rows(i + 1, c)

                for c in range(2):
                    load_gidx(0, c)
                    load_attr(0, c)
                    load_rows(0, c)
                with sp.Fori(0, REAL - 1) as i:
                    turn(i, load_attr)
                with sp.Fori(REAL - 1, TURNS - 1) as i:
                    turn(i, load_attr_full)
                turn(TURNS - 1, None, False)

            @block.tensor
            def _(pe):
                t = nc.tensor

                def products_h(lhs, ps, pairs):
                    for j in range(pairs):
                        ins = t.matmul(ps[:, 1, 2 * j:2 * j + 2, :], lhs[:, j * P:(j + 1) * P], w1_blk[:, :], start=True, stop=True)
                    return ins

                def turn(i, attr_incs):
                    for c in range(2):
                        pe.wait_ge(attr_ready[c], attr_incs)
                        pe.wait_ge(h_ready, kth(i, c))
                        pe.wait_ge(copied, 4 * i + 2 * c)
                        for j in range(CT):
                            t.transpose(tr_g[c][:, j * P:(j + 1) * P], grow[c][:, j, :], ident[:, :])
                        for j in range(CT // 2):
                            ins = t.transpose(tr_h[c][:, j * P:(j + 1) * P], hrow[c][:, j * P:(j + 1) * P], ident[:, :])
                        ins.then_inc(tr_ready, 1)
                        pe.wait_ge(copied, 4 * i + 2 * c + 2)
                        pe.wait_ge(sum_ready, 2 * i + c)
                        for j in range(CT):
                            t.matmul(mm[c][:, 0, j, :], growT[c][:, j * P:(j + 1) * P], w1_all[:, :], start=True, stop=True)
                        products_h(hrowT[c], mm[c], CT // 2).then_inc(mm_ready, 1)

                with pe.Fori(0, REAL) as i:
                    turn(i, 48 * (i + 1))
                with pe.Fori(REAL, TURNS) as i:
                    turn(i, 32 * (i + 1) + 16 * REAL)
                pe.wait_ge(sum_ready, 2 * TURNS)
                t.transpose(tr_h[0][:, 0:P], border_h1[:, :, :].rearrange("p k f -> p (k f)"), ident[:, :]).then_inc(tr_ready, 1)
                pe.wait_ge(copied, 4 * TURNS + 1)
                products_h(hrowT[0], mm[0], 1)
                for k, (from_first, from_last) in enumerate(((same_aa, same_ba), (same_ab, same_bb))):
                    t.matmul(ext_ps[:, k, :], from_first[:, :], first_sum[:, 1, :], start=True, stop=False)
                    ins = t.matmul(ext_ps[:, k, :], from_last[:, :], run[1][:, CT - 1, :], start=False, stop=True)
                ins.then_inc(border_sum, 1)

            @block.scalar
            def _(act):
                a = nc.scalar
                own_step = Chain(act, act_step)

                def inverse_roots(c, k, done):
                    own_step.step(a.activation(lnv[c][:, 0:k], var[c][:, 0:k], ACT.Ln, bias=eps[:, :], scale=1.0 / D))
                    a.activation(rstd[c][:, 0:k], lnv[c][:, 0:k], ACT.Exp, scale=-0.5).then_inc(done, 1)

                def rstds(i, c):
                    act.wait_ge(var_ready, kth(i, c))
                    inverse_roots(c, R, rstd_ready)

                def copies(i):
                    for c in range(2):
                        act.wait_ge(tr_ready, kth(i, c))
                        wait_from(act, mm_ready, 2 * i + c)
                        a.activation(growT[c][:, :], tr_g[c][:, :], ACT.Copy).then_inc(copied, 1)
                        a.activation(hrowT[c][:, :], tr_h[c][:, :], ACT.Copy).then_inc(copied, 1)
                        if exists(*ago(i, c, -1)):
                            rstds(*ago(i, c, -1))

                act.wait_ge(border_var, 1)
                inverse_roots(0, 2, border_rstd)
                rstds(0, 0)
                own_step.enter()
                with act.Fori(0, TURNS - 1) as i:
                    own_step.turn(i, 2)
                    copies(i)
                own_step.leave(TURNS - 1)
                copies(TURNS - 1)
                act.wait_ge(tr_ready, 2 * TURNS + 1)
                act.wait_ge(mm_ready, 2 * TURNS)
                a.activation(hrowT[0][:, 0:P], tr_h[0][:, 0:P], ACT.Copy).then_inc(copied, 1)

            @block.vector
            def _(dve):
                v = nc.vector
                do = Chain(dve, dve_step)

                def mid(ap):
                    return ap.unsqueeze(2).to_broadcast([P, ap.shape[1], D])

                def moments(c, k, centre_rows, signal):
                    st, sq, df, va = stats[c][:, 0:k, :], sumq[c][:, 0:k, :], diff[c][:, 0:k], var[c][:, 0:k]
                    do.wait(do.n)
                    nd = do.mark(v.tensor_tensor(df, st[:, :, 1], st[:, :, 4], ALU.subtract))
                    do.mark(v.tensor_tensor(sq, st[:, :, 1:3], st[:, :, 4:6], ALU.add))
                    do.wait(nd)
                    n = do.mark(v.scalar_tensor_tensor(va, df, D / 4.0, df, ALU.mult, ALU.mult))
                    do.wait(n - 1)
                    for lo, rows in centre_rows:
                        hi = lo + rows.shape[1]
                        do.mark(v.scalar_tensor_tensor(cen[:, lo:hi, :], mid(sumq[c][:, lo:hi, 0]), -0.5, rows, ALU.mult, ALU.add))
                    do.wait(n)
                    v.tensor_tensor(va, va, sq[:, :, 1], ALU.add).then_inc(signal, 1)

                def scale(c, lo, to):
                    hi = lo + to.shape[1]
                    return v.scalar_tensor_tensor(to, cen[:, lo:hi, :], 0.0, mid(rstd[c][:, lo:hi]), ALU.max, ALU.mult)

                def norm(i, c):
                    dve.wait_ge(gathered[c], 16 * CT * (i + 1))
                    for j in range(CT):
                        v.bn_stats(stats[c][:, j, :], grow[c][:, j, 0:D])
                    dve.wait_ge(rows_ready[c], 16 * (i + 1))
                    for j in range(CT):
                        ins = v.bn_stats(stats[c][:, CT + j, :], xrow[c][:, j, :])
                    do.mark(ins)
                    wait_from(dve, h_ready, 2 * i + c)
                    moments(c, R, ((0, grow[c][:, :, 0:D]), (CT, xrow[c][:, :, :])), var_ready)

                def apply(i, c):
                    do.wait(do.n)
                    dve.wait_ge(rstd_ready, kth(i, c))
                    scale(c, 0, grow[c][:, :, 0:D])
                    wait_from(dve, tr_ready, 2 * i + (c - 1))
                    scale(c, CT, r3(hrow[c][:, :], D)).then_inc(h_ready, 1)

                def take_masks(i, c):
                    do.mark(v.tensor_copy(mask_c[c][:, :, :], masks[:, cols(i, c), :]))

                def running_sums(i, c):
                    do.wait(do.n)
                    dve.wait_ge(mm_ready, kth(i, c))
                    for j in range(CT):
                        before = run[c][:, j - 1, :] if j else run[1 - c][:, CT - 1, :]
                        if j:
                            do.wait(do.n - 1)
                        do.mark(v.scalar_tensor_tensor(run[c][:, j, :], before, mask_c[c][:, j, 0:1], mm[c][:, 0, j, :], ALU.mult, ALU.add))
                        if j:
                            do.wait(do.n - 1)
                        do.mark(v.scalar_tensor_tensor(first_sum[:, 1, :], mm[c][:, 0, j, :], mask_c[c][:, j, 1:2], first_sum[:, 1, :], ALU.mult, ALU.add))
                    do.wait(do.n - 1)

                def close(i, c, sum_ap, x_ap, k):
                    wait_from(dve, res_ready, 2 * i + (c - 1))
                    v.tensor_tensor(pre[c][:, 0:k, :], sum_ap, mm[c][:, 1, 0:k, :], ALU.add).then_inc(sum_ready, 1)
                    dve.wait_ge(sum_ready, kth(i, c))
                    do.step(v.tensor_tensor(pre[c][:, 0:k, :], pre[c][:, 0:k, :], bias1_b[:, :].unsqueeze(1).to_broadcast([P, k, D]), ALU.add))
                    wait_from(dve, scattered[c], 16 * CT * i)
                    v.scalar_tensor_tensor(res[c][:, 0:k, :], pre[c][:, 0:k, :], 0.0, x_ap, ALU.max, ALU.add).then_inc(res_ready, 1)

                def turn(i):
                    for c in range(2):
                        following = exists(*ago(i, c, -1))
                        if following:
                            norm(*ago(i, c, -1))
                        take_masks(i, c)
                        if following:
                            apply(*ago(i, c, -1))
                        running_sums(i, c)
                        close(i, c, run[c][:, :, :], xrow[c][:, :, :], CT)

                do.step(v.memset(run[1][:, :, :], 0.0))
                for k in range(2):
                    ins = v.bn_stats(stats[0][:, k, :], border_x1[:, k, :])
                do.mark(ins)
                moments(0, 2, ((0, border_x1[:, :, :]),), border_var)
                do.wait(do.n)
                dve.wait_ge(border_rstd, 1)
                do.step(scale(0, 0, border_h1[:, :, :]))
                norm(0, 0)
                apply(0, 0)
                turn(0)
                do.enter()
                with dve.Fori(1, TURNS - 1) as i:
                    do.turn(i - 1, 2 * (2 * CT + 8))
                    turn(i)
                do.leave(TURNS - 2)
                turn(TURNS - 1)
                dve.wait_ge(border_sum, 1)
                do.step(v.tensor_tensor(border[:, 0, :], first_sum[:, 1, :], ext_ps[:, 0, :], ALU.add))
                do.step(v.tensor_tensor(border[:, 1, :], run[1][:, CT - 1, :], ext_ps[:, 1, :], ALU.add))
                close(TURNS, 0, border[:, :, :], border_x1[:, :, :], 2)


def kernel(x, src, dst, edge_attr_16, L0_gnn_W_l, L0_gnn_W_r, L0_gnn_att, L0_gnn_bias, L1_gnn_W, L1_gnn_b):
    import numpy as np
    import concourse.bacc as bacc
    from concourse.bass_utils import run_bass_kernel_spmd

    nc = bacc.Bacc("TRN2", target_bir_lowering=False, num_devices=1)
    named = dict(x=x, src=src, dst=dst, edge_attr=edge_attr_16, w_l=L0_gnn_W_l, w_r=L0_gnn_W_r, att=L0_gnn_att,
                 bias0=L0_gnn_bias, w1=L1_gnn_W, bias1=L1_gnn_b)
    arrays, args = {}, {}
    for name, a in named.items():
        a = np.ascontiguousarray(a)
        arrays[f"in_{name}"] = a
        args[name] = nc.dram_tensor(f"in_{name}", a.shape, mybir.dt.from_np(a.dtype), kind="ExternalInput").ap()
    out = nc.dram_tensor("out_x", tuple(x.shape), F32, kind="ExternalOutput").ap()
    gnn_program(nc, out=out, **args)
    result = run_bass_kernel_spmd(nc, [arrays], core_ids=[0])
    return result.results[0]["out_x"]
```
